# Optimizing a Trainium2 kernel written in Bass

```python
import numpy as np
import jax
import jax.numpy as jnp

def _softmax(x, axis=-1):
    return jax.nn.softmax(x, axis=axis)

def _gelu(x):
    return jax.nn.gelu(x, approximate=True)

def _silu(x):
    return jax.nn.silu(x)

def _sigmoid(x):
    return jax.nn.sigmoid(x)

def _layernorm(x, axis=-1, eps=1e-05):
    m = jnp.mean(x, axis=axis, keepdims=True)
    v = jnp.var(x, axis=axis, keepdims=True)
    return (x - m) / jnp.sqrt(v + eps)

def _scatter_add(tgt, idx, src, axis=0):
    return tgt.at[idx].add(src)

def _segment_sum(src, seg, n):
    return jax.ops.segment_sum(src, seg, n)
kernel_name = 'mk_seq_preln_d1_jaxref_r8_2855b1'

def setup_inputs(seed: int=0):
    np.random.seed(seed)
    _w = jnp.asarray

    def _L0_attn_setup():
        import jax, jax.numpy as jnp
        import numpy as np
        D_MODEL = 128
        N_HEADS = 16
        HEAD_DIM = D_MODEL // N_HEADS
        ROPE_BASE = 10000.0

        def _rope(q, k):
            S, Dh = (q.shape[1], q.shape[-1])
            inv_freq = 1.0 / ROPE_BASE ** (jnp.arange(0, Dh, 2, dtype=jnp.float32) / Dh)
            t = jnp.arange(S, dtype=jnp.float32)
            freqs = jnp.outer(t, inv_freq)
            emb = jnp.concatenate([freqs, freqs], axis=-1)
            cos = jnp.cos(emb)[None, :, None, :]
            sin = jnp.sin(emb)[None, :, None, :]

            def rotate_half(v):
                v1, v2 = (v[..., :Dh // 2], v[..., Dh // 2:])
                return jnp.concatenate([-v2, v1], axis=-1)
            return (q * cos + rotate_half(q) * sin, k * cos + rotate_half(k) * sin)
        key = jax.random.key(seed)
        ks = jax.random.split(key, 5)
        B, S = (1, 512)
        scale = 1.0 / np.sqrt(D_MODEL)
        x = jax.random.normal(ks[0], (B, S, D_MODEL), dtype=jnp.float32)
        Wq = jax.random.normal(ks[1], (D_MODEL, D_MODEL), dtype=jnp.float32) * scale
        Wk = jax.random.normal(ks[2], (D_MODEL, D_MODEL), dtype=jnp.float32) * scale
        Wv = jax.random.normal(ks[3], (D_MODEL, D_MODEL), dtype=jnp.float32) * scale
        Wo = jax.random.normal(ks[4], (D_MODEL, D_MODEL), dtype=jnp.float32) * scale
        return {'x': x, 'Wq': Wq, 'Wk': Wk, 'Wv': Wv, 'Wo': Wo}
    _L0_attn_in = _L0_attn_setup()

    def _L0_ffn_setup():
        import jax, jax.numpy as jnp
        import numpy as np
        DIM = 128
        DEPTH = 2
        HEADS = 8
        DIM_HEAD = 64
        WINDOW = 64
        INNER = HEADS * DIM_HEAD
        HID = int(DIM * 4 * 2 / 3)
        B, N = (2, 1024)
        QK_SCALE = 8.0

        def shift_token(t):
            t1, t2 = jnp.split(t, 2, axis=-1)
            t2 = jnp.pad(t2, ((0, 0), (1, 0), (0, 0)))[:, :-1]
            return jnp.concatenate([t1, t2], axis=-1)

        def l2norm(t):
            return t / jnp.clip(jnp.linalg.norm(t, axis=-1, keepdims=True), 1e-12)

        def rotate_half(x):
            x1, x2 = jnp.split(x, 2, axis=-1)
            return jnp.concatenate([-x2, x1], axis=-1)

        def rotary_xpos(q, k):
            n = q.shape[-2]
            half_idx = jnp.arange(0, DIM_HEAD, 2, dtype=jnp.float32)
            inv_freq = 1.0 / 10000.0 ** (half_idx / DIM_HEAD)
            t = jnp.arange(n, dtype=jnp.float32)
            freqs = t[:, None] * inv_freq[None, :]
            freqs = jnp.concatenate([freqs, freqs], axis=-1)
            base = (half_idx + 0.4 * DIM_HEAD) / (1.4 * DIM_HEAD)
            power = (t - n // 2) / float(WINDOW // 2)
            scale = base[None, :] ** power[:, None]
            scale = jnp.concatenate([scale, scale], axis=-1)
            cos, sin = (jnp.cos(freqs), jnp.sin(freqs))
            q = q * cos * scale + rotate_half(q) * sin * scale
            k = k * cos / scale + rotate_half(k) * sin / scale
            return (q, k)

        def local_attention(q, k, v):
            b, h, n, d = q.shape
            w = n // WINDOW
            bq = q.reshape(b, h, w, WINDOW, d) * QK_SCALE
            bk = k.reshape(b, h, w, WINDOW, d)
            bv = v.reshape(b, h, w, WINDOW, d)

            def look_around(t):
                p = jnp.pad(t, ((0, 0), (0, 0), (1, 0), (0, 0), (0, 0)))
                return jnp.concatenate([p[:, :, :w], p[:, :, 1:]], axis=3)
            bk, bv = (look_around(bk), look_around(bv))
            bt = jnp.arange(n).reshape(w, WINDOW)
            btp = jnp.pad(bt, ((1, 0), (0, 0)), constant_values=-1)
            btk = jnp.concatenate([btp[:w], btp[1:]], axis=1)
            sim = jnp.einsum('bhwid,bhwjd->bhwij', bq, bk)
            i = bt[:, :, None]
            j = btk[:, None, :]
            mask = (i < j) | (i > j + WINDOW) | (j == -1)
            sim = jnp.where(mask, -jnp.finfo(sim.dtype).max, sim)
            attn = jax.nn.softmax(sim, axis=-1)
            out = jnp.einsum('bhwij,bhwjd->bhwid', attn, bv)
            return out.reshape(b, h, n, d)

        def _layer(x, wqkv, qs, ksc, wo, lg, lb, w1, b1, w2, b2):
            b, n, _ = x.shape
            h = shift_token(x)
            qkv = h @ wqkv
            q, k, v = jnp.split(qkv, 3, axis=-1)
            to_heads = lambda t: t.reshape(b, n, HEADS, DIM_HEAD).transpose(0, 2, 1, 3)
            q, k, v = (to_heads(q), to_heads(k), to_heads(v))
            q = l2norm(q) * qs
            k = l2norm(k) * ksc
            q, k = rotary_xpos(q, k)
            o = local_attention(q, k, v)
            o = o.transpose(0, 2, 1, 3).reshape(b, n, INNER)
            x = x + o @ wo
            h = shift_token(x)
            mu = h.mean(-1, keepdims=True)
            var = h.var(-1, keepdims=True)
            h = (h - mu) / jnp.sqrt(var + 1e-05) * lg + lb
            h = h @ w1 + b1
            a, g = jnp.split(h, 2, axis=-1)
            h = a * jax.nn.gelu(g, approximate=False)
            x = x + h @ w2 + b2
            return x
        key = jax.random.key(seed)
        ks = jax.random.split(key, 6)
        return {'x': jax.random.normal(ks[0], (B, N, DIM), jnp.float32), 'wqkv': jax.random.normal(ks[1], (DEPTH, DIM, 3 * INNER), jnp.float32) * 0.02, 'q_scale': jnp.ones((DEPTH, DIM_HEAD), jnp.float32), 'k_scale': jnp.ones((DEPTH, DIM_HEAD), jnp.float32), 'wo': jax.random.normal(ks[2], (DEPTH, INNER, DIM), jnp.float32) * 0.02, 'ln_g': jnp.ones((DEPTH, DIM), jnp.float32), 'ln_b': jnp.zeros((DEPTH, DIM), jnp.float32), 'w1': jax.random.normal(ks[3], (DEPTH, DIM, 2 * HID), jnp.float32) * 0.02, 'b1': jnp.zeros((DEPTH, 2 * HID), jnp.float32), 'w2': jax.random.normal(ks[4], (DEPTH, HID, DIM), jnp.float32) * 0.02, 'b2': jnp.zeros((DEPTH, DIM), jnp.float32)}
    _L0_ffn_in = _L0_ffn_setup()
    _d = {'L0_attn_x': _L0_attn_in['x'], 'L0_attn_Wq': _L0_attn_in['Wq'], 'L0_attn_Wk': _L0_attn_in['Wk'], 'L0_attn_Wv': _L0_attn_in['Wv'], 'L0_attn_Wo': _L0_attn_in['Wo'], 'L0_ffn_wqkv': _L0_ffn_in['wqkv'], 'L0_ffn_q_scale': _L0_ffn_in['q_scale'], 'L0_ffn_k_scale': _L0_ffn_in['k_scale'], 'L0_ffn_wo': _L0_ffn_in['wo'], 'L0_ffn_ln_g': _L0_ffn_in['ln_g'], 'L0_ffn_ln_b': _L0_ffn_in['ln_b'], 'L0_ffn_w1': _L0_ffn_in['w1'], 'L0_ffn_b1': _L0_ffn_in['b1'], 'L0_ffn_w2': _L0_ffn_in['w2'], 'L0_ffn_b2': _L0_ffn_in['b2']}
    _x0 = _d['L0_attn_x']
    _d['L0_attn_x'] = jax.random.normal(jax.random.fold_in(jax.random.key(seed), 1), (1, 2048, 128), dtype=_x0.dtype)
    del _x0
    return _d

def reference(L0_attn_x, L0_attn_Wq, L0_attn_Wk, L0_attn_Wv, L0_attn_Wo, L0_ffn_wqkv, L0_ffn_q_scale, L0_ffn_k_scale, L0_ffn_wo, L0_ffn_ln_g, L0_ffn_ln_b, L0_ffn_w1, L0_ffn_b1, L0_ffn_w2, L0_ffn_b2):

    def _L0_attn_ref(x, Wq, Wk, Wv, Wo):
        import jax, jax.numpy as jnp
        import numpy as np
        D_MODEL = 128
        N_HEADS = 16
        HEAD_DIM = D_MODEL // N_HEADS
        ROPE_BASE = 10000.0

        def _rope(q, k):
            S, Dh = (q.shape[1], q.shape[-1])
            inv_freq = 1.0 / ROPE_BASE ** (jnp.arange(0, Dh, 2, dtype=jnp.float32) / Dh)
            t = jnp.arange(S, dtype=jnp.float32)
            freqs = jnp.outer(t, inv_freq)
            emb = jnp.concatenate([freqs, freqs], axis=-1)
            cos = jnp.cos(emb)[None, :, None, :]
            sin = jnp.sin(emb)[None, :, None, :]

            def rotate_half(v):
                v1, v2 = (v[..., :Dh // 2], v[..., Dh // 2:])
                return jnp.concatenate([-v2, v1], axis=-1)
            return (q * cos + rotate_half(q) * sin, k * cos + rotate_half(k) * sin)
        B, S, _ = x.shape
        H, Dh = (N_HEADS, HEAD_DIM)
        q = (x @ Wq.T).reshape(B, S, H, Dh)
        k = (x @ Wk.T).reshape(B, S, H, Dh)
        v = (x @ Wv.T).reshape(B, S, H, Dh)
        q, k = _rope(q, k)
        scale = 1.0 / np.sqrt(Dh)
        scores = jnp.einsum('bqhd,bkhd->bhqk', q, k) * scale
        causal = jnp.triu(jnp.ones((S, S), dtype=bool), k=1)
        scores = jnp.where(causal, -jnp.inf, scores)
        attn = jax.nn.softmax(scores, axis=-1)
        out = jnp.einsum('bhqk,bkhd->bqhd', attn, v).reshape(B, S, H * Dh)
        return out @ Wo.T

    def _L0_ffn_ref(x, wqkv, q_scale, k_scale, wo, ln_g, ln_b, w1, b1, w2, b2):
        import jax, jax.numpy as jnp
        import numpy as np
        DIM = 128
        DEPTH = 2
        HEADS = 8
        DIM_HEAD = 64
        WINDOW = 64
        INNER = HEADS * DIM_HEAD
        HID = int(DIM * 4 * 2 / 3)
        B, N = (2, 1024)
        QK_SCALE = 8.0

        def shift_token(t):
            t1, t2 = jnp.split(t, 2, axis=-1)
            t2 = jnp.pad(t2, ((0, 0), (1, 0), (0, 0)))[:, :-1]
            return jnp.concatenate([t1, t2], axis=-1)

        def l2norm(t):
            return t / jnp.clip(jnp.linalg.norm(t, axis=-1, keepdims=True), 1e-12)

        def rotate_half(x):
            x1, x2 = jnp.split(x, 2, axis=-1)
            return jnp.concatenate([-x2, x1], axis=-1)

        def rotary_xpos(q, k):
            n = q.shape[-2]
            half_idx = jnp.arange(0, DIM_HEAD, 2, dtype=jnp.float32)
            inv_freq = 1.0 / 10000.0 ** (half_idx / DIM_HEAD)
            t = jnp.arange(n, dtype=jnp.float32)
            freqs = t[:, None] * inv_freq[None, :]
            freqs = jnp.concatenate([freqs, freqs], axis=-1)
            base = (half_idx + 0.4 * DIM_HEAD) / (1.4 * DIM_HEAD)
            power = (t - n // 2) / float(WINDOW // 2)
            scale = base[None, :] ** power[:, None]
            scale = jnp.concatenate([scale, scale], axis=-1)
            cos, sin = (jnp.cos(freqs), jnp.sin(freqs))
            q = q * cos * scale + rotate_half(q) * sin * scale
            k = k * cos / scale + rotate_half(k) * sin / scale
            return (q, k)

        def local_attention(q, k, v):
            b, h, n, d = q.shape
            w = n // WINDOW
            bq = q.reshape(b, h, w, WINDOW, d) * QK_SCALE
            bk = k.reshape(b, h, w, WINDOW, d)
            bv = v.reshape(b, h, w, WINDOW, d)

            def look_around(t):
                p = jnp.pad(t, ((0, 0), (0, 0), (1, 0), (0, 0), (0, 0)))
                return jnp.concatenate([p[:, :, :w], p[:, :, 1:]], axis=3)
            bk, bv = (look_around(bk), look_around(bv))
            bt = jnp.arange(n).reshape(w, WINDOW)
            btp = jnp.pad(bt, ((1, 0), (0, 0)), constant_values=-1)
            btk = jnp.concatenate([btp[:w], btp[1:]], axis=1)
            sim = jnp.einsum('bhwid,bhwjd->bhwij', bq, bk)
            i = bt[:, :, None]
            j = btk[:, None, :]
            mask = (i < j) | (i > j + WINDOW) | (j == -1)
            sim = jnp.where(mask, -jnp.finfo(sim.dtype).max, sim)
            attn = jax.nn.softmax(sim, axis=-1)
            out = jnp.einsum('bhwij,bhwjd->bhwid', attn, bv)
            return out.reshape(b, h, n, d)

        def _layer(x, wqkv, qs, ksc, wo, lg, lb, w1, b1, w2, b2):
            b, n, _ = x.shape
            h = shift_token(x)
            qkv = h @ wqkv
            q, k, v = jnp.split(qkv, 3, axis=-1)
            to_heads = lambda t: t.reshape(b, n, HEADS, DIM_HEAD).transpose(0, 2, 1, 3)
            q, k, v = (to_heads(q), to_heads(k), to_heads(v))
            q = l2norm(q) * qs
            k = l2norm(k) * ksc
            q, k = rotary_xpos(q, k)
            o = local_attention(q, k, v)
            o = o.transpose(0, 2, 1, 3).reshape(b, n, INNER)
            x = x + o @ wo
            h = shift_token(x)
            mu = h.mean(-1, keepdims=True)
            var = h.var(-1, keepdims=True)
            h = (h - mu) / jnp.sqrt(var + 1e-05) * lg + lb
            h = h @ w1 + b1
            a, g = jnp.split(h, 2, axis=-1)
            h = a * jax.nn.gelu(g, approximate=False)
            x = x + h @ w2 + b2
            return x
        for l in range(DEPTH):
            x = _layer(x, wqkv[l], q_scale[l], k_scale[l], wo[l], ln_g[l], ln_b[l], w1[l], b1[l], w2[l], b2[l])
        return x
    x = L0_attn_x
    x = x + _L0_attn_ref(_layernorm(x, axis=-1), L0_attn_Wq, L0_attn_Wk, L0_attn_Wv, L0_attn_Wo)
    x = x + _L0_ffn_ref(_layernorm(x, axis=-1), L0_ffn_wqkv, L0_ffn_q_scale, L0_ffn_k_scale, L0_ffn_wo, L0_ffn_ln_g, L0_ffn_ln_b, L0_ffn_w1, L0_ffn_b1, L0_ffn_w2, L0_ffn_b2)
    return x

_drawn_inputs = setup_inputs


def setup_inputs(seed=0):
    import zlib

    import numpy as np

    out = dict(_drawn_inputs(seed))
    spreads = {'L0_ffn_q_scale': (1.0, 0.6),
     'L0_ffn_k_scale': (1.0, 0.6),
     'L0_ffn_ln_g': (1.0, 0.6),
     'L0_ffn_ln_b': (0.0, 0.8),
     'L0_ffn_b1': (0.0, 0.8),
     'L0_ffn_b2': (0.0, 0.418)}
    factors = {'L0_ffn_wqkv': 3.945, 'L0_ffn_wo': 3.963, 'L0_ffn_w1': 6.184, 'L0_ffn_w2': 6.089}
    for name, (base, spread) in spreads.items():
        noise = np.random.default_rng([zlib.crc32(name.encode()), seed]).standard_normal(out[name].shape)
        drawn = base * np.exp(spread * noise) if base else spread * noise
        out[name] = jnp.asarray(drawn.astype(out[name].dtype))
    for name, factor in factors.items():
        out[name] = (out[name] * factor).astype(out[name].dtype)
    return out
```

```python
from contextlib import ExitStack

import numpy as np

import concourse.bass as bass
from concourse import mybir

F32 = mybir.dt.float32
BF16 = mybir.dt.bfloat16
ALU = mybir.AluOpType
ACT = mybir.ActivationFunctionType
X_AXIS = mybir.AxisListType.X

P = 128
S = 2048
D = 128
T = S // P
BLK = 512
NB = S // BLK
TPB = BLK // P
H = 16
DH = D // H
PAIRS = H // 2
GROUPS = H // 4
HALF = 64
SPLIT = 6 * DH
SROWS = SPLIT + 2
VW = 32
NEG = -1e30
CHUNKS = [(q, g) for q in (1, 2, 3, 0) for g in range(GROUPS)]
NC = len(CHUNKS)

LH = 8
LD = 64
WIN = 64
INNER = LH * LD
HID = 341
HCH = (128, 128, 85)
LAYERS = 2
KEYS = WIN + P


def max_units(q, g):
    return [(t, pair, c, par) for t in range(TPB * q, TPB * (q + 1)) for pair in (2 * g, 2 * g + 1)
            for c in range(t // TPB + 1) for par in range(2)]


def share(units, i, n):
    return units[len(units) * i // n:len(units) * (i + 1) // n]


def build(nc, a, out):
    with ExitStack() as ctx:
        def sb(name, shape, dt=F32):
            return ctx.enter_context(nc.sbuf_tensor(name, shape, dt))

        keep = {
            "ps": ctx.enter_context(nc.psum_tensor("ps", [P, 8, BLK], F32)),
            "x": sb("x_rows", [P, T, D]),
            "ident": sb("ident", [P, P]),
            "identb": sb("identb", [P, P], BF16),
            "half": sb("minus_half", [P, 16]),
            "mv": sb("mean_var", [P, T, 2]),
            "rstd": sb("rstd", [P, T]),
            "stat": sb("stat", [P, 2, 6]),
        }
        with ExitStack() as attn:
            first_attention(nc, attn, a, keep)
        with ExitStack() as ffn:
            layers(nc, ffn, a, keep, out)


def first_attention(nc, ctx, a, keep):
    def sb(name, shape, dt=F32):
        return ctx.enter_context(nc.sbuf_tensor(name, shape, dt))

    def sem(name):
        return ctx.enter_context(nc.semaphore(name))

    ps, x, ident, identb = keep["ps"], keep["x"], keep["ident"], keep["identb"]
    half, mv, rstd, stat = keep["half"], keep["mv"], keep["rstd"], keep["stat"]

    early = sb("early", [P, 4, S])
    xn = early[:, 0, :].rearrange("p (t c) -> p t c", t=T)
    xT = early[:, 1, :]
    rope = early[:, 2:4, :]
    outT = early
    wqk = sb("wqk", [P, 4, D])
    wv = sb("wv", [P, D])
    wo = sb("wo_t", [P, D])
    mask_q = sb("mask_q", [P, P], BF16)
    mask_k = sb("mask_k", [P, P], BF16)
    pick = sb("pick", [P, 4 * 9])
    probs = sb("probs", [P, 2, 2, 2, BLK])
    prod = probs[:, 0, :, :, :]
    full = probs[:, 1, 0, :, :]
    rest = probs[:, 1, 1, :, :]
    part = sb("split_part", [P, 2, 2, 3, BLK], BF16)
    qs = sb("q_stack", [P, NB, PAIRS, BLK], BF16)
    ks = sb("k_stack", [P, 2, NB, PAIRS, BLK], BF16)
    v = sb("v_rows", [P, T, H, VW])
    mpart = sb("max_part", [P, TPB, 4, NB])
    mneg = sb("max_neg", [P, 2, TPB, 4])
    mrow = sb("max_rows", [4, 2, BLK], BF16)
    rden = sb("rden", [P, 2, H])
    on = sb("o_norm", [P, 2, D])
    onT = sb("o_norm_t", [P, BLK])

    s_x, s_w, s_rope, s_const = sem("x_loaded"), sem("weights_loaded"), sem("rope_loaded"), sem("const_loaded")
    s_half, s_vset = sem("half_set"), sem("v_ones_set")
    s_dve, s_dstat = sem("dve_chain"), sem("stats_done")
    s_pool, s_rstd = sem("pool_chain"), sem("rstd_done")
    s_xn, s_xt, s_xtc = sem("xn_done"), sem("xt_turned"), sem("xt_copied")
    s_proj, s_v, s_vc = sem("projected"), sem("v_projected"), sem("v_copied")
    s_prod, s_full, s_high, s_rest, s_mid, s_low = (sem(n) for n in (
        "rope_products", "rope_sum", "high_part", "rest_left", "middle_part", "low_part"))
    s_stack = [sem(f"stacked{b}") for b in range(NB)]
    s_ones, s_zero = sem("ones_rows"), sem("stacks_zeroed")
    s_spread = [sem(f"spread{b}") for b in range(NB)]
    spread = nc.dram_tensor("spread", (NB, 2, 3, 2, DH, PAIRS * BLK), BF16, kind="Internal").ap()

    with nc.Block() as block:
        @block.sync
        def _(sp):
            sp.dma_start(x[:, :, :], a["x"].rearrange("(t p) c -> p t c", p=P)).then_inc(s_x, 16)
            sp.dma_start(ident[:, :], a["ident"]).then_inc(s_const, 16)
            sp.dma_start(wqk[:, :, :], a["wqk"].rearrange("n c f -> c n f")).then_inc(s_w, 16)
            sp.dma_start(wv[:, :], a["wv"]).then_inc(s_w, 16)
            sp.dma_start(wo[:, :], a["wo"]).then_inc(s_w, 16)
            sp.dma_start(rope[:, :, :], a["rope"].rearrange("n r s -> r n s")).then_inc(s_rope, 16)
            for dst, name in ((identb, "identb"), (mask_q, "mask_q"), (mask_k, "mask_k"), (pick, "pick")):
                sp.dma_start(dst[:, :], a[name]).then_inc(s_const, 16)
            for par in range(2):
                at = HALF * par + SPLIT
                if par == 0:
                    sp.wait_ge(s_zero, 2)
                sp.dma_start(ks[at:at + 2, par, :, :, :].rearrange("r b n s -> r (b n s)"), a["ones"]).then_inc(s_ones, 16)
            for b in range(NB):
                sp.wait_ge(s_low, 2 * b + 2)
                sp.dma_start(spread[b].rearrange("i w par d (n s) -> (par d n) (i w) s", s=BLK),
                             part[:, b % 2, :, :, :].rearrange("p i w s -> p (i w) s")).then_inc(s_spread[b], 16)
                sp.wait_ge(s_spread[b], 16)
                for par in range(2):
                    at = HALF * par
                    row = at
                    for w, times in ((0, 3), (1, 2), (2, 1)):
                        sp.dma_start(qs[row:row + DH * times, b, :, :].rearrange("r n s -> r (n s)"),
                                     spread[b, 0, w:w + 1, par].to_broadcast([times, DH, PAIRS * BLK])
                                     ).then_inc(s_stack[b], 16)
                        sp.dma_start(ks[row:row + DH * times, par, b, :, :].rearrange("r n s -> r (n s)"),
                                     spread[b, 1, 0:times, par]).then_inc(s_stack[b], 16)
                        row += DH * times
            for b in range(NB):
                sp.wait_ge(s_stack[b], 16 * 12)
            sp.wait_ge(s_ones, 32)

        @block.gpsimd
        def _(pool):
            pool.memset(half[:, :], -0.5).then_inc(s_half, 1)
            pool.memset(qs[:, :, :, :].rearrange("p b n s -> p (b n s)").bitcast(F32), 0.0).then_inc(s_zero, 1)
            pool.memset(ks[:, :, :, :, :].rearrange("p a b n s -> p (a b n s)").bitcast(F32), 0.0).then_inc(s_zero, 1)
            pool.memset(v[:, :, :, :], 0.0).then_inc(s_vset, 1)
            pool.wait_ge(s_vset, 1)
            pool.memset(v[:, :, :, DH:DH + 1], 1.0).then_inc(s_vset, 1)
            pool.wait_ge(s_half, 1)
            pool.wait_ge(s_dstat, 1)
            pool.tensor_scalar(rstd[:, :], mv[:, :, 1], 1e-5, None, ALU.add).then_inc(s_pool, 1)
            pool.wait_ge(s_pool, 1)
            pool.tensor_tensor(rstd[:, :], rstd[:, :], half[:, :], ALU.pow).then_inc(s_rstd, 1)
            for n in range(2 * NB):
                pool.wait_ge(s_prod, 2 * n + 2)
                if n >= 2:
                    pool.wait_ge(s_rest, n - 1)
                pool.tensor_tensor(full[:, n % 2, :], prod[:, n % 2, 0, :], prod[:, n % 2, 1, :],
                                   ALU.add).then_inc(s_full, 1)

        @block.vector
        def _(dve):
            count = [0]

            def link(ins):
                count[0] += 1
                ins.then_inc(s_dve, 1)
                dve.wait_ge(s_dve, count[0])

            dve.wait_ge(s_x, 16)
            for t in range(T):
                link(dve.bn_stats(stat[:, t % 2, :], x[:, t, :]))
                ins = dve.bn_aggr(mv[:, t, :], stat[:, t % 2, :])
                if t == T - 1:
                    ins.then_inc(s_dstat, 1)
                else:
                    link(ins)
            dve.wait_ge(s_rstd, 1)
            for t in range(T):
                dve.tensor_scalar(xn[:, t, :], x[:, t, :], mv[:, t, 0:1], rstd[:, t:t + 1],
                                  ALU.subtract, ALU.mult).then_inc(s_xn, 1)
            dve.wait_ge(s_rope, 16)

            def products(n):
                b, i = divmod(n, 2)
                dve.wait_ge(s_proj, 2 * n + 2)
                if n >= 2:
                    dve.wait_ge(s_full, n - 1)
                for k in range(2):
                    dve.tensor_tensor(prod[:, i, k, :], ps[:, 2 + 2 * i + k, :], rope[:, k, b * BLK:(b + 1) * BLK],
                                      ALU.mult).then_inc(s_prod, 1)

            def lower(n):
                b, i = divmod(n, 2)
                dve.wait_ge(s_high, n + 1)
                if n >= 2:
                    dve.wait_ge(s_low, n - 1)
                dve.tensor_tensor(rest[:, i, :], full[:, i, :], part[:, b % 2, i, 0, :],
                                  ALU.subtract).then_inc(s_rest, 1)
                dve.wait_ge(s_rest, n + 1)
                dve.wait_ge(s_mid, n + 1)
                dve.tensor_tensor(part[:, b % 2, i, 2, :], rest[:, i, :], part[:, b % 2, i, 1, :],
                                  ALU.subtract).then_inc(s_low, 1)

            for n in range(2 * NB + 1):
                if n < 2 * NB:
                    products(n)
                if n >= 1:
                    lower(n - 1)

        @block.scalar
        def _(act):
            def copy_turned(b):
                act.wait_ge(s_xt, TPB * (b + 1))
                act.activation(xT[:, b * BLK:(b + 1) * BLK], ps[:, b % 2, :], ACT.Copy).then_inc(s_xtc, 1)

            copy_turned(0)
            for b in range(NB):
                if b + 1 < NB:
                    copy_turned(b + 1)
                act.wait_ge(s_v, b + 1)
                act.wait_ge(s_vset, 2)
                act.activation(v[:, TPB * b:TPB * (b + 1), :, 0:DH],
                               ps[:, 6, :].rearrange("p (t h d) -> p t h d", t=TPB, h=H), ACT.Copy).then_inc(s_vc, 1)
                for i in range(2):
                    n = 2 * b + i
                    act.wait_ge(s_full, n + 1)
                    if b >= 2:
                        act.wait_ge(s_spread[b - 2], 16)
                    act.activation(part[:, b % 2, i, 0, :], full[:, i, :], ACT.Copy).then_inc(s_high, 1)
                    act.wait_ge(s_rest, n + 1)
                    act.activation(part[:, b % 2, i, 1, :], rest[:, i, :], ACT.Copy).then_inc(s_mid, 1)

        @block.tensor
        def _(pe):
            pe.wait_ge(s_const, 16 * 5)
            pe.wait_ge(s_w, 48)

            def turn(b):
                if b >= 2:
                    pe.wait_ge(s_xtc, b - 1)
                for j in range(TPB):
                    t = TPB * b + j
                    pe.wait_ge(s_xn, t + 1)
                    pe.transpose(ps[:, b % 2, j * P:(j + 1) * P], xn[:, t, :], ident[:, :]).then_inc(s_xt, 1)

            def project(b):
                pe.wait_ge(s_xtc, b + 1)
                if b >= 1:
                    pe.wait_ge(s_vc, b)
                for j in range(TPB):
                    t = TPB * b + j
                    mm = pe.matmul(ps[:, 6, j * P:(j + 1) * P], xT[:, t * P:(t + 1) * P], wv[:, :],
                                   start=True, stop=True)
                mm.then_inc(s_v, 1)
                for i in range(2):
                    if b >= 1:
                        pe.wait_ge(s_prod, 4 * (b - 1) + 2 * i + 2)
                    for k in range(2):
                        pe.matmul(ps[:, 2 + 2 * i + k, :], wqk[:, 2 * i + k, :], xT[:, b * BLK:(b + 1) * BLK],
                                  start=True, stop=True).then_inc(s_proj, 1)

            turn(0)
            for b in range(NB):
                if b + 1 < NB:
                    turn(b + 1)
                project(b)

    OB, SM, RING = 4, 5, 3
    scale = float(DH) ** -0.5
    s_sm, s_smr = sem("max_scores"), sem("max_taken")
    s_mneg, s_mh = sem("row_max"), sem("max_high")
    s_mrow = [sem(f"max_rows_in{i}") for i in range(2)]
    s_st, s_e, s_av, s_oc = sem("scores"), sem("exps"), sem("values"), sem("out_copied")

    units, step_at = [], []
    for q, g in CHUNKS:
        units.append(max_units(q, g))
        step_at.append(step_at[-1] + TPB * (CHUNKS[len(step_at) - 1][0] + 1) if step_at else 0)

    def n_steps(k):
        return TPB * (CHUNKS[k][0] + 1) if k >= 0 else 1

    def beside(k, i, third):
        mine = range(len(units[k + 2])) if k + 2 < NC and i < n_steps(k) else []
        return share(mine, 3 * i + third, 3 * n_steps(k))

    slot, turn_slot = {}, {}
    for k in range(-2, NC):
        for i in range(n_steps(k) + 1):
            for third in range(3):
                for n in beside(k, i, third):
                    slot[k + 2, n] = len(slot) + len(turn_slot)
            if i == 0 and 0 <= k + 1 < NC:
                turn_slot[k + 1] = len(slot) + len(turn_slot)

    with nc.Block() as block:
        @block.tensor
        def _(pe):
            def max_scores(k, n):
                t, pair, c, par = units[k][n]
                n = slot[k, n]
                width = min(BLK, P * (t + 1) - BLK * c)
                if n >= RING:
                    pe.wait_ge(s_smr, n - RING + 1)
                last = c == t // TPB
                dst = ps[:, SM + n % RING, :]
                mm = pe.matmul(dst[:, 0:width], qs[:, t // TPB, pair, t % TPB * P:(t % TPB + 1) * P],
                               ks[:, par, c, pair, 0:width], start=True, stop=not last)
                if last:
                    mm = pe.matmul(dst[:, width - P:width], identb[:, :], mask_q[:, :], start=False, stop=True)
                mm.then_inc(s_sm, 1)

            def scores(k, kt, pr):
                q, g = CHUNKS[k]
                n = 2 * (step_at[k] + kt) + pr
                off = max(0, kt - TPB * q) * P
                pair = 2 * g + pr
                if n >= 2:
                    pe.wait_ge(s_e, n - 1)
                diag = kt >= TPB * q
                for par in range(2):
                    dst = ps[:, 2 * (n % 2) + par, 0:BLK - off]
                    mm = pe.matmul(dst, ks[:, par, kt // TPB, pair, kt % TPB * P:(kt % TPB + 1) * P],
                                   qs[:, q, pair, off:BLK], start=True, stop=not diag)
                if diag:
                    for par in range(2):
                        mm = pe.matmul(ps[:, 2 * (n % 2) + par, 0:P], identb[:, :], mask_k[:, :],
                                       start=False, stop=True)
                mm.then_inc(s_st, 1)

            def values(k, kt):
                q, g = CHUNKS[k]
                n = step_at[k] + kt
                off = max(0, kt - TPB * q) * P
                pe.wait_ge(s_e, 2 * n + 2)
                if kt == 0 and k >= 1:
                    pe.wait_ge(s_oc, k)
                for j in range(4):
                    mm = pe.matmul(ps[VW * j:VW * (j + 1), OB, off:BLK], v[:, kt, 4 * g + j, :],
                                   probs[:, n % 2, j // 2, j % 2, 0:BLK - off],
                                   start=kt == 0, stop=kt == TPB * (q + 1) - 1)
                mm.then_inc(s_av, 1)

            def turn_max(k):
                n = turn_slot[k]
                pe.wait_ge(s_mneg, TPB * (k + 1))
                if n >= RING:
                    pe.wait_ge(s_smr, n - RING + 1)
                for j in range(TPB):
                    mm = pe.transpose(ps[0:4, SM + n % RING, j * P:(j + 1) * P], mneg[:, k % 2, j, :], ident[:, :])
                mm.then_inc(s_sm, 1)

            for k in range(-2, NC):
                if k >= 0:
                    pe.wait_ge(s_mrow[k % 2], 64 * (k // 2 + 1))
                for i in range(n_steps(k) + 1):
                    for third in range(3):
                        if k >= 0 and third < 2 and i < n_steps(k):
                            scores(k, i, third)
                        if k >= 0 and third == 2 and i >= 1:
                            values(k, i - 1)
                        for n in beside(k, i, third):
                            max_scores(k + 2, n)
                    if i == 0 and 0 <= k + 1 < NC:
                        turn_max(k + 1)

        @block.scalar
        def _(act):
            for k, (q, g) in enumerate(CHUNKS):
                for kt in range(n_steps(k)):
                    off = max(0, kt - TPB * q) * P
                    for pr in range(2):
                        n = 2 * (step_at[k] + kt) + pr
                        act.wait_ge(s_st, n + 1)
                        if n >= 4:
                            act.wait_ge(s_av, n // 2 - 1)
                        act.activation(probs[:, n // 2 % 2, pr, :, 0:BLK - off],
                                       ps[:, 2 * (n % 2):2 * (n % 2) + 2, 0:BLK - off], ACT.Exp,
                                       scale=scale).then_inc(s_e, 1)

        @block.vector
        def _(dve):
            def take_max(k, n):
                t, pair, c, par = units[k][n]
                width = min(BLK, P * (t + 1) - BLK * c)
                dve.wait_ge(s_sm, slot[k, n] + 1)
                at = 2 * par + pair % 2
                dve.tensor_reduce(mpart[:, t % TPB, at, c:c + 1], ps[:, SM + slot[k, n] % RING, 0:width], X_AXIS,
                                  ALU.max).then_inc(s_smr, 1)
                if n + 1 == len(units[k]) or units[k][n + 1][0] != t:
                    dve.wait_ge(s_smr, slot[k, n] + 1)
                    if k >= 2:
                        dve.wait_ge(s_sm, turn_slot[k - 2] + 1)
                    dve.tensor_reduce(mneg[:, k % 2, t % TPB, :], mpart[:, t % TPB, :, 0:t // TPB + 1], X_AXIS,
                                      ALU.max, negate=True).then_inc(s_mneg, 1)

            def copy_out(k):
                q, g = CHUNKS[k]
                dve.wait_ge(s_av, step_at[k] + n_steps(k))
                dve.tensor_copy(outT[:, g, q * BLK:(q + 1) * BLK], ps[:, OB, :]).then_inc(s_oc, 1)

            def split_max(k):
                n = turn_slot[k]
                dve.wait_ge(s_sm, n + 1)
                turned = ps[0:4, SM + n % RING, :]
                if k >= 1:
                    dve.wait_ge(s_mrow[(k - 1) % 2], 64 * ((k - 1) // 2 + 1))
                dve.tensor_copy(mrow[:, 0, :], turned).then_inc(s_mh, 1)
                dve.wait_ge(s_mh, k + 1)
                dve.tensor_tensor(mrow[:, 1, :], turned, mrow[:, 0, :], ALU.subtract).then_inc(s_smr, 1)

            for k in range(-2, NC):
                for i in range(n_steps(k) + 1):
                    for third in range(3):
                        for n in beside(k, i, third):
                            take_max(k + 2, n)
                    if i == 0 and 0 <= k + 1 < NC:
                        split_max(k + 1)
                if k >= 0:
                    copy_out(k)

        @block.sync
        def _(sp):
            for k, (q, g) in enumerate(CHUNKS):
                sp.wait_ge(s_smr, turn_slot[k] + 1)
                for w in range(2):
                    for par in range(2):
                        at = HALF * par + SPLIT + w
                        sp.dma_start(qs[at:at + 1, q, 2 * g:2 * g + 2, :],
                                     mrow[2 * par:2 * par + 2, w, :]).then_inc(s_mrow[k % 2], 16)
            for k in (NC - 2, NC - 1):
                sp.wait_ge(s_mrow[k % 2], 64 * (k // 2 + 1))

    s_pick, s_rd, s_on, s_ont, s_ontc, s_y, s_yadd = (sem(n) for n in (
        "picked", "rden_done", "o_normed", "o_turned", "o_turned_copied", "o_projected", "o_added"))
    with nc.Block() as block:
        @block.tensor
        def _(pe):
            def gather(t):
                if t >= 2:
                    pe.wait_ge(s_on, t - 1)
                for g in range(GROUPS):
                    mm = pe.matmul(ps[:, t % 2, 36 * g:36 * (g + 1)], outT[:, g, t * P:(t + 1) * P], pick[:, :],
                                   start=True, stop=True)
                mm.then_inc(s_pick, 1)

            def turn(t):
                pe.wait_ge(s_on, t + 1)
                if t >= 2:
                    pe.wait_ge(s_ontc, t - 1)
                pe.transpose(ps[:, 2 + t % 2, 0:P], on[:, t % 2, :], ident[:, :]).then_inc(s_ont, 1)

            def project(t):
                pe.wait_ge(s_ontc, t + 1)
                if t >= 2:
                    pe.wait_ge(s_yadd, t - 1)
                pe.matmul(ps[:, 4 + t % 2, 0:D], onT[:, (t % 2) * P:(t % 2) * P + P], wo[:, :],
                          start=True, stop=True).then_inc(s_y, 1)

            for i in range(T + 2):
                if i < T:
                    gather(i)
                if 0 <= i - 1 < T:
                    turn(i - 1)
                if 0 <= i - 2 < T:
                    project(i - 2)

        @block.vector
        def _(dve):
            def norm(t):
                dve.wait_ge(s_pick, t + 1)
                got = ps[:, t % 2, 0:H * 9].rearrange("p (h d) -> p h d", d=9)
                dve.reciprocal(rden[:, t % 2, :], got[:, :, DH]).then_inc(s_rd, 1)
                dve.wait_ge(s_rd, t + 1)
                if t >= 2:
                    dve.wait_ge(s_ont, t - 1)
                dve.tensor_tensor(on[:, t % 2, :].rearrange("p (h d) -> p h d", d=DH), got[:, :, 0:DH],
                                  rden[:, t % 2, :].unsqueeze(2).to_broadcast([P, H, DH]), ALU.mult).then_inc(s_on, 1)

            def add(t):
                dve.wait_ge(s_y, t + 1)
                dve.tensor_tensor(x[:, t, :], x[:, t, :], ps[:, 4 + t % 2, 0:D], ALU.add).then_inc(s_yadd, 1)

            for i in range(T + 3):
                if i < T:
                    norm(i)
                if 0 <= i - 3 < T:
                    add(i - 3)

        @block.scalar
        def _(act):
            for t in range(T):
                act.wait_ge(s_ont, t + 1)
                if t >= 2:
                    act.wait_ge(s_y, t - 1)
                act.activation(onT[:, (t % 2) * P:(t % 2) * P + P], ps[:, 2 + t % 2, 0:P],
                               ACT.Copy).then_inc(s_ontc, 1)


def layers(nc, ctx, a, keep, out):
    def sb(name, shape, dt=F32):
        return ctx.enter_context(nc.sbuf_tensor(name, shape, dt))

    def sem(name):
        return ctx.enter_context(nc.semaphore(name))

    w = {
        "xs": sb("xs", [P, T, D]),
        "xa": sb("xa", [P, T, D]),
        "hT": sb("h_t", [P, WIN + S]),
        "wqkv": sb("wqkv", [P, LAYERS, 3 * INNER]),
        "wo": sb("wo_l", [P, LAYERS, INNER // P, D]),
        "w1": sb("w1", [P, LAYERS, 2 * HID]),
        "w2": sb("w2", [P, LAYERS, len(HCH), D]),
        "gb": sb("ln_gb", [P, LAYERS, 2]),
        "b1": sb("b1", [P, LAYERS, 2, len(HCH)]),
        "b2": sb("b2", [1, LAYERS, D]),
        "onesr": sb("ones_row", [1, P]),
        "tab": sb("xpos_tab", [P, 2, T, 2, LD]),
        "qks": sb("qk_scale", [P, LAYERS, 2, LD]),
        "qkT": sb("qk_t", [P, 2, INNER // P, WIN + S]),
        "v": sb("v_l", [P, T + 1, LH, LD + 1]),
        "mask": sb("mask_l", [P, 2, KEYS], BF16),
        "shift": sb("shift", [P, 2, P]),
        "work": sb("work", [P, 7 * 1024]),
    }
    xs, tab, qks = w["xs"], w["tab"], w["qks"]
    x, mv, rstd, stat, half = keep["x"], keep["mv"], keep["rstd"], keep["stat"], keep["half"]
    s_lw, s_tab, s_zero, s_scaled = sem("layer_weights"), sem("tables_in"), sem("pads_zeroed"), sem("tables_scaled")
    s_dve, s_stat, s_pool, s_rstd, s_xs = (sem(n) for n in (
        "l_dve_chain", "l_stats", "l_pool_chain", "l_rstd", "l_xs"))

    with nc.Block() as block:
        @block.sync
        def _(sp):
            for i, n in enumerate(("q_scale", "k_scale")):
                sp.dma_start(qks[:, :, i, :], a[n].unsqueeze(0).to_broadcast([P, LAYERS, LD])).then_inc(s_tab, 16)
            for i in range(2):
                sp.dma_start(tab[:, i, :, :, :], a["xpos"][i]).then_inc(s_tab, 16)
            for dst, src in (
                (w["wqkv"][:, :, :], a["wqkv"].rearrange("l c f -> c l f")),
                (w["w1"][:, :, :], a["w1"].rearrange("l c f -> c l f")),
                (w["mask"][:, :, :], a["mask_l"]),
                (w["shift"][:, :, :], a["shift"]),
                (w["b2"][:, :, :], a["b2"].unsqueeze(0)),
                (w["onesr"][:, :], a["ones_row"]),
                (w["gb"][:, :, :], a["ln_gb"]),
                (w["b1"][:, :, :, :], a["b1"]),
            ):
                sp.dma_start(dst, src).then_inc(s_lw, 16)
            for layer in range(LAYERS):
                sp.dma_start(w["wo"][:, layer, :, :], a["lwo"][layer].rearrange("(c p) n -> p c n", p=P)).then_inc(s_lw, 16)
                for c, rows in enumerate(HCH):
                    at = c * P
                    sp.dma_start(w["w2"][0:rows, layer, c, :], a["w2"][layer, at:at + rows, :]).then_inc(s_lw, 16)
            sp.wait_ge(s_lw, 16 * (8 + LAYERS * (1 + len(HCH))))

        @block.gpsimd
        def _(pool):
            pool.memset(w["hT"][:, 0:WIN + 1], 0.0).then_inc(s_zero, 1)
            pool.memset(w["qkT"][:, 1, :, 0:WIN], 0.0).then_inc(s_zero, 1)
            pool.memset(w["v"][:, :, :, LD:LD + 1], 1.0).then_inc(s_zero, 1)
            pool.wait_ge(s_tab, 16 * 4)
            for i in range(2):
                scale_table(pool, w, 0, i).then_inc(s_scaled, 1)
                if i == 0:
                    pool.wait_ge(s_stat, 1)
                    pool.tensor_scalar(rstd[:, :], mv[:, :, 1], 1e-5, None, ALU.add).then_inc(s_pool, 1)
                    pool.wait_ge(s_pool, 1)
                    pool.tensor_tensor(rstd[:, :], rstd[:, :], half[:, :], ALU.pow).then_inc(s_rstd, 1)
            pool.wait_ge(s_zero, 3)
            pool.wait_ge(s_scaled, 2)

        @block.vector
        def _(dve):
            count = [0]

            def link(ins):
                count[0] += 1
                ins.then_inc(s_dve, 1)
                dve.wait_ge(s_dve, count[0])

            for t in range(T):
                link(dve.bn_stats(stat[:, t % 2, :], x[:, t, :]))
                ins = dve.bn_aggr(mv[:, t, :], stat[:, t % 2, :])
                if t == T - 1:
                    ins.then_inc(s_stat, 1)
                else:
                    link(ins)
            dve.wait_ge(s_rstd, 1)
            for t in range(T):
                dve.tensor_scalar(xs[:, t, :], x[:, t, :], mv[:, t, 0:1], rstd[:, t:t + 1],
                                  ALU.subtract, ALU.mult).then_inc(s_xs, 1)
            dve.wait_ge(s_xs, T)

    for layer in range(LAYERS):
        with ExitStack() as part:
            project_heads(nc, part, keep, w, layer)
        with ExitStack() as part:
            window_attention(nc, part, a, keep, w, layer)
        with ExitStack() as part:
            feed_forward(nc, part, keep, w, layer, out)


def scale_table(pool, w, layer, i):
    t4 = w["tab"][:, i, :, :, :]
    return pool.tensor_tensor(t4, t4, w["qks"][:, layer, :, :].unsqueeze(1).to_broadcast([P, T, 2, LD]), ALU.mult)


def project_heads(nc, ctx, keep, w, layer):
    def sem(name):
        return ctx.enter_context(nc.semaphore(f"{name}_{layer}"))

    ps, ident, half = keep["ps"], keep["ident"], keep["half"]
    xs, hT, qkT, v = w["xs"], w["hT"], w["qkT"], w["v"]
    straight, exchanged = w["tab"][:, 0], w["tab"][:, 1]
    NH = 2 * LH
    work = w["work"][:, :].rearrange("p (n f) -> p n f", n=7)
    sq, hat, turned, plain = work[:, 0, :], work[:, 1:3, :], work[:, 3:5, :], work[:, 5:7, :]
    norm = ctx.enter_context(nc.sbuf_tensor(f"norms_{layer}", [P, 2, 2, NH], F32))
    TURN, VB, OUT = 0, 1, 2
    s_tx, s_h, s_qk, s_v, s_vc, s_sq, s_ss, s_clip, s_inv, s_hat, s_turned, s_plain, s_sum, s_t, s_tc = (
        sem(n) for n in ("x_turned", "h_ready", "qk_ready", "v_ready", "v_copied", "squares", "square_sums", "clipped",
                         "inverse_norms", "normalised", "exchanged_part", "straight_part", "rotated", "qk_turned",
                         "qk_copied"))

    s_root = sem("norms_rooted")

    def heads(ap):
        return ap.rearrange("p (i h d) -> p i h d", i=2, d=LD)

    with nc.Block() as block:
        @block.tensor
        def _(pe):
            def turn_x(b):
                if b >= 1:
                    pe.wait_ge(s_h, 2 * b)
                for j in range(TPB):
                    mm = pe.transpose(ps[:, TURN, j * P:(j + 1) * P], xs[:, TPB * b + j, :], ident[:, :])
                mm.then_inc(s_tx, 1)

            def project(t):
                pe.wait_ge(s_h, 2 * (t // TPB + 1))
                if t >= 2:
                    pe.wait_ge(s_hat, t - 1)
                    pe.wait_ge(s_sq, t - 1)
                at = WIN + t * P
                for i in range(2):
                    mm = pe.matmul(ps[:, 4 + 2 * (t % 2) + i, :], hT[:, at:at + P],
                                   w["wqkv"][:, layer, i * INNER:(i + 1) * INNER], start=True, stop=True)
                mm.then_inc(s_qk, 1)

            def values(t):
                rows = P if t < T else WIN
                pe.wait_ge(s_h, 2 * min(t // TPB + 1, NB))
                if t >= 1:
                    pe.wait_ge(s_vc, t)
                pe.matmul(ps[0:rows, VB, :], hT[:, t * P:t * P + rows], w["wqkv"][:, layer, 2 * INNER:3 * INNER],
                          start=True, stop=True).then_inc(s_v, 1)

            def turn(t):
                pe.wait_ge(s_sum, t + 1)
                if t >= 1:
                    pe.wait_ge(s_tc, t)
                for n in range(2 * INNER // P):
                    mm = pe.transpose(ps[:, OUT + n // 4, n % 4 * P:(n % 4 + 1) * P],
                                      hat[:, t % 2, n * P:(n + 1) * P], ident[:, :])
                mm.then_inc(s_t, 1)

            turn_x(0)
            for i in range(T + 3):
                if i < T:
                    if i % TPB == 2 and i // TPB + 1 < NB:
                        turn_x(i // TPB + 1)
                    project(i)
                if i < T + 1:
                    values(i)
                if i >= 3:
                    turn(i - 3)

        @block.scalar
        def _(act):
            def copy_h(b):
                act.wait_ge(s_tx, b + 1)
                at = WIN + b * BLK
                act.activation(hT[0:D // 2, at:at + BLK], ps[0:D // 2, TURN, :], ACT.Copy).then_inc(s_h, 1)
                n = BLK if b < NB - 1 else BLK - 1
                act.activation(hT[D // 2:D, at + 1:at + 1 + n], ps[D // 2:D, TURN, 0:n], ACT.Copy).then_inc(s_h, 1)

            def copy_qk(t):
                act.wait_ge(s_t, t + 1)
                at = WIN + t * P
                act.activation(qkT[:, :, :, at:at + P],
                               ps[:, OUT:OUT + 2, :].rearrange("p i (n q) -> p i n q", q=P), ACT.Copy).then_inc(s_tc, 1)

            copy_h(0)
            for i in range(T + 3):
                if i < T:
                    if i % TPB == 2 and i // TPB + 1 < NB:
                        copy_h(i // TPB + 1)
                    act.wait_ge(s_qk, i + 1)
                    act.activation(sq, ps[:, 4 + 2 * (i % 2):6 + 2 * (i % 2), :].rearrange("p a b -> p (a b)"),
                                   ACT.Square).then_inc(s_sq, 1)
                if i < T + 1:
                    rows = P if i < T else WIN
                    act.wait_ge(s_v, i + 1)
                    act.activation(v[0:rows, i, :, 0:LD], ps[0:rows, VB, :].rearrange("p (h d) -> p h d", d=LD),
                                   ACT.Copy).then_inc(s_vc, 1)
                if i < T:
                    act.wait_ge(s_ss, i + 1)
                    act.activation(norm[:, i % 2, 0, :], norm[:, i % 2, 0, :], ACT.Sqrt).then_inc(s_root, 1)
                if i >= 3:
                    copy_qk(i - 3)
            act.wait_ge(s_tc, T)

        @block.gpsimd
        def _(pool):
            def plain_part(t):
                pool.wait_ge(s_hat, t + 1)
                if t >= 2:
                    pool.wait_ge(s_sum, t - 1)
                pool.tensor_tensor(heads(plain[:, t % 2, :]), heads(hat[:, t % 2, :]),
                                   straight[:, t].unsqueeze(2).to_broadcast([P, 2, LH, LD]), ALU.mult).then_inc(s_plain, 1)

            for t in range(T):
                plain_part(t)

        @block.vector
        def _(dve):
            def sums(t):
                dve.wait_ge(s_sq, t + 1)
                dve.tensor_reduce(norm[:, t % 2, 0, :], sq.rearrange("p (h d) -> p h d", d=LD), X_AXIS,
                                  ALU.add).then_inc(s_ss, 1)

            def normalise(t):
                dve.wait_ge(s_root, t + 1)
                dve.tensor_scalar(norm[:, t % 2, 0, :], norm[:, t % 2, 0, :], 1e-12, None, ALU.max).then_inc(s_clip, 1)
                dve.wait_ge(s_clip, t + 1)
                dve.reciprocal(norm[:, t % 2, 1, :], norm[:, t % 2, 0, :]).then_inc(s_inv, 1)
                dve.wait_ge(s_inv, t + 1)
                if t >= 2:
                    dve.wait_ge(s_t, t - 1)
                qk = ps[:, 4 + 2 * (t % 2):6 + 2 * (t % 2), :].rearrange("p i (h d) -> p (i h) d", d=LD)
                dve.tensor_tensor(hat[:, t % 2, :].rearrange("p (h d) -> p h d", d=LD), qk,
                                  norm[:, t % 2, 1, :].unsqueeze(2).to_broadcast([P, NH, LD]), ALU.mult).then_inc(s_hat, 1)

            def rotate(t):
                dve.wait_ge(s_hat, t + 1)
                for k in range(2):
                    a, b = k * LD // 2, (1 - k) * LD // 2
                    dve.tensor_tensor(heads(turned[:, t % 2, :])[:, :, :, b:b + LD // 2],
                                      heads(hat[:, t % 2, :])[:, :, :, a:a + LD // 2],
                                      exchanged[:, t, :, a:a + LD // 2].unsqueeze(2).to_broadcast([P, 2, LH, LD // 2]),
                                      ALU.mult).then_inc(s_turned, 1)
                dve.wait_ge(s_turned, 2 * t + 2)
                dve.wait_ge(s_plain, t + 1)
                dve.tensor_tensor(hat[:, t % 2, :], turned[:, t % 2, :], plain[:, t % 2, :], ALU.add).then_inc(s_sum, 1)

            for i in range(T + 2):
                if 0 <= i - 1 < T:
                    normalise(i - 1)
                if i < T:
                    sums(i)
                if 0 <= i - 2 < T:
                    rotate(i - 2)


def window_attention(nc, ctx, a, keep, w, layer):
    def sem(name):
        return ctx.enter_context(nc.semaphore(f"{name}_{layer}"))

    ps, ident, identb = keep["ps"], keep["ident"], keep["identb"]
    xs, xa, qkT, v, mask = w["xs"], w["xa"], w["qkT"], w["v"], w["mask"]
    HH = LH // 2
    work = w["work"]
    sub = work[:, 0:2 * HH * KEYS].rearrange("p (b h k) -> p b h k", b=2, h=HH)
    at = 2 * HH * KEYS
    pa = work[:, at:at + 2 * HH * P].rearrange("p (b h q) -> p b h q", b=2, h=HH)
    at += 2 * HH * P
    pb = work[0:WIN, at:at + 2 * HH * WIN].rearrange("p (b h q) -> p b h q", b=2, h=HH)
    at += 2 * HH * WIN
    o = work[:, at:at + 2 * INNER].rearrange("p (b f) -> p b f", b=2)
    at += 2 * INNER
    oT = work[:, at:at + INNER]
    at += INNER
    qpad = work[:, at:at + 4 * HH * P].rearrange("p (par b h q) -> p par b h q", par=2, b=2, h=HH)
    U = 2 * T
    s_pad0, s_pad = sem("w_pads_zeroed"), sem("w_padded")
    nmax = ctx.enter_context(nc.sbuf_tensor(f"nmax_{layer}", [P, 2, HH], F32))
    rden = ctx.enter_context(nc.sbuf_tensor(f"rden_l{layer}", [P, 2, HH], F32))
    PA, PB, OB, YB = 4, 5, 6, 7
    s_s, s_nm, s_sub, s_e, s_pa, s_pb, s_pac, s_pbc, s_av, s_rd, s_o, s_ot, s_otc, s_y, s_xa = (
        sem(n) for n in ("w_scores", "w_max", "w_less_max", "w_exp", "w_turned_a", "w_turned_b", "w_copied_a",
                         "w_copied_b", "w_values", "w_rden", "w_out", "w_out_turned", "w_out_copied", "w_projected",
                         "w_added"))

    s_tab, s_scaled = sem("w_tables_in"), sem("w_tables_scaled")

    with nc.Block() as block:
        if layer + 1 < LAYERS:
            @block.sync
            def _(sp):
                for i in range(2):
                    sp.dma_start(w["tab"][:, i, :, :, :], a["xpos"][i]).then_inc(s_tab, 16)

        @block.gpsimd
        def _(pool):
            for par in range(2):
                pool.memset(qpad[HALF * (1 - par):HALF * (2 - par), par, :, :, :], 0.0).then_inc(s_pad0, 1)
            for u in range(U):
                t, par = divmod(u, 2)
                if u >= 4:
                    pool.wait_ge(s_s, u - 3)
                if u >= 1:
                    pool.wait_ge(s_pad, u)
                else:
                    pool.wait_ge(s_pad0, 2)
                rows = slice(HALF * par, HALF * (par + 1))
                pool.tensor_copy(qpad[rows, par, t % 2, :, :],
                                 qkT[rows, 0, :, WIN + t * P:WIN + (t + 1) * P]).then_inc(s_pad, 1)
            if layer + 1 < LAYERS:
                pool.wait_ge(s_tab, 32)
                pool.wait_ge(s_pad, U)
                for i in range(2):
                    scale_table(pool, w, layer + 1, i).then_inc(s_scaled, 1)
                pool.wait_ge(s_scaled, 2)

        @block.tensor
        def _(pe):
            def scores(u):
                t, par = divmod(u, 2)
                if u >= 2:
                    pe.wait_ge(s_sub, u - 1)
                pe.wait_ge(s_pad, u + 1)
                for b in range(2):
                    bank = ps[:, 2 * (u % 2) + b, 0:2 * KEYS].rearrange("p (h k) -> p h k", h=2)
                    for j in range(2):
                        n = 2 * b + j
                        pe.matmul(bank[:, j, :], qpad[:, par, t % 2, n, :], qkT[:, 1, n, t * P:t * P + KEYS], start=j == 0, stop=False, skip_group_check=True)
                    m = mask[:, min(t, 1):min(t, 1) + 1, :].to_broadcast([P, 2, KEYS])
                    mm = pe.matmul(bank, identb[:, :], m, start=False, stop=True, skip_group_check=True)
                mm.then_inc(s_s, 1)

            def turn(u):
                pe.wait_ge(s_e, u + 1)
                if u >= 1:
                    pe.wait_ge(s_pac, u)
                    pe.wait_ge(s_pbc, u)
                for n in range(HH):
                    mm = pe.transpose(ps[:, PA, n * P:(n + 1) * P], sub[:, u % 2, n, 0:P], ident[:, :])
                mm.then_inc(s_pa, 1)
                for n in range(HH):
                    mm = pe.transpose(ps[0:WIN, PB, n * WIN:(n + 1) * WIN], sub[WIN:P, u % 2, n, P:KEYS],
                                      ident[WIN:P, WIN:P])
                mm.then_inc(s_pb, 1)

            def values(u):
                t, par = divmod(u, 2)
                pe.wait_ge(s_pac, u + 1)
                pe.wait_ge(s_pbc, u + 1)
                if u >= 1:
                    pe.wait_ge(s_o, u)
                for n in range(HH):
                    cols = slice(n * (LD + 1), (n + 1) * (LD + 1))
                    pe.matmul(ps[:, OB, cols], pa[:, u % 2, n, :], v[:, t, 2 * n + par, :],
                              start=True, stop=False, skip_group_check=True)
                    mm = pe.matmul(ps[WIN:P, OB, cols], pb[:, u % 2, n, :], v[0:WIN, t + 1, 2 * n + par, :],
                                   start=False, stop=True, skip_group_check=True)
                mm.then_inc(s_av, 1)

            def turn_out(t):
                pe.wait_ge(s_o, 2 * t + 2)
                if t >= 1:
                    pe.wait_ge(s_xa, t)
                for c in range(INNER // P):
                    mm = pe.transpose(ps[:, YB, c * P:(c + 1) * P], o[:, t % 2, c * P:(c + 1) * P], ident[:, :])
                mm.then_inc(s_ot, 1)

            def project(t):
                pe.wait_ge(s_otc, t + 1)
                for c in range(INNER // P):
                    mm = pe.matmul(ps[:, YB, 0:D], oT[:, c * P:(c + 1) * P], w["wo"][:, layer, c, :],
                                   start=c == 0, stop=c == INNER // P - 1)
                mm.then_inc(s_y, 1)

            for i in range(U + 5):
                if i < U:
                    scores(i)
                if 0 <= i - 1 < U:
                    turn(i - 1)
                if i >= 4 and i % 2 == 0 and i // 2 - 2 < T:
                    project(i // 2 - 2)
                if 0 <= i - 2 < U:
                    values(i - 2)
                if i >= 3 and i % 2 == 1 and (i - 3) // 2 < T:
                    turn_out((i - 3) // 2)

        @block.vector
        def _(dve):
            def less_max(u):
                dve.wait_ge(s_s, u + 1)
                got = ps[:, 2 * (u % 2):2 * (u % 2) + 2, 0:2 * KEYS].rearrange("p b (h k) -> p b h k", h=2)
                dve.tensor_reduce(nmax[:, u % 2, :].rearrange("p (b h) -> p b h", b=2), got, X_AXIS, ALU.max,
                                  negate=True).then_inc(s_nm, 1)
                dve.wait_ge(s_nm, u + 1)
                if u >= 2:
                    dve.wait_ge(s_pb, u - 1)
                dve.tensor_tensor(sub[:, u % 2].rearrange("p (b h) k -> p b h k", b=2), got,
                                  nmax[:, u % 2, :].rearrange("p (b h) -> p b h", b=2).unsqueeze(3)
                                  .to_broadcast([P, 2, 2, KEYS]), ALU.add).then_inc(s_sub, 1)

            def divide(u):
                t, par = divmod(u, 2)
                dve.wait_ge(s_av, u + 1)
                got = ps[:, OB, 0:HH * (LD + 1)].rearrange("p (h d) -> p h d", d=LD + 1)
                dve.reciprocal(rden[:, u % 2, :], got[:, :, LD]).then_inc(s_rd, 1)
                dve.wait_ge(s_rd, u + 1)
                if t >= 2:
                    dve.wait_ge(s_ot, t - 1)
                dve.tensor_tensor(o[:, t % 2, :].rearrange("p (h a d) -> p h a d", a=2, d=LD)[:, :, par, :],
                                  got[:, :, 0:LD], rden[:, u % 2, :].unsqueeze(2).to_broadcast([P, HH, LD]),
                                  ALU.mult).then_inc(s_o, 1)

            for i in range(U + 5):
                if i < U:
                    less_max(i)
                if i >= 4 and i % 2 == 0 and i // 2 - 2 < T:
                    t = i // 2 - 2
                    dve.wait_ge(s_y, t + 1)
                    dve.tensor_tensor(xa[:, t, :], xs[:, t, :], ps[:, YB, 0:D], ALU.add).then_inc(s_xa, 1)
                if 0 <= i - 2 < U:
                    divide(i - 2)

        @block.scalar
        def _(act):
            for i in range(U + 4):
                if i < U:
                    act.wait_ge(s_sub, i + 1)
                    act.activation(sub[:, i % 2, :, :], sub[:, i % 2, :, :], ACT.Exp, scale=8.0).then_inc(s_e, 1)
                if 0 <= i - 1 < U:
                    u = i - 1
                    act.wait_ge(s_pa, u + 1)
                    if u >= 2:
                        act.wait_ge(s_av, u - 1)
                    act.activation(pa[:, u % 2].rearrange("p h q -> p (h q)"), ps[:, PA, :], ACT.Copy).then_inc(s_pac, 1)
                    act.wait_ge(s_pb, u + 1)
                    act.activation(pb[:, u % 2].rearrange("p h q -> p (h q)"), ps[0:WIN, PB, 0:HH * WIN],
                                   ACT.Copy).then_inc(s_pbc, 1)
                if i >= 3 and i % 2 == 1 and (i - 3) // 2 < T:
                    t = (i - 3) // 2
                    act.wait_ge(s_ot, t + 1)
                    if t >= 1:
                        act.wait_ge(s_y, t)
                    act.activation(oT, ps[:, YB, :], ACT.Copy).then_inc(s_otc, 1)


def feed_forward(nc, ctx, keep, w, layer, out):
    def sem(name):
        return ctx.enter_context(nc.semaphore(f"{name}_{layer}"))

    ps, ident, half, x, rstd, mv = (keep[n] for n in ("ps", "ident", "half", "x", "rstd", "mv"))
    xs, xa, shift = w["xs"], w["xa"], w["shift"]
    stat = ctx.enter_context(nc.sbuf_tensor(f"stat_{layer}", [P, 2, 2, 6], F32))
    work = w["work"]
    hn = work[:, 0:TPB * D].rearrange("p (t c) -> p t c", t=TPB)
    hnT = work[:, 512:512 + 2 * BLK].rearrange("p (b s) -> p b s", b=2)
    gate = work[:, 1536:1536 + 2 * BLK].rearrange("p (b s) -> p b s", b=2)
    hid = work[:, 2560:2560 + 2 * 3 * BLK].rearrange("p (b c s) -> p b c s", b=2, c=3)
    SH, HB, YB = 4, 5, 6
    last = layer == LAYERS - 1
    C = len(HCH)
    s_sh, s_st, s_mv, s_eps, s_rs, s_hn, s_ht, s_htc, s_ag, s_gate, s_hid, s_y, s_x = (
        sem(n) for n in ("f_shifted", "f_stats", "f_mean_var", "f_eps", "f_rstd", "f_normed", "f_turned", "f_copied",
                         "f_hidden", "f_gate", "f_product", "f_out", "f_added"))
    s_store = sem("stored")

    with nc.Block() as block:
        @block.tensor
        def _(pe):
            def shift_tokens(t):
                if t >= 1:
                    pe.wait_ge(s_hn, 2 * t)
                pe.matmul(ps[:, SH, 0:D // 2], shift[:, 0, :], xa[:, t, D // 2:D], start=True, stop=t == 0)
                if t >= 1:
                    pe.matmul(ps[:, SH, 0:D // 2], shift[:, 1, :], xa[:, t - 1, D // 2:D], start=False, stop=True
                              ).then_inc(s_sh, 1)
                else:
                    pe.matmul(ps[:, SH, 0:D // 2], shift[:, 0, :], xa[:, t, D // 2:D], start=True, stop=True
                              ).then_inc(s_sh, 1)

            def turn(t):
                pe.wait_ge(s_hn, 2 * t + 2)
                b = t // TPB
                if t % TPB == 0 and b >= 1:
                    pe.wait_ge(s_htc, b)
                mm = pe.transpose(ps[:, HB, t % TPB * P:(t % TPB + 1) * P], hn[:, t % TPB, :], ident[:, :])
                if t % TPB == TPB - 1:
                    mm.then_inc(s_ht, 1)

            def hidden(b, c):
                n = C * b + c
                rows = HCH[c]
                pe.wait_ge(s_htc, b + 1)
                if n >= 2:
                    pe.wait_ge(s_hid, n - 1)
                for i in range(2):
                    at = i * HID + c * P
                    mm = pe.matmul(ps[0:rows, 2 * (n % 2) + i, :], w["w1"][:, layer, at:at + rows], hnT[:, b % 2, :],
                                   start=True, stop=True)
                mm.then_inc(s_ag, 1)

            def down(t):
                b = t // TPB
                pe.wait_ge(s_hid, C * (b + 1))
                if t >= 2:
                    pe.wait_ge(s_x, t - 1)
                dst = ps[:, YB + t % 2, 0:D]
                pe.matmul(dst, w["onesr"][:, :], w["b2"][:, layer, :], start=True, stop=False)
                for c, rows in enumerate(HCH):
                    mm = pe.matmul(dst, hid[0:rows, b % 2, c, t % TPB * P:(t % TPB + 1) * P],
                                   w["w2"][0:rows, layer, c, :], start=False, stop=c == C - 1)
                mm.then_inc(s_y, 1)

            for i in range(T + 6 + 2):
                if i < T:
                    shift_tokens(i)
                if 0 <= i - 1 < T:
                    turn(i - 1)
                j = i - 5
                if j >= 0 and j % TPB < C and j // TPB < NB:
                    hidden(j // TPB, j % TPB)
                if j >= 3 and (j - 3) % TPB == 0 and (j - 3) // TPB < NB:
                    for t in range(TPB):
                        down((j - 3) + t)

        @block.vector
        def _(dve):
            def stats(t):
                dve.bn_stats(stat[:, t % 2, 0, :], xa[:, t, 0:D // 2]).then_inc(s_st, 1)
                dve.wait_ge(s_sh, t + 1)
                dve.bn_stats(stat[:, t % 2, 1, :], ps[:, SH, 0:D // 2]).then_inc(s_st, 1)
                dve.wait_ge(s_st, 2 * t + 2)
                dve.bn_aggr(mv[:, t, :], stat[:, t % 2, :, :].rearrange("p a b -> p (a b)")).then_inc(s_mv, 1)
                dve.wait_ge(s_rs, t + 1)
                if t >= TPB and t % TPB == 0:
                    dve.wait_ge(s_ht, t // TPB)
                dve.tensor_scalar(hn[:, t % TPB, 0:D // 2], xa[:, t, 0:D // 2], mv[:, t, 0:1], rstd[:, t:t + 1],
                                  ALU.subtract, ALU.mult).then_inc(s_hn, 1)
                dve.tensor_scalar(hn[:, t % TPB, D // 2:D], ps[:, SH, 0:D // 2], mv[:, t, 0:1], rstd[:, t:t + 1],
                                  ALU.subtract, ALU.mult).then_inc(s_hn, 1)

            def product(b, c):
                n = C * b + c
                rows = HCH[c]
                dve.wait_ge(s_gate, n + 1)
                if b >= 2:
                    dve.wait_ge(s_y, TPB * (b - 1))
                dve.scalar_tensor_tensor(out=hid[0:rows, b % 2, c, :], in0=ps[0:rows, 2 * (n % 2), :],
                                         scalar=w["b1"][0:rows, layer, 0, c:c + 1], in1=gate[0:rows, n % 2, :],
                                         op0=ALU.add, op1=ALU.mult).then_inc(s_hid, 1)

            def add(t):
                dve.wait_ge(s_y, t + 1)
                dve.tensor_tensor(xs[:, t, :], xa[:, t, :], ps[:, YB + t % 2, 0:D], ALU.add).then_inc(s_x, 1)

            for i in range(T + 6 + 2):
                if i < T:
                    stats(i)
                j = i - 5
                if j >= 0 and j % TPB < C and j // TPB < NB:
                    product(j // TPB, j % TPB)
                if j >= 3 and (j - 3) % TPB == 0 and (j - 3) // TPB < NB:
                    for t in range(TPB):
                        add((j - 3) + t)
            dve.wait_ge(s_x, T)

        @block.gpsimd
        def _(pool):
            for t in range(T):
                pool.wait_ge(s_mv, t + 1)
                pool.tensor_scalar(mv[:, t, 1:2], mv[:, t, 1:2], 1e-5, None, ALU.add).then_inc(s_eps, 1)
                pool.wait_ge(s_eps, t + 1)
                pool.tensor_tensor(rstd[:, t:t + 1], mv[:, t, 1:2], half[:, 0:1], ALU.pow).then_inc(s_rs, 1)
            if last:
                for t in range(T):
                    pool.wait_ge(s_x, t + 1)
                    pool.tensor_tensor(x[:, t, :], x[:, t, :], xs[:, t, :], ALU.add).then_inc(s_eps, 1)

        @block.scalar
        def _(act):
            for b in range(NB):
                act.wait_ge(s_ht, b + 1)
                if b >= 2:
                    act.wait_ge(s_ag, C * (b - 1))
                act.activation(hnT[:, b % 2, :], ps[:, HB, :], ACT.Identity, bias=w["gb"][:, layer, 1:2],
                               scale=w["gb"][:, layer, 0:1]).then_inc(s_htc, 1)
                for c, rows in enumerate(HCH):
                    n = C * b + c
                    act.wait_ge(s_ag, n + 1)
                    if n >= 2:
                        act.wait_ge(s_hid, n - 1)
                    act.activation(gate[0:rows, n % 2, :], ps[0:rows, 2 * (n % 2) + 1, :], ACT.Gelu,
                                   bias=w["b1"][0:rows, layer, 1, c:c + 1]).then_inc(s_gate, 1)

        if last:
            @block.sync
            def _(sp):
                for b in range(NB):
                    sp.wait_ge(s_eps, T + TPB * (b + 1))
                    sp.dma_start(out[b * BLK:(b + 1) * BLK, :].rearrange("(t p) c -> p t c", p=P),
                                 x[:, TPB * b:TPB * (b + 1), :]).then_inc(s_store, 16)
                sp.wait_ge(s_store, 16 * NB)


def shape_constants():
    f32, bf16 = np.float32, mybir.dt.np(BF16)
    c = {}
    c["ident"] = np.eye(P, dtype=f32)
    c["identb"] = np.eye(P, dtype=bf16)
    ahead = np.where(np.arange(P)[None, :] > np.arange(P)[:, None], NEG, 0.0)
    c["mask_q"] = ahead.astype(bf16)
    c["mask_k"] = np.ascontiguousarray(ahead.T).astype(bf16)
    c["ones"] = np.ones((2, PAIRS * S), bf16)
    pick = np.zeros((P, 4 * 9), f32)
    for j in range(4):
        for d in range(9):
            pick[VW * j + d, 9 * j + d] = 1.0
    c["pick"] = pick
    inv = (1.0 / np.power(10000.0, np.arange(0, DH, 2, dtype=f32).astype(np.float64) / DH).astype(f32)).astype(f32)
    ang = np.outer(np.arange(S, dtype=f32), inv).astype(f32).astype(np.float64)
    ang = np.concatenate([ang, ang], axis=1)
    sign = np.where(np.arange(DH) < DH // 2, -1.0, 1.0)
    rows = np.arange(P) // PAIRS % DH
    c["rope"] = np.stack([np.cos(ang)[:, rows].T, (np.sin(ang) * sign)[:, rows].T]).astype(f32)
    inv = (1.0 / np.power(10000.0, np.arange(0, LD, 2, dtype=f32).astype(np.float64) / LD).astype(f32)).astype(f32)
    tok = np.arange(S, dtype=f32)
    ang = (tok[:, None] * inv[None, :]).astype(f32).astype(np.float64)
    base = (np.arange(0, LD, 2) + 0.4 * LD) / (1.4 * LD)
    power = (tok.astype(np.float64) - S // 2) / (WIN // 2)
    grow = base.astype(f32).astype(np.float64)[None, :] ** power[:, None]
    both = [np.concatenate([m, m], axis=1) for m in (np.cos(ang), np.sin(ang), grow)]
    sign = np.where(np.arange(LD) < LD // 2, 1.0, -1.0)
    tabs = []
    for m in (both[0], both[1] * sign):
        qk = np.stack([m * both[2], m / both[2]], axis=1)
        tabs.append(qk.reshape(T, P, 2, LD).transpose(1, 0, 2, 3))
    c["xpos"] = np.ascontiguousarray(np.stack(tabs)).astype(f32)
    i, j = np.arange(P)[:, None], np.arange(KEYS)[None, :] - WIN
    hidden = (j > i) | (j < i - WIN)
    c["mask_l"] = np.where(np.stack([hidden | (j < 0), hidden], axis=1), NEG, 0.0).astype(bf16)
    c["shift"] = np.ascontiguousarray(np.stack([np.eye(P, k=1), np.eye(P, k=1 - P)], axis=1)).astype(f32)
    c["ones_row"] = np.ones((1, P), f32)
    return c


def kernel(L0_attn_x, L0_attn_Wq, L0_attn_Wk, L0_attn_Wv, L0_attn_Wo, L0_ffn_wqkv, L0_ffn_q_scale, L0_ffn_k_scale,
           L0_ffn_wo, L0_ffn_ln_g, L0_ffn_ln_b, L0_ffn_w1, L0_ffn_b1, L0_ffn_w2, L0_ffn_b2):
    import concourse.bacc as _bacc
    from concourse.bass_utils import run_bass_kernel_spmd as _run

    arrays = shape_constants()
    order = np.array([(2 * pair + par) * DH + d for par in range(2) for d in range(DH) for pair in range(PAIRS)])
    turned = order // DH * DH + (order % DH + DH // 2) % DH
    wq, wk = np.asarray(L0_attn_Wq), np.asarray(L0_attn_Wk)
    arrays["wqk"] = np.ascontiguousarray(np.stack([wq[order].T, wq[turned].T, wk[order].T, wk[turned].T]))
    arrays["wv"] = np.ascontiguousarray(np.asarray(L0_attn_Wv).T)
    arrays["wo"] = np.ascontiguousarray(np.asarray(L0_attn_Wo).T)
    for name, value in (("wqkv", L0_ffn_wqkv), ("q_scale", L0_ffn_q_scale), ("k_scale", L0_ffn_k_scale),
                        ("lwo", L0_ffn_wo), ("w1", L0_ffn_w1), ("w2", L0_ffn_w2), ("b2", L0_ffn_b2)):
        arrays[name] = np.ascontiguousarray(np.asarray(value))
    arrays["ln_gb"] = np.ascontiguousarray(np.stack([np.asarray(L0_ffn_ln_g), np.asarray(L0_ffn_ln_b)], 2).transpose(1, 0, 2))
    b1 = np.zeros((P, LAYERS, 2, len(HCH)), np.float32)
    for c, rows in enumerate(HCH):
        for i in range(2):
            b1[:rows, :, i, c] = np.asarray(L0_ffn_b1)[:, i * HID + c * P:i * HID + c * P + rows].T
    arrays["b1"] = b1
    arrays["x"] = np.ascontiguousarray(np.asarray(L0_attn_x).reshape(S, D))

    nc = _bacc.Bacc("TRN2", target_bir_lowering=False, num_devices=1)
    arrays = {"in_" + n: v for n, v in arrays.items()}
    aps = {n[3:]: nc.dram_tensor(n, v.shape, mybir.dt.from_np(v.dtype), kind="ExternalInput").ap()
           for n, v in arrays.items()}
    out = nc.dram_tensor("out", (S, D), F32, kind="ExternalOutput").ap()
    build(nc, aps, out)
    r = _run(nc, [arrays], core_ids=[0])
    return r.results[0]["out"].reshape(1, S, D)
```

```python
from contextlib import ExitStack

import numpy as np

import concourse.bass as bass
from concourse import mybir

F32 = mybir.dt.float32
BF16 = mybir.dt.bfloat16
ALU = mybir.AluOpType
ACT = mybir.ActivationFunctionType
X_AXIS = mybir.AxisListType.X

P = 128
S = 2048
D = 128
T = S // P
BLK = 512
NB = S // BLK
TPB = BLK // P
H = 16
DH = D // H
PAIRS = H // 2
GROUPS = H // 4
HALF = 64
SPLIT = 6 * DH
SROWS = SPLIT + 2
VW = 32
NEG = -1e30
CHUNKS = [(q, g) for q in (1, 2, 3, 0) for g in range(GROUPS)]
NC = len(CHUNKS)

LH = 8
LD = 64
WIN = 64
INNER = LH * LD
HID = 341
HCH = (128, 128, 85)
LAYERS = 2
KEYS = WIN + P


def max_units(q, g):
    return [(t, pair, c, par) for t in range(TPB * q, TPB * (q + 1)) for pair in (2 * g, 2 * g + 1)
            for c in range(t // TPB + 1) for par in range(2)]


def share(units, i, n):
    return units[len(units) * i // n:len(units) * (i + 1) // n]


def build(nc, a, out):
    with ExitStack() as ctx:
        def sb(name, shape, dt=F32):
            return ctx.enter_context(nc.sbuf_tensor(name, shape, dt))

        keep = {
            "ps": ctx.enter_context(nc.psum_tensor("ps", [P, 8, BLK], F32)),
            "x": sb("x_rows", [P, T, D]),
            "ident": sb("ident", [P, P]),
            "identb": sb("identb", [P, P], BF16),
            "half": sb("minus_half", [P, 16]),
            "mv": sb("mean_var", [P, T, 2]),
            "rstd": sb("rstd", [P, T]),
            "stat": sb("stat", [P, T, 6]),
        }
        with ExitStack() as attn:
            first_attention(nc, attn, a, keep)
        with ExitStack() as ffn:
            layers(nc, ffn, a, keep, out)


def first_attention(nc, ctx, a, keep):
    def sb(name, shape, dt=F32):
        return ctx.enter_context(nc.sbuf_tensor(name, shape, dt))

    def sem(name):
        return ctx.enter_context(nc.semaphore(name))

    ps, x, ident, identb = keep["ps"], keep["x"], keep["ident"], keep["identb"]
    half, mv, rstd, stat = keep["half"], keep["mv"], keep["rstd"], keep["stat"]

    early = sb("early", [P, 4, S])
    xn = early[:, 0, :].rearrange("p (t c) -> p t c", t=T)
    xT = early[:, 1, :]
    rope = early[:, 2:4, :]
    outT = early
    wqk = sb("wqk", [P, 4, D])
    wv = sb("wv", [P, D])
    wo = sb("wo_t", [P, D])
    mask_q = sb("mask_q", [P, P], BF16)
    mask_k = sb("mask_k", [P, P], BF16)
    pick = sb("pick", [P, 4 * 9])
    probs = sb("probs", [P, 2, 2, 2, BLK])
    prod = probs[:, 0, :, :, :]
    full = probs[:, 1, 0, :, :]
    rest = probs[:, 1, 1, :, :]
    part = sb("split_part", [P, 2, 2, 3, BLK], BF16)
    qs = sb("q_stack", [P, NB // 2, PAIRS, 2, BLK], BF16)
    ks = sb("k_stack", [P, 2, NB // 2, PAIRS, 2, BLK], BF16)
    v = sb("v_rows", [P, T, H, VW])
    mpart = sb("max_part", [P, TPB, 4, NB])
    mneg = sb("max_neg", [P, 2, TPB, 4])
    mrow = sb("max_rows", [4, 2, BLK], BF16)
    rden = sb("rden", [P, 2, H])
    on = sb("o_norm", [P, 2, D])
    onT = sb("o_norm_t", [P, BLK])

    s_x, s_w, s_rope, s_const = sem("x_loaded"), sem("weights_loaded"), sem("rope_loaded"), sem("const_loaded")
    nil = sb("zero", [P, 1])
    s_half, s_vset, s_nil = sem("half_set"), sem("v_ones_set"), sem("zero_set")
    s_dve, s_dstat = sem("dve_chain"), sem("stats_done")
    s_pool, s_rstd = sem("pool_chain"), sem("rstd_done")
    s_xn, s_xt, s_xtc = sem("xn_done"), sem("xt_turned"), sem("xt_copied")
    s_proj, s_v, s_vc = sem("projected"), sem("v_projected"), sem("v_copied")
    s_prod, s_full, s_high, s_rest, s_mid, s_low = (sem(n) for n in (
        "rope_products", "rope_sum", "high_part", "rest_left", "middle_part", "low_part"))
    s_stack = [sem(f"stacked{h}") for h in range(NB // 2)]
    s_ones, s_zero = sem("ones_rows"), sem("stacks_zeroed")
    s_spread = [sem(f"spread{b}") for b in range(NB)]
    spread = nc.dram_tensor("spread", (NB // 2, 2, 3, 2 * DH, PAIRS, 2, BLK), BF16, kind="Internal").ap()

    def send_to_stacks(sp, h):
        both = range(2 * h, 2 * h + 2)
        for b in both:
            sp.wait_ge(s_low, 2 * b + 2)
            sp.dma_start(spread[h, :, :, :, :, b % 2, :].rearrange("i w r n s -> (r n) (i w) s"),
                         part[:, b % 2, :, :, :].rearrange("p i w s -> p (i w) s")).then_inc(s_spread[b], 16)
        for b in both:
            sp.wait_ge(s_spread[b], 16)
        for par in range(2):
            row = HALF * par
            d = slice(DH * par, DH * (par + 1))
            for w, times in ((0, 3), (1, 2), (2, 1)):
                sp.dma_start(qs[row:row + DH * times, h, :, :, :].rearrange("r n b s -> r (n b s)"),
                             spread[h, 0, w:w + 1, d].rearrange("w d n b s -> w d (n b s)")
                             .to_broadcast([times, DH, PAIRS * 2 * BLK])).then_inc(s_stack[h], 16)
                sp.dma_start(ks[row:row + DH * times, par, h, :, :, :].rearrange("r n b s -> r (n b s)"),
                             spread[h, 1, 0:times, d].rearrange("w d n b s -> w d (n b s)")
                             ).then_inc(s_stack[h], 16)
                row += DH * times

    with nc.Block() as block:
        @block.sync
        def _(sp):
            sp.dma_start(x[:, :, :], a["x"].rearrange("(t p) c -> p t c", p=P)).then_inc(s_x, 16)
            sp.dma_start(ident[:, :], a["ident"]).then_inc(s_const, 16)
            sp.dma_start(wqk[:, :, :], a["wqk"].rearrange("n c f -> c n f")).then_inc(s_w, 16)
            sp.dma_start(wv[:, :], a["wv"]).then_inc(s_w, 16)
            sp.dma_start(wo[:, :], a["wo"]).then_inc(s_w, 16)
            sp.dma_start(rope[:, :, :], a["rope"].rearrange("n r s -> r n s")).then_inc(s_rope, 16)
            for dst, name in ((identb, "identb"), (mask_q, "mask_q"), (mask_k, "mask_k"), (pick, "pick")):
                sp.dma_start(dst[:, :], a[name]).then_inc(s_const, 16)
            for par in range(2):
                at = HALF * par + SPLIT
                if par == 0:
                    sp.wait_ge(s_zero, 3)
                sp.dma_start(ks[at:at + 2, par, :, :, :, :].rearrange("r h n b s -> r (h n b s)"), a["ones"]).then_inc(s_ones, 16)
            send_to_stacks(sp, 0)
            sp.wait_ge(s_ones, 32)

        @block.gpsimd
        def _(pool):
            pool.memset(nil[:, :], 0.0).then_inc(s_nil, 1)
            pool.memset(half[:, :], -0.5).then_inc(s_half, 1)
            pool.memset(v[:, :, :, :], 0.0).then_inc(s_vset, 1)
            pool.wait_ge(s_vset, 1)
            pool.memset(v[:, :, :, DH:DH + 1], 1.0).then_inc(s_vset, 1)
            pool.wait_ge(s_half, 1)
            pool.wait_ge(s_dstat, T)
            pool.tensor_scalar(rstd[:, :], mv[:, :, 1], 1e-5, None, ALU.add).then_inc(s_pool, 1)
            pool.wait_ge(s_pool, 1)
            pool.tensor_tensor(rstd[:, :], rstd[:, :], half[:, :], ALU.pow).then_inc(s_rstd, 1)
            pool.memset(ks[:, 1, :, :, :, :].rearrange("p h n b s -> p (h n b s)").bitcast(F32), 0.0).then_inc(s_zero, 1)
            for n in range(2 * NB):
                pool.wait_ge(s_prod, 2 * n + 2)
                if n >= 2:
                    pool.wait_ge(s_rest, n - 1)
                pool.tensor_tensor(full[:, n % 2, :], prod[:, n % 2, 0, :], prod[:, n % 2, 1, :],
                                   ALU.add).then_inc(s_full, 1)

        @block.vector
        def _(dve):
            dve.wait_ge(s_x, 16)
            for t in range(T):
                dve.bn_stats(stat[:, t, :], x[:, t, :]).then_inc(s_dve, 1)
            for t in range(T):
                dve.wait_ge(s_dve, t + 1)
                dve.bn_aggr(mv[:, t, :], stat[:, t, :]).then_inc(s_dstat, 1)
            dve.memset(ks[:, 0, :, :, :, :].rearrange("p h n b s -> p (h n b s)").bitcast(F32), 0.0).then_inc(s_zero, 1)
            dve.wait_ge(s_rstd, 1)
            for t in range(T):
                dve.tensor_scalar(xn[:, t, :], x[:, t, :], mv[:, t, 0:1], rstd[:, t:t + 1],
                                  ALU.subtract, ALU.mult).then_inc(s_xn, 1)
            dve.wait_ge(s_rope, 16)

            def products(n):
                b, i = divmod(n, 2)
                dve.wait_ge(s_proj, 2 * n + 2)
                if n >= 2:
                    dve.wait_ge(s_full, n - 1)
                for k in range(2):
                    dve.tensor_tensor(prod[:, i, k, :], ps[:, 2 + 2 * i + k, :], rope[:, k, b * BLK:(b + 1) * BLK],
                                      ALU.mult).then_inc(s_prod, 1)

            def lower(n):
                b, i = divmod(n, 2)
                dve.wait_ge(s_high, n + 1)
                if n >= 2:
                    dve.wait_ge(s_low, n - 1)
                dve.tensor_tensor(rest[:, i, :], full[:, i, :], part[:, b % 2, i, 0, :],
                                  ALU.subtract).then_inc(s_rest, 1)
                dve.wait_ge(s_rest, n + 1)
                dve.wait_ge(s_mid, n + 1)
                dve.tensor_tensor(part[:, b % 2, i, 2, :], rest[:, i, :], part[:, b % 2, i, 1, :],
                                  ALU.subtract).then_inc(s_low, 1)

            for n in range(2 * NB + 1):
                if n < 2 * NB:
                    products(n)
                if n >= 1:
                    lower(n - 1)

        @block.scalar
        def _(act):
            def copy_turned(b):
                act.wait_ge(s_xt, TPB * (b + 1))
                act.activation(xT[:, b * BLK:(b + 1) * BLK], ps[:, b % 2, :], ACT.Copy).then_inc(s_xtc, 1)

            act.wait_ge(s_nil, 1)
            flat = qs[:, :, :, :, :].rearrange("p h n b s -> p (h n b s)").bitcast(F32)
            act.activation(flat, nil[:, :].to_broadcast([P, NB * PAIRS * BLK // 2]), ACT.Copy).then_inc(s_zero, 1)
            copy_turned(0)
            for b in range(NB):
                if b + 1 < NB:
                    copy_turned(b + 1)
                act.wait_ge(s_v, b + 1)
                act.wait_ge(s_vset, 2)
                act.activation(v[:, TPB * b:TPB * (b + 1), :, 0:DH],
                               ps[:, 6, :].rearrange("p (t h d) -> p t h d", t=TPB, h=H), ACT.Copy).then_inc(s_vc, 1)
                for i in range(2):
                    n = 2 * b + i
                    act.wait_ge(s_full, n + 1)
                    if b >= 2:
                        act.wait_ge(s_spread[b - 2], 16)
                    act.activation(part[:, b % 2, i, 0, :], full[:, i, :], ACT.Copy).then_inc(s_high, 1)
                    act.wait_ge(s_rest, n + 1)
                    act.activation(part[:, b % 2, i, 1, :], rest[:, i, :], ACT.Copy).then_inc(s_mid, 1)

        @block.tensor
        def _(pe):
            pe.wait_ge(s_const, 16 * 5)
            pe.wait_ge(s_w, 48)

            def turn(b):
                if b >= 2:
                    pe.wait_ge(s_xtc, b - 1)
                for j in range(TPB):
                    t = TPB * b + j
                    pe.wait_ge(s_xn, t + 1)
                    pe.transpose(ps[:, b % 2, j * P:(j + 1) * P], xn[:, t, :], ident[:, :]).then_inc(s_xt, 1)

            def project(b):
                pe.wait_ge(s_xtc, b + 1)
                if b >= 1:
                    pe.wait_ge(s_vc, b)
                for j in range(TPB):
                    t = TPB * b + j
                    mm = pe.matmul(ps[:, 6, j * P:(j + 1) * P], xT[:, t * P:(t + 1) * P], wv[:, :],
                                   start=True, stop=True)
                mm.then_inc(s_v, 1)
                for i in range(2):
                    if b >= 1:
                        pe.wait_ge(s_prod, 4 * (b - 1) + 2 * i + 2)
                    for k in range(2):
                        pe.matmul(ps[:, 2 + 2 * i + k, :], wqk[:, 2 * i + k, :], xT[:, b * BLK:(b + 1) * BLK],
                                  start=True, stop=True).then_inc(s_proj, 1)

            turn(0)
            for b in range(NB):
                if b + 1 < NB:
                    turn(b + 1)
                project(b)

    OB, SM, RING = 4, 5, 3
    scale = float(DH) ** -0.5
    s_sm, s_smr = sem("max_scores"), sem("max_taken")
    s_mneg, s_mh = sem("row_max"), sem("max_high")
    s_mrow = [sem(f"max_rows_in{i}") for i in range(2)]
    s_st, s_e, s_av, s_oc = sem("scores"), sem("exps"), sem("values"), sem("out_copied")

    units, step_at = [], []
    for q, g in CHUNKS:
        units.append(max_units(q, g))
        step_at.append(step_at[-1] + TPB * (CHUNKS[len(step_at) - 1][0] + 1) if step_at else 0)

    def n_steps(k):
        return TPB * (CHUNKS[k][0] + 1) if k >= 0 else 1

    def beside(k, i, third):
        mine = range(len(units[k + 2])) if k + 2 < NC and i < n_steps(k) else []
        return share(mine, 3 * i + third, 3 * n_steps(k))

    slot, turn_slot = {}, {}
    for k in range(-2, NC):
        for i in range(n_steps(k) + 1):
            for third in range(3):
                for n in beside(k, i, third):
                    slot[k + 2, n] = len(slot) + len(turn_slot)
            if i == 0 and 0 <= k + 1 < NC:
                turn_slot[k + 1] = len(slot) + len(turn_slot)

    with nc.Block() as block:
        @block.tensor
        def _(pe):
            def max_scores(k, n):
                t, pair, c, par = units[k][n]
                n = slot[k, n]
                width = min(BLK, P * (t + 1) - BLK * c)
                if n >= RING:
                    pe.wait_ge(s_smr, n - RING + 1)
                last = c == t // TPB
                dst = ps[:, SM + n % RING, :]
                mm = pe.matmul(dst[:, 0:width], qs[:, t // TPB // 2, pair, t // TPB % 2, t % TPB * P:(t % TPB + 1) * P],
                               ks[:, par, c // 2, pair, c % 2, 0:width], start=True, stop=not last)
                if last:
                    mm = pe.matmul(dst[:, width - P:width], identb[:, :], mask_q[:, :], start=False, stop=True)
                mm.then_inc(s_sm, 1)

            def scores(k, kt, pr):
                q, g = CHUNKS[k]
                n = 2 * (step_at[k] + kt) + pr
                off = max(0, kt - TPB * q) * P
                pair = 2 * g + pr
                if n >= 2:
                    pe.wait_ge(s_e, n - 1)
                diag = kt >= TPB * q
                for par in range(2):
                    dst = ps[:, 2 * (n % 2) + par, 0:BLK - off]
                    mm = pe.matmul(dst, ks[:, par, kt // TPB // 2, pair, kt // TPB % 2, kt % TPB * P:(kt % TPB + 1) * P],
                                   qs[:, q // 2, pair, q % 2, off:BLK], start=True, stop=not diag)
                if diag:
                    for par in range(2):
                        mm = pe.matmul(ps[:, 2 * (n % 2) + par, 0:P], identb[:, :], mask_k[:, :],
                                       start=False, stop=True)
                mm.then_inc(s_st, 1)

            def values(k, kt):
                q, g = CHUNKS[k]
                n = step_at[k] + kt
                off = max(0, kt - TPB * q) * P
                pe.wait_ge(s_e, 2 * n + 2)
                if kt == 0 and k >= 1:
                    pe.wait_ge(s_oc, k)
                for j in range(4):
                    mm = pe.matmul(ps[VW * j:VW * (j + 1), OB, off:BLK], v[:, kt, 4 * g + j, :],
                                   probs[:, n % 2, j // 2, j % 2, 0:BLK - off],
                                   start=kt == 0, stop=kt == TPB * (q + 1) - 1)
                mm.then_inc(s_av, 1)

            def turn_max(k):
                n = turn_slot[k]
                pe.wait_ge(s_mneg, TPB * (k + 1))
                if n >= RING:
                    pe.wait_ge(s_smr, n - RING + 1)
                for j in range(TPB):
                    mm = pe.transpose(ps[0:4, SM + n % RING, j * P:(j + 1) * P], mneg[:, k % 2, j, :], ident[:, :])
                mm.then_inc(s_sm, 1)

            pe.wait_ge(s_stack[0], 16 * 12)
            for k in range(-2, NC):
                if k == 2:
                    pe.wait_ge(s_stack[1], 16 * 12)
                if k >= 0:
                    pe.wait_ge(s_mrow[k % 2], 64 * (k // 2 + 1))
                for i in range(n_steps(k) + 1):
                    for third in range(3):
                        if k >= 0 and third < 2 and i < n_steps(k):
                            scores(k, i, third)
                        if k >= 0 and third == 2 and i >= 1:
                            values(k, i - 1)
                        for n in beside(k, i, third):
                            max_scores(k + 2, n)
                    if i == 0 and 0 <= k + 1 < NC:
                        turn_max(k + 1)

        @block.scalar
        def _(act):
            for k, (q, g) in enumerate(CHUNKS):
                for kt in range(n_steps(k)):
                    off = max(0, kt - TPB * q) * P
                    for pr in range(2):
                        n = 2 * (step_at[k] + kt) + pr
                        act.wait_ge(s_st, n + 1)
                        if n >= 4:
                            act.wait_ge(s_av, n // 2 - 1)
                        act.activation(probs[:, n // 2 % 2, pr, :, 0:BLK - off],
                                       ps[:, 2 * (n % 2):2 * (n % 2) + 2, 0:BLK - off], ACT.Exp,
                                       scale=scale).then_inc(s_e, 1)

        @block.vector
        def _(dve):
            def take_max(k, n):
                t, pair, c, par = units[k][n]
                width = min(BLK, P * (t + 1) - BLK * c)
                dve.wait_ge(s_sm, slot[k, n] + 1)
                at = 2 * par + pair % 2
                dve.tensor_reduce(mpart[:, t % TPB, at, c:c + 1], ps[:, SM + slot[k, n] % RING, 0:width], X_AXIS,
                                  ALU.max).then_inc(s_smr, 1)
                if n + 1 == len(units[k]) or units[k][n + 1][0] != t:
                    dve.wait_ge(s_smr, slot[k, n] + 1)
                    if k >= 2:
                        dve.wait_ge(s_sm, turn_slot[k - 2] + 1)
                    dve.tensor_reduce(mneg[:, k % 2, t % TPB, :], mpart[:, t % TPB, :, 0:t // TPB + 1], X_AXIS,
                                      ALU.max, negate=True).then_inc(s_mneg, 1)

            def copy_out(k):
                q, g = CHUNKS[k]
                dve.wait_ge(s_av, step_at[k] + n_steps(k))
                dve.tensor_copy(outT[:, g, q * BLK:(q + 1) * BLK], ps[:, OB, :]).then_inc(s_oc, 1)

            def split_max(k):
                n = turn_slot[k]
                dve.wait_ge(s_sm, n + 1)
                turned = ps[0:4, SM + n % RING, :]
                if k >= 1:
                    dve.wait_ge(s_mrow[(k - 1) % 2], 64 * ((k - 1) // 2 + 1))
                dve.tensor_copy(mrow[:, 0, :], turned).then_inc(s_mh, 1)
                dve.wait_ge(s_mh, k + 1)
                dve.tensor_tensor(mrow[:, 1, :], turned, mrow[:, 0, :], ALU.subtract).then_inc(s_smr, 1)

            for k in range(-2, NC):
                for i in range(n_steps(k) + 1):
                    for third in range(3):
                        for n in beside(k, i, third):
                            take_max(k + 2, n)
                    if i == 0 and 0 <= k + 1 < NC:
                        split_max(k + 1)
                if k >= 0:
                    copy_out(k)

        @block.sync
        def _(sp):
            send_to_stacks(sp, 1)
            for k, (q, g) in enumerate(CHUNKS):
                sp.wait_ge(s_smr, turn_slot[k] + 1)
                for w in range(2):
                    for par in range(2):
                        at = HALF * par + SPLIT + w
                        sp.dma_start(qs[at:at + 1, q // 2, 2 * g:2 * g + 2, q % 2, :],
                                     mrow[2 * par:2 * par + 2, w, :]).then_inc(s_mrow[k % 2], 16)
            for k in (NC - 2, NC - 1):
                sp.wait_ge(s_mrow[k % 2], 64 * (k // 2 + 1))

    s_pick, s_rd, s_on, s_ont, s_ontc, s_y, s_yadd = (sem(n) for n in (
        "picked", "rden_done", "o_normed", "o_turned", "o_turned_copied", "o_projected", "o_added"))
    with nc.Block() as block:
        @block.tensor
        def _(pe):
            def gather(t):
                if t >= 2:
                    pe.wait_ge(s_on, t - 1)
                for g in range(GROUPS):
                    mm = pe.matmul(ps[:, t % 2, 36 * g:36 * (g + 1)], outT[:, g, t * P:(t + 1) * P], pick[:, :],
                                   start=True, stop=True)
                mm.then_inc(s_pick, 1)

            def turn(t):
                pe.wait_ge(s_on, t + 1)
                if t >= 2:
                    pe.wait_ge(s_ontc, t - 1)
                pe.transpose(ps[:, 2 + t % 2, 0:P], on[:, t % 2, :], ident[:, :]).then_inc(s_ont, 1)

            def project(t):
                pe.wait_ge(s_ontc, t + 1)
                if t >= 2:
                    pe.wait_ge(s_yadd, t - 1)
                pe.matmul(ps[:, 4 + t % 2, 0:D], onT[:, (t % 2) * P:(t % 2) * P + P], wo[:, :],
                          start=True, stop=True).then_inc(s_y, 1)

            for i in range(T + 2):
                if i < T:
                    gather(i)
                if 0 <= i - 1 < T:
                    turn(i - 1)
                if 0 <= i - 2 < T:
                    project(i - 2)

        @block.vector
        def _(dve):
            def norm(t):
                dve.wait_ge(s_pick, t + 1)
                got = ps[:, t % 2, 0:H * 9].rearrange("p (h d) -> p h d", d=9)
                dve.reciprocal(rden[:, t % 2, :], got[:, :, DH]).then_inc(s_rd, 1)
                dve.wait_ge(s_rd, t + 1)
                if t >= 2:
                    dve.wait_ge(s_ont, t - 1)
                dve.tensor_tensor(on[:, t % 2, :].rearrange("p (h d) -> p h d", d=DH), got[:, :, 0:DH],
                                  rden[:, t % 2, :].unsqueeze(2).to_broadcast([P, H, DH]), ALU.mult).then_inc(s_on, 1)

            def add(t):
                dve.wait_ge(s_y, t + 1)
                dve.tensor_tensor(x[:, t, :], x[:, t, :], ps[:, 4 + t % 2, 0:D], ALU.add).then_inc(s_yadd, 1)

            for i in range(T + 3):
                if i < T:
                    norm(i)
                if 0 <= i - 3 < T:
                    add(i - 3)

        @block.scalar
        def _(act):
            for t in range(T):
                act.wait_ge(s_ont, t + 1)
                if t >= 2:
                    act.wait_ge(s_y, t - 1)
                act.activation(onT[:, (t % 2) * P:(t % 2) * P + P], ps[:, 2 + t % 2, 0:P],
                               ACT.Copy).then_inc(s_ontc, 1)


def layers(nc, ctx, a, keep, out):
    def sb(name, shape, dt=F32):
        return ctx.enter_context(nc.sbuf_tensor(name, shape, dt))

    def sem(name):
        return ctx.enter_context(nc.semaphore(name))

    w = {
        "xs": sb("xs", [P, T, D]),
        "xa": sb("xa", [P, T, D]),
        "hT": sb("h_t", [P, WIN + S]),
        "wqkv": sb("wqkv", [P, LAYERS, 3 * INNER]),
        "wo": sb("wo_l", [P, LAYERS, INNER // P, D]),
        "w1": sb("w1", [P, LAYERS, 2 * HID]),
        "w2": sb("w2", [P, LAYERS, len(HCH), D]),
        "gb": sb("ln_gb", [P, LAYERS, 2]),
        "b1": sb("b1", [P, LAYERS, 2, len(HCH)]),
        "b2": sb("b2", [P, LAYERS, D]),
        "tab": sb("xpos_tab", [P, 2, T, 2, LD]),
        "qks": sb("qk_scale", [P, LAYERS, 2, LD]),
        "kT": sb("k_t", [P, INNER // P, WIN + S]),
        "qpad": sb("q_padded", [P, 2, 2, INNER // P, P]),
        "v": sb("v_l", [P, T + 1, LH, LD + 1]),
        "mask": sb("mask_l", [P, 2, KEYS], BF16),
        "shift": sb("shift", [P, 2, P]),
        "work": sb("work", [P, 7 * 1024]),
    }
    xs, tab, qks = w["xs"], w["tab"], w["qks"]
    x, mv, rstd, stat, half = keep["x"], keep["mv"], keep["rstd"], keep["stat"], keep["half"]
    s_lw, s_tab, s_zero, s_scaled = sem("layer_weights"), sem("tables_in"), sem("pads_zeroed"), sem("tables_scaled")
    s_dve, s_stat, s_pool, s_rstd, s_xs = (sem(n) for n in (
        "l_dve_chain", "l_stats", "l_pool_chain", "l_rstd", "l_xs"))

    with nc.Block() as block:
        @block.sync
        def _(sp):
            for i, n in enumerate(("q_scale", "k_scale")):
                sp.dma_start(qks[:, :, i, :], a[n].unsqueeze(0).to_broadcast([P, LAYERS, LD])).then_inc(s_tab, 16)
            for i in range(2):
                sp.dma_start(tab[:, i, :, :, :], a["xpos"][i]).then_inc(s_tab, 16)
            for dst, src in (
                (w["wqkv"][:, :, :], a["wqkv"].rearrange("l c f -> c l f")),
                (w["w1"][:, :, :], a["w1"].rearrange("l c f -> c l f")),
                (w["mask"][:, :, :], a["mask_l"]),
                (w["shift"][:, :, :], a["shift"]),
                (w["b2"][:, :, :], a["b2"].unsqueeze(0).to_broadcast([P, LAYERS, D])),
                (w["gb"][:, :, :], a["ln_gb"]),
                (w["b1"][:, :, :, :], a["b1"]),
            ):
                sp.dma_start(dst, src).then_inc(s_lw, 16)
            for layer in range(LAYERS):
                sp.dma_start(w["wo"][:, layer, :, :], a["lwo"][layer].rearrange("(c p) n -> p c n", p=P)).then_inc(s_lw, 16)
                for c, rows in enumerate(HCH):
                    at = c * P
                    sp.dma_start(w["w2"][0:rows, layer, c, :], a["w2"][layer, at:at + rows, :]).then_inc(s_lw, 16)
            sp.wait_ge(s_lw, 16 * (7 + LAYERS * (1 + len(HCH))))

        @block.gpsimd
        def _(pool):
            pool.memset(w["hT"][:, 0:WIN + 1], 0.0).then_inc(s_zero, 1)
            pool.memset(w["kT"][:, :, 0:WIN], 0.0).then_inc(s_zero, 1)
            for par in range(2):
                pool.wait_ge(s_zero, 2 + par)
                pool.memset(w["qpad"][HALF * (1 - par):HALF * (2 - par), par, :, :, :], 0.0).then_inc(s_zero, 1)
            pool.wait_ge(s_zero, 4)
            pool.memset(w["v"][:, :, :, LD:LD + 1], 1.0).then_inc(s_zero, 1)
            pool.wait_ge(s_tab, 16 * 4)
            for i in range(2):
                scale_table(pool, w, 0, i).then_inc(s_scaled, 1)
                if i == 0:
                    pool.wait_ge(s_stat, T)
                    pool.tensor_scalar(rstd[:, :], mv[:, :, 1], 1e-5, None, ALU.add).then_inc(s_pool, 1)
                    pool.wait_ge(s_pool, 1)
                    pool.tensor_tensor(rstd[:, :], rstd[:, :], half[:, :], ALU.pow).then_inc(s_rstd, 1)
            pool.wait_ge(s_zero, 5)
            pool.wait_ge(s_scaled, 2)

        @block.vector
        def _(dve):
            for t in range(T):
                dve.bn_stats(stat[:, t, :], x[:, t, :]).then_inc(s_dve, 1)
            for t in range(T):
                dve.wait_ge(s_dve, t + 1)
                dve.bn_aggr(mv[:, t, :], stat[:, t, :]).then_inc(s_stat, 1)
            dve.wait_ge(s_rstd, 1)
            for t in range(T):
                dve.tensor_scalar(xs[:, t, :], x[:, t, :], mv[:, t, 0:1], rstd[:, t:t + 1],
                                  ALU.subtract, ALU.mult).then_inc(s_xs, 1)
            dve.wait_ge(s_xs, T)

    for layer in range(LAYERS):
        with ExitStack() as part:
            layer_attention(nc, part, a, keep, w, layer)
        with ExitStack() as part:
            feed_forward(nc, part, keep, w, layer, out)


def scale_table(pool, w, layer, i):
    t4 = w["tab"][:, i, :, :, :]
    return pool.tensor_tensor(t4, t4, w["qks"][:, layer, :, :].unsqueeze(1).to_broadcast([P, T, 2, LD]), ALU.mult)


def layer_attention(nc, ctx, a, keep, w, layer):
    def sem(name):
        return ctx.enter_context(nc.semaphore(f"{name}_{layer}"))

    def sb(name, shape):
        return ctx.enter_context(nc.sbuf_tensor(f"{name}_l{layer}", shape, F32))

    ps, ident, identb, half = keep["ps"], keep["ident"], keep["identb"], keep["half"]
    xs, xa, hT, kT, v, mask = w["xs"], w["xa"], w["hT"], w["kT"], w["v"], w["mask"]
    straight, exchanged = w["tab"][:, 0], w["tab"][:, 1]
    NH = 2 * LH
    HH = LH // 2
    U = 2 * T
    LAG = 3
    work = w["work"][:, :].rearrange("p (n f) -> p n f", n=7)
    sq, hat, turned, plain = work[:, 0, :], work[:, 1:3, :], work[:, 3:5, :], work[:, 5:7, :]
    norm = sb("norms", [P, 2, 2, NH])
    sub = sb("less_max", [P, 2, HH, KEYS])
    pa = sb("probs_a", [P, 2, HH, P])
    pb = sb("probs_b", [WIN, 2, HH, WIN])
    o = sb("out", [P, 2, INNER])
    oT = sb("out_t", [P, INNER])
    nmax = sb("nmax", [P, 2, HH])
    rden = sb("rden", [P, 2, HH])
    qpad = w["qpad"]
    QK, VB, SC, PA, PB, OB = 0, 2, 3, 5, 6, 7
    s_tx, s_h, s_qk, s_v, s_vc, s_sq, s_ss, s_clip, s_inv, s_hat, s_turned, s_plain, s_sum, s_t, s_tc = (
        sem(n) for n in ("x_turned", "h_ready", "qk_ready", "v_ready", "v_copied", "squares", "square_sums", "clipped",
                         "inverse_norms", "normalised", "exchanged_part", "straight_part", "rotated", "qk_turned",
                         "qk_copied"))
    s_s, s_nm, s_sub, s_e, s_pa, s_pb, s_pac, s_pbc, s_av, s_rd, s_o, s_ot, s_otc, s_y, s_xa = (
        sem(n) for n in ("w_scores", "w_max", "w_less_max", "w_exp", "w_turned_a", "w_turned_b", "w_copied_a",
                         "w_copied_b", "w_values", "w_rden", "w_out", "w_out_turned", "w_out_copied", "w_projected",
                         "w_added"))
    s_tab, s_scaled = sem("w_tables_in"), sem("w_tables_scaled")

    def heads(ap):
        return ap.rearrange("p (i h d) -> p i h d", i=2, d=LD)

    ROUNDS = T + LAG + 3

    with nc.Block() as block:
        if layer + 1 < LAYERS:
            @block.sync
            def _(sp):
                sp.wait_ge(s_plain, T)
                sp.wait_ge(s_turned, 2 * T)
                for i in range(2):
                    sp.dma_start(w["tab"][:, i, :, :, :], a["xpos"][i]).then_inc(s_tab, 16)

        @block.tensor
        def _(pe):
            def turn_x(b):
                if b >= 1:
                    pe.wait_ge(s_vc, TPB * (b - 1) + 1)
                for j in range(TPB):
                    mm = pe.transpose(ps[:, VB, j * P:(j + 1) * P], xs[:, TPB * b + j, :], ident[:, :])
                mm.then_inc(s_tx, 1)

            def project(t):
                pe.wait_ge(s_h, 2 * (t // TPB + 1))
                if t >= 2:
                    pe.wait_ge(s_tc, 3 * (t - 1))
                elif t == 1:
                    pe.wait_ge(s_hat, 1)
                    pe.wait_ge(s_sq, 1)
                at = WIN + t * P
                for i in range(2):
                    mm = pe.matmul(ps[:, QK + i, :], hT[:, at:at + P],
                                   w["wqkv"][:, layer, i * INNER:(i + 1) * INNER], start=True, stop=True)
                mm.then_inc(s_qk, 1)

            def turn(t):
                pe.wait_ge(s_sum, t + 1)
                pe.wait_ge(s_hat, min(t + 2, T))
                pe.wait_ge(s_sq, min(t + 2, T))
                if t == T - 1:
                    pe.wait_ge(s_tc, 3 * t)
                for n in range(2 * INNER // P):
                    mm = pe.transpose(ps[:, QK + n // 4, n % 4 * P:(n % 4 + 1) * P],
                                      hat[:, t % 2, n * P:(n + 1) * P], ident[:, :])
                mm.then_inc(s_t, 1)

            def project_values(t):
                rows = P if t < T else WIN
                pe.wait_ge(s_h, 2 * min(t // TPB + 1, NB))
                if t % TPB == 1 and t // TPB + 1 < NB:
                    pe.wait_ge(s_h, 2 * (t // TPB + 2))
                if t >= 1:
                    pe.wait_ge(s_vc, t)
                pe.matmul(ps[0:rows, VB, :], hT[:, t * P:t * P + rows], w["wqkv"][:, layer, 2 * INNER:3 * INNER],
                          start=True, stop=True).then_inc(s_v, 1)

            def scores(u):
                t, par = divmod(u, 2)
                if u >= 1:
                    pe.wait_ge(s_sub, u)
                pe.wait_ge(s_tc, 3 * (t + 1))
                for b in range(2):
                    bank = ps[:, SC + b, 0:2 * KEYS].rearrange("p (h k) -> p h k", h=2)
                    for j in range(2):
                        n = 2 * b + j
                        pe.matmul(bank[:, j, :], qpad[:, par, t % 2, n, :], kT[:, n, t * P:t * P + KEYS],
                                  start=j == 0, stop=False, skip_group_check=True)
                    m = mask[:, min(t, 1):min(t, 1) + 1, :].to_broadcast([P, 2, KEYS])
                    mm = pe.matmul(bank, identb[:, :], m, start=False, stop=True, skip_group_check=True)
                mm.then_inc(s_s, 1)

            def turn_probs(u):
                t, par = divmod(u, 2)
                pe.wait_ge(s_e, u + 1)
                if u >= 1:
                    pe.wait_ge(s_pac, u)
                if par == 0 and t >= 2:
                    pe.wait_ge(s_otc, t - 1)
                elif par == 0 and t == 1:
                    pe.wait_ge(s_pbc, u)
                elif par == 1 and t >= 2:
                    pe.wait_ge(s_xa, t - 1)
                elif par == 1:
                    pe.wait_ge(s_pbc, u)
                for n in range(HH):
                    mm = pe.transpose(ps[0:WIN, PB, n * WIN:(n + 1) * WIN], sub[WIN:P, u % 2, n, P:KEYS],
                                      ident[WIN:P, WIN:P])
                mm.then_inc(s_pb, 1)
                for n in range(HH):
                    mm = pe.transpose(ps[:, PA, n * P:(n + 1) * P], sub[:, u % 2, n, 0:P], ident[:, :])
                mm.then_inc(s_pa, 1)

            def values(u):
                t, par = divmod(u, 2)
                pe.wait_ge(s_pac, u + 1)
                pe.wait_ge(s_pbc, u + 1)
                pe.wait_ge(s_vc, t + 2)
                if u >= 1:
                    pe.wait_ge(s_o, u)
                for n in range(HH):
                    cols = slice(n * (LD + 1), (n + 1) * (LD + 1))
                    pe.matmul(ps[:, OB, cols], pa[:, u % 2, n, :], v[:, t, 2 * n + par, :],
                              start=True, stop=False, skip_group_check=True)
                    mm = pe.matmul(ps[WIN:P, OB, cols], pb[:, u % 2, n, :], v[0:WIN, t + 1, 2 * n + par, :],
                                   start=False, stop=True, skip_group_check=True)
                mm.then_inc(s_av, 1)

            def turn_out(t):
                pe.wait_ge(s_o, 2 * t + 2)
                pe.wait_ge(s_pbc, min(2 * t + 4, U))
                if t >= 1:
                    pe.wait_ge(s_xa, t)
                for c in range(INNER // P):
                    mm = pe.transpose(ps[:, PB, c * P:(c + 1) * P], o[:, t % 2, c * P:(c + 1) * P], ident[:, :])
                mm.then_inc(s_ot, 1)

            def project_out(t):
                pe.wait_ge(s_otc, t + 1)
                pe.wait_ge(s_pbc, min(2 * t + 5, U))
                for c in range(INNER // P):
                    mm = pe.matmul(ps[:, PB, 0:D], oT[:, c * P:(c + 1) * P], w["wo"][:, layer, c, :],
                                   start=c == 0, stop=c == INNER // P - 1)
                mm.then_inc(s_y, 1)

            turn_x(0)
            for i in range(ROUNDS):
                u = 2 * (i - LAG)
                if 0 <= u < U:
                    scores(u)
                if i % TPB == 1 and i // TPB + 1 < NB:
                    turn_x(i // TPB + 1)
                if 0 <= i - 2 < T:
                    turn(i - 2)
                if 0 <= u - 1 < U:
                    turn_probs(u - 1)
                if i < T:
                    project(i)
                if 0 <= u - 2 < U:
                    values(u - 2)
                if 0 <= u - 4 < U:
                    turn_out(u // 2 - 2)
                u += 1
                if 0 <= u < U:
                    scores(u)
                if 0 <= u - 1 < U:
                    turn_probs(u - 1)
                if i < T + 1:
                    project_values(i)
                if 0 <= u - 2 < U:
                    values(u - 2)
                if 0 <= u - 5 < U:
                    project_out(u // 2 - 2)

        @block.scalar
        def _(act):
            def copy_h(b):
                act.wait_ge(s_tx, b + 1)
                at = WIN + b * BLK
                act.activation(hT[0:D // 2, at:at + BLK], ps[0:D // 2, VB, :], ACT.Copy).then_inc(s_h, 1)
                n = BLK if b < NB - 1 else BLK - 1
                act.activation(hT[D // 2:D, at + 1:at + 1 + n], ps[D // 2:D, VB, 0:n], ACT.Copy).then_inc(s_h, 1)

            def square(t):
                act.wait_ge(s_qk, t + 1)
                if t >= 1:
                    act.wait_ge(s_ss, t)
                act.activation(sq, ps[:, QK:QK + 2, :].rearrange("p a b -> p (a b)"), ACT.Square).then_inc(s_sq, 1)

            def copy_values(t):
                rows = P if t < T else WIN
                act.wait_ge(s_v, t + 1)
                act.activation(v[0:rows, t, :, 0:LD], ps[0:rows, VB, :].rearrange("p (h d) -> p h d", d=LD),
                               ACT.Copy).then_inc(s_vc, 1)

            def copy_qk(t):
                act.wait_ge(s_t, t + 1)
                if t >= 2:
                    act.wait_ge(s_s, 2 * (t - 1))
                at = WIN + t * P
                for par in range(2):
                    rows = slice(HALF * par, HALF * (par + 1))
                    act.activation(qpad[rows, par, t % 2, :, :],
                                   ps[rows, QK, :].rearrange("p (n q) -> p n q", q=P), ACT.Copy).then_inc(s_tc, 1)
                act.activation(kT[:, :, at:at + P], ps[:, QK + 1, :].rearrange("p (n q) -> p n q", q=P),
                               ACT.Copy).then_inc(s_tc, 1)

            def exp(u):
                act.wait_ge(s_sub, u + 1)
                act.activation(sub[:, u % 2, :, :], sub[:, u % 2, :, :], ACT.Exp, scale=8.0).then_inc(s_e, 1)

            def copy_probs(u):
                if u >= 2:
                    act.wait_ge(s_av, u - 1)
                act.wait_ge(s_pb, u + 1)
                act.activation(pb[:, u % 2].rearrange("p h q -> p (h q)"), ps[0:WIN, PB, 0:HH * WIN],
                               ACT.Copy).then_inc(s_pbc, 1)
                act.wait_ge(s_pa, u + 1)
                act.activation(pa[:, u % 2].rearrange("p h q -> p (h q)"), ps[:, PA, :], ACT.Copy).then_inc(s_pac, 1)

            def copy_out(t):
                act.wait_ge(s_ot, t + 1)
                if t >= 1:
                    act.wait_ge(s_y, t)
                act.activation(oT[:, :], ps[:, PB, :], ACT.Copy).then_inc(s_otc, 1)

            copy_h(0)
            for i in range(ROUNDS):
                u = 2 * (i - LAG)
                if i % TPB == 1 and i // TPB + 1 < NB:
                    copy_h(i // TPB + 1)
                if 0 <= i - 2 < T:
                    copy_qk(i - 2)
                if 0 <= u - 1 < U:
                    copy_probs(u - 1)
                if 0 <= u < U:
                    exp(u)
                if i < T:
                    square(i)
                if 0 <= u - 4 < U:
                    copy_out(u // 2 - 2)
                u += 1
                if 0 <= u - 1 < U:
                    copy_probs(u - 1)
                if 0 <= u < U:
                    exp(u)
                if i < T + 1:
                    copy_values(i)

        @block.gpsimd
        def _(pool):
            def inverse_norm(t):
                pool.wait_ge(s_ss, t + 1)
                pool.tensor_scalar(norm[:, t % 2, 0, :], norm[:, t % 2, 0, :], 1e-24, None, ALU.max).then_inc(s_clip, 1)
                pool.wait_ge(s_clip, t + 1)
                if t >= 2:
                    pool.wait_ge(s_hat, t - 1)
                pool.tensor_tensor(norm[:, t % 2, 1, :], norm[:, t % 2, 0, :], half[:, :], ALU.pow).then_inc(s_inv, 1)

            def plain_part(t):
                pool.wait_ge(s_hat, t + 1)
                if t >= 2:
                    pool.wait_ge(s_sum, t - 1)
                pool.tensor_tensor(heads(plain[:, t % 2, :]), heads(hat[:, t % 2, :]),
                                   straight[:, t].unsqueeze(2).to_broadcast([P, 2, LH, LD]), ALU.mult).then_inc(s_plain, 1)

            for t in range(T):
                inverse_norm(t)
                plain_part(t)
            if layer + 1 < LAYERS:
                pool.wait_ge(s_tab, 32)
                for i in range(2):
                    scale_table(pool, w, layer + 1, i).then_inc(s_scaled, 1)
                pool.wait_ge(s_scaled, 2)

        @block.vector
        def _(dve):
            def sums(t):
                dve.wait_ge(s_sq, t + 1)
                if t >= 2:
                    dve.wait_ge(s_inv, t - 1)
                dve.tensor_reduce(norm[:, t % 2, 0, :], sq.rearrange("p (h d) -> p h d", d=LD), X_AXIS,
                                  ALU.add).then_inc(s_ss, 1)

            def normalise(t):
                dve.wait_ge(s_inv, t + 1)
                if t >= 2:
                    dve.wait_ge(s_t, t - 1)
                qk = ps[:, QK:QK + 2, :].rearrange("p i (h d) -> p (i h) d", d=LD)
                dve.tensor_tensor(hat[:, t % 2, :].rearrange("p (h d) -> p h d", d=LD), qk,
                                  norm[:, t % 2, 1, :].unsqueeze(2).to_broadcast([P, NH, LD]), ALU.mult).then_inc(s_hat, 1)

            def exchange(t):
                dve.wait_ge(s_hat, t + 1)
                for k in range(2):
                    a, b = k * LD // 2, (1 - k) * LD // 2
                    dve.tensor_tensor(heads(turned[:, t % 2, :])[:, :, :, b:b + LD // 2],
                                      heads(hat[:, t % 2, :])[:, :, :, a:a + LD // 2],
                                      exchanged[:, t, :, a:a + LD // 2].unsqueeze(2).to_broadcast([P, 2, LH, LD // 2]),
                                      ALU.mult).then_inc(s_turned, 1)

            def rotate(t):
                dve.wait_ge(s_turned, 2 * t + 2)
                dve.wait_ge(s_plain, t + 1)
                dve.tensor_tensor(hat[:, t % 2, :], turned[:, t % 2, :], plain[:, t % 2, :], ALU.add).then_inc(s_sum, 1)

            def less_max(u):
                dve.wait_ge(s_s, u + 1)
                got = ps[:, SC:SC + 2, 0:2 * KEYS].rearrange("p b (h k) -> p b h k", h=2)
                dve.tensor_reduce(nmax[:, u % 2, :].rearrange("p (b h) -> p b h", b=2), got, X_AXIS, ALU.max,
                                  negate=True).then_inc(s_nm, 1)
                dve.wait_ge(s_nm, u + 1)
                if u >= 2:
                    dve.wait_ge(s_pa, u - 1)
                dve.tensor_tensor(sub[:, u % 2].rearrange("p (b h) k -> p b h k", b=2), got,
                                  nmax[:, u % 2, :].rearrange("p (b h) -> p b h", b=2).unsqueeze(3)
                                  .to_broadcast([P, 2, 2, KEYS]), ALU.add).then_inc(s_sub, 1)

            def divide(u):
                t, par = divmod(u, 2)
                dve.wait_ge(s_av, u + 1)
                got = ps[:, OB, 0:HH * (LD + 1)].rearrange("p (h d) -> p h d", d=LD + 1)
                dve.reciprocal(rden[:, u % 2, :], got[:, :, LD]).then_inc(s_rd, 1)
                dve.wait_ge(s_rd, u + 1)
                if t >= 2:
                    dve.wait_ge(s_ot, t - 1)
                dve.tensor_tensor(o[:, t % 2, :].rearrange("p (h a d) -> p h a d", a=2, d=LD)[:, :, par, :],
                                  got[:, :, 0:LD], rden[:, u % 2, :].unsqueeze(2).to_broadcast([P, HH, LD]),
                                  ALU.mult).then_inc(s_o, 1)

            def add(t):
                dve.wait_ge(s_y, t + 1)
                dve.tensor_tensor(xa[:, t, :], xs[:, t, :], ps[:, PB, 0:D], ALU.add).then_inc(s_xa, 1)

            for i in range(ROUNDS):
                u = 2 * (i - LAG)
                if 0 <= i - 1 < T:
                    exchange(i - 1)
                if 0 <= u < U:
                    less_max(u)
                if i < T:
                    sums(i)
                if 0 <= u - 2 < U:
                    divide(u - 2)
                u += 1
                if 0 <= i - 1 < T:
                    rotate(i - 1)
                if 0 <= u < U:
                    less_max(u)
                if 0 <= u - 2 < U:
                    divide(u - 2)
                if i < T:
                    normalise(i)
                if 0 <= u - 5 < U:
                    add(u // 2 - 2)


def feed_forward(nc, ctx, keep, w, layer, out):
    def sem(name):
        return ctx.enter_context(nc.semaphore(f"{name}_{layer}"))

    ps, ident, half, x, rstd, mv = (keep[n] for n in ("ps", "ident", "half", "x", "rstd", "mv"))
    xs, xa, shift = w["xs"], w["xa"], w["shift"]
    stat = ctx.enter_context(nc.sbuf_tensor(f"stat_{layer}", [P, TPB, 2, 6], F32))
    work = w["work"]
    hn = work[:, 0:TPB * D].rearrange("p (t c) -> p t c", t=TPB)
    hnT = work[:, 512:512 + 2 * BLK].rearrange("p (b s) -> p b s", b=2)
    gate = work[:, 1536:1536 + 2 * BLK].rearrange("p (b s) -> p b s", b=2)
    hid = work[:, 2560:2560 + 2 * 3 * BLK].rearrange("p (b c s) -> p b c s", b=2, c=3)
    res = work[:, 5632:5632 + 2 * TPB * D].rearrange("p (b t c) -> p b t c", b=2, t=TPB)
    SH, HB, YB = 4, 5, 6
    last = layer == LAYERS - 1
    C = len(HCH)
    s_sh, s_st, s_mv, s_eps, s_rs, s_hn, s_ht, s_htc, s_ag, s_gate, s_hid, s_y, s_x = (
        sem(n) for n in ("f_shifted", "f_stats", "f_mean_var", "f_eps", "f_rstd", "f_normed", "f_turned", "f_copied",
                         "f_hidden", "f_gate", "f_product", "f_out", "f_added"))
    s_store, s_res, s_bias = sem("stored"), sem("f_residual"), sem("f_bias_in")

    with nc.Block() as block:
        @block.tensor
        def _(pe):
            def shift_tokens(b):
                if b >= 1:
                    pe.wait_ge(s_hn, 2 * TPB * b)
                for j in range(TPB):
                    t = TPB * b + j
                    dst = ps[:, SH, j * D // 2:(j + 1) * D // 2]
                    mm = pe.matmul(dst, shift[:, 0, :], xa[:, t, D // 2:D], start=True, stop=t == 0)
                    if t >= 1:
                        mm = pe.matmul(dst, shift[:, 1, :], xa[:, t - 1, D // 2:D], start=False, stop=True)
                mm.then_inc(s_sh, 1)

            def turn(b):
                pe.wait_ge(s_hn, 2 * TPB * (b + 1))
                if b >= 1:
                    pe.wait_ge(s_htc, b)
                for j in range(TPB):
                    mm = pe.transpose(ps[:, HB, j * P:(j + 1) * P], hn[:, j, :], ident[:, :])
                mm.then_inc(s_ht, 1)

            def hidden(b, c):
                n = C * b + c
                rows = HCH[c]
                pe.wait_ge(s_htc, b + 1)
                if n >= 2:
                    pe.wait_ge(s_hid, n - 1)
                for i in range(2):
                    at = i * HID + c * P
                    mm = pe.matmul(ps[0:rows, 2 * (n % 2) + i, :], w["w1"][:, layer, at:at + rows], hnT[:, b % 2, :],
                                   start=True, stop=True)
                mm.then_inc(s_ag, 1)

            def down(b):
                pe.wait_ge(s_hid, C * (b + 1))
                if b >= 2:
                    pe.wait_ge(s_x, b - 1)
                for j in range(TPB):
                    for c, rows in enumerate(HCH):
                        mm = pe.matmul(ps[:, YB + b % 2, j * D:(j + 1) * D], hid[0:rows, b % 2, c, j * P:(j + 1) * P],
                                       w["w2"][0:rows, layer, c, :], start=c == 0, stop=c == C - 1)
                mm.then_inc(s_y, 1)

            shift_tokens(0)
            turn(0)
            shift_tokens(1)
            for b in range(NB + 1):
                if b < NB:
                    hidden(b, 0)
                if b >= 1:
                    down(b - 1)
                if b < NB:
                    hidden(b, 1)
                if b + 1 < NB:
                    turn(b + 1)
                if b + 2 < NB:
                    shift_tokens(b + 2)
                if b < NB:
                    hidden(b, 2)

        @block.vector
        def _(dve):
            def stats(b):
                n = 2 * TPB * b
                for j in range(TPB):
                    dve.bn_stats(stat[:, j, 0, :], xa[:, TPB * b + j, 0:D // 2]).then_inc(s_st, 1)
                dve.wait_ge(s_sh, b + 1)
                for j in range(TPB):
                    dve.bn_stats(stat[:, j, 1, :], ps[:, SH, j * D // 2:(j + 1) * D // 2]).then_inc(s_st, 1)
                for j in range(TPB):
                    dve.wait_ge(s_st, n + TPB + j + 1)
                    dve.bn_aggr(mv[:, TPB * b + j, :], stat[:, j, :, :].rearrange("p a b -> p (a b)")).then_inc(s_mv, 1)

            def normalise(b):
                dve.wait_ge(s_rs, b + 1)
                if b >= 1:
                    dve.wait_ge(s_ht, b)
                for j in range(TPB):
                    t = TPB * b + j
                    dve.tensor_scalar(hn[:, j, 0:D // 2], xa[:, t, 0:D // 2], mv[:, t, 0:1], rstd[:, t:t + 1],
                                      ALU.subtract, ALU.mult).then_inc(s_hn, 1)
                    dve.tensor_scalar(hn[:, j, D // 2:D], ps[:, SH, j * D // 2:(j + 1) * D // 2], mv[:, t, 0:1],
                                      rstd[:, t:t + 1], ALU.subtract, ALU.mult).then_inc(s_hn, 1)

            def product(b, c):
                n = C * b + c
                rows = HCH[c]
                dve.wait_ge(s_gate, n + 1)
                if b >= 2:
                    dve.wait_ge(s_y, b - 1)
                dve.scalar_tensor_tensor(out=hid[0:rows, b % 2, c, :], in0=ps[0:rows, 2 * (n % 2), :],
                                         scalar=w["b1"][0:rows, layer, 0, c:c + 1], in1=gate[0:rows, n % 2, :],
                                         op0=ALU.add, op1=ALU.mult).then_inc(s_hid, 1)

            def add(b):
                tiles = slice(TPB * b, TPB * (b + 1))
                dve.wait_ge(s_y, b + 1)
                dve.wait_ge(s_res, b + 1)
                dve.tensor_tensor((x if last else xs)[:, tiles, :], res[:, b % 2, :, :],
                                  ps[:, YB + b % 2, :].rearrange("p (t c) -> p t c", t=TPB), ALU.add).then_inc(s_x, 1)

            stats(0)
            normalise(0)
            stats(1)
            for b in range(NB + 1):
                if b < NB:
                    product(b, 0)
                if b + 1 < NB:
                    normalise(b + 1)
                if b >= 1:
                    add(b - 1)
                if b < NB:
                    product(b, 1)
                if b + 2 < NB:
                    stats(b + 2)
                if b < NB:
                    product(b, 2)
            dve.wait_ge(s_x, NB)

        @block.gpsimd
        def _(pool):
            for b in range(NB):
                tiles = slice(TPB * b, TPB * (b + 1))
                pool.wait_ge(s_mv, TPB * (b + 1))
                pool.tensor_scalar(mv[:, tiles, 1], mv[:, tiles, 1], 1e-5, None, ALU.add).then_inc(s_eps, 1)
                pool.wait_ge(s_eps, b + 1)
                pool.tensor_tensor(rstd[:, tiles], mv[:, tiles, 1], half[:, 0:TPB], ALU.pow).then_inc(s_rs, 1)
                if b >= 2:
                    pool.wait_ge(s_x, b - 1)
                ins = pool.tensor_tensor(res[:, b % 2, :, :], xa[:, tiles, :],
                                         w["b2"][:, layer, :].unsqueeze(1).to_broadcast([P, TPB, D]), ALU.add)
                if last:
                    ins.then_inc(s_bias, 1)
                    pool.wait_ge(s_bias, b + 1)
                    ins = pool.tensor_tensor(res[:, b % 2, :, :], res[:, b % 2, :, :], x[:, tiles, :], ALU.add)
                ins.then_inc(s_res, 1)

        @block.scalar
        def _(act):
            def copy_turned(b):
                act.wait_ge(s_ht, b + 1)
                if b >= 2:
                    act.wait_ge(s_ag, C * (b - 1))
                act.activation(hnT[:, b % 2, :], ps[:, HB, :], ACT.Identity, bias=w["gb"][:, layer, 1:2],
                               scale=w["gb"][:, layer, 0:1]).then_inc(s_htc, 1)

            def gelu(b, c):
                n = C * b + c
                rows = HCH[c]
                act.wait_ge(s_ag, n + 1)
                if n >= 2:
                    act.wait_ge(s_hid, n - 1)
                act.activation(gate[0:rows, n % 2, :], ps[0:rows, 2 * (n % 2) + 1, :], ACT.Gelu,
                               bias=w["b1"][0:rows, layer, 1, c:c + 1]).then_inc(s_gate, 1)

            copy_turned(0)
            for b in range(NB):
                gelu(b, 0)
                gelu(b, 1)
                if b + 1 < NB:
                    copy_turned(b + 1)
                gelu(b, 2)

        if last:
            @block.sync
            def _(sp):
                for b in range(NB):
                    sp.wait_ge(s_x, b + 1)
                    sp.dma_start(out[b * BLK:(b + 1) * BLK, :].rearrange("(t p) c -> p t c", p=P),
                                 x[:, TPB * b:TPB * (b + 1), :]).then_inc(s_store, 16)
                sp.wait_ge(s_store, 16 * NB)


def shape_constants():
    f32, bf16 = np.float32, mybir.dt.np(BF16)
    c = {}
    c["ident"] = np.eye(P, dtype=f32)
    c["identb"] = np.eye(P, dtype=bf16)
    ahead = np.where(np.arange(P)[None, :] > np.arange(P)[:, None], NEG, 0.0)
    c["mask_q"] = ahead.astype(bf16)
    c["mask_k"] = np.ascontiguousarray(ahead.T).astype(bf16)
    c["ones"] = np.ones((2, PAIRS * S), bf16)
    pick = np.zeros((P, 4 * 9), f32)
    for j in range(4):
        for d in range(9):
            pick[VW * j + d, 9 * j + d] = 1.0
    c["pick"] = pick
    inv = (1.0 / np.power(10000.0, np.arange(0, DH, 2, dtype=f32).astype(np.float64) / DH).astype(f32)).astype(f32)
    ang = np.outer(np.arange(S, dtype=f32), inv).astype(f32).astype(np.float64)
    ang = np.concatenate([ang, ang], axis=1)
    sign = np.where(np.arange(DH) < DH // 2, -1.0, 1.0)
    rows = np.arange(P) // PAIRS % DH
    c["rope"] = np.stack([np.cos(ang)[:, rows].T, (np.sin(ang) * sign)[:, rows].T]).astype(f32)
    inv = (1.0 / np.power(10000.0, np.arange(0, LD, 2, dtype=f32).astype(np.float64) / LD).astype(f32)).astype(f32)
    tok = np.arange(S, dtype=f32)
    ang = (tok[:, None] * inv[None, :]).astype(f32).astype(np.float64)
    base = (np.arange(0, LD, 2) + 0.4 * LD) / (1.4 * LD)
    power = (tok.astype(np.float64) - S // 2) / (WIN // 2)
    grow = base.astype(f32).astype(np.float64)[None, :] ** power[:, None]
    both = [np.concatenate([m, m], axis=1) for m in (np.cos(ang), np.sin(ang), grow)]
    sign = np.where(np.arange(LD) < LD // 2, 1.0, -1.0)
    tabs = []
    for m in (both[0], both[1] * sign):
        qk = np.stack([m * both[2], m / both[2]], axis=1)
        tabs.append(qk.reshape(T, P, 2, LD).transpose(1, 0, 2, 3))
    c["xpos"] = np.ascontiguousarray(np.stack(tabs)).astype(f32)
    i, j = np.arange(P)[:, None], np.arange(KEYS)[None, :] - WIN
    hidden = (j > i) | (j < i - WIN)
    c["mask_l"] = np.where(np.stack([hidden | (j < 0), hidden], axis=1), NEG, 0.0).astype(bf16)
    c["shift"] = np.ascontiguousarray(np.stack([np.eye(P, k=1), np.eye(P, k=1 - P)], axis=1)).astype(f32)
    return c


def kernel(L0_attn_x, L0_attn_Wq, L0_attn_Wk, L0_attn_Wv, L0_attn_Wo, L0_ffn_wqkv, L0_ffn_q_scale, L0_ffn_k_scale,
           L0_ffn_wo, L0_ffn_ln_g, L0_ffn_ln_b, L0_ffn_w1, L0_ffn_b1, L0_ffn_w2, L0_ffn_b2):
    import concourse.bacc as _bacc
    from concourse.bass_utils import run_bass_kernel_spmd as _run

    arrays = shape_constants()
    order = np.array([(2 * pair + par) * DH + d for par in range(2) for d in range(DH) for pair in range(PAIRS)])
    turned = order // DH * DH + (order % DH + DH // 2) % DH
    wq, wk = np.asarray(L0_attn_Wq), np.asarray(L0_attn_Wk)
    arrays["wqk"] = np.ascontiguousarray(np.stack([wq[order].T, wq[turned].T, wk[order].T, wk[turned].T]))
    arrays["wv"] = np.ascontiguousarray(np.asarray(L0_attn_Wv).T)
    arrays["wo"] = np.ascontiguousarray(np.asarray(L0_attn_Wo).T)
    for name, value in (("wqkv", L0_ffn_wqkv), ("q_scale", L0_ffn_q_scale), ("k_scale", L0_ffn_k_scale),
                        ("lwo", L0_ffn_wo), ("w1", L0_ffn_w1), ("w2", L0_ffn_w2), ("b2", L0_ffn_b2)):
        arrays[name] = np.ascontiguousarray(np.asarray(value))
    arrays["ln_gb"] = np.ascontiguousarray(np.stack([np.asarray(L0_ffn_ln_g), np.asarray(L0_ffn_ln_b)], 2).transpose(1, 0, 2))
    b1 = np.zeros((P, LAYERS, 2, len(HCH)), np.float32)
    for c, rows in enumerate(HCH):
        for i in range(2):
            b1[:rows, :, i, c] = np.asarray(L0_ffn_b1)[:, i * HID + c * P:i * HID + c * P + rows].T
    arrays["b1"] = b1
    arrays["x"] = np.ascontiguousarray(np.asarray(L0_attn_x).reshape(S, D))

    nc = _bacc.Bacc("TRN2", target_bir_lowering=False, num_devices=1)
    arrays = {"in_" + n: v for n, v in arrays.items()}
    aps = {n[3:]: nc.dram_tensor(n, v.shape, mybir.dt.from_np(v.dtype), kind="ExternalInput").ap()
           for n, v in arrays.items()}
    out = nc.dram_tensor("out", (S, D), F32, kind="ExternalOutput").ap()
    build(nc, aps, out)
    r = _run(nc, [arrays], core_ids=[0])
    return r.results[0]["out"].reshape(1, S, D)
```

```python
from contextlib import ExitStack

import numpy as np

import concourse.bass as bass
from concourse import mybir

F32 = mybir.dt.float32
BF16 = mybir.dt.bfloat16
ALU = mybir.AluOpType
ACT = mybir.ActivationFunctionType
X_AXIS = mybir.AxisListType.X

P = 128
S = 2048
D = 128
T = S // P
BLK = 512
NB = S // BLK
TPB = BLK // P
H = 16
DH = D // H
PAIRS = H // 2
GROUPS = H // 4
HALF = 64
SPLIT = 6 * DH
VW = 32
NEG = -1e30
ORDER = (0, 0, 1, 1, 2, 2, 2, 3, 2, 3, 3, 1, 3, 0, 1, 0)
CHUNKS = [(q, ORDER[:k].count(q)) for k, q in enumerate(ORDER)]
NC = len(CHUNKS)

LH = 8
LD = 64
WIN = 64
INNER = LH * LD
HID = 341
HCH = (128, 128, 85)
LAYERS = 2
SCORE_SCALE = 8.0
KEYS = WIN + P


def max_units(q, g):
    return [(t, pair, c, par) for t in range(TPB * q, TPB * (q + 1)) for pair in (2 * g, 2 * g + 1)
            for c in range(t // TPB + 1) for par in range(2)]


def share(weights, steps):
    marks, done = [], 0
    for weight in steps:
        done += weight
        marks.append(done / sum(steps) * sum(weights))
    ranges, n, at = [], 0, 0
    for k, mark in enumerate(marks):
        first = n
        while n < len(weights) and (k + 1 == len(marks) or at + weights[n] / 2 <= mark):
            at += weights[n]
            n += 1
        ranges.append(range(first, n))
    return ranges


def build(nc, a, out):
    with ExitStack() as ctx:
        def sb(name, shape, dt=F32):
            return ctx.enter_context(nc.sbuf_tensor(name, shape, dt))

        keep = {
            "ps": ctx.enter_context(nc.psum_tensor("ps", [P, 8, BLK], F32)),
            "x": sb("x_rows", [P, T, D]),
            "ident": sb("ident", [P, P]),
            "identb": sb("identb", [P, P], BF16),
            "half": sb("minus_half", [P, 16]),
            "mv": sb("mean_var", [P, T, 2]),
            "rstd": sb("rstd", [P, T]),
            "stat": sb("stat", [P, T, 6]),
            "early": sb("early", [P, 4, S]),
            "wo": sb("wo_t", [P, D]),
            "pick": sb("pick", [P, 4 * 9]),
        }
        with ExitStack() as attn:
            first_attention(nc, attn, a, keep)
        with ExitStack() as ffn:
            layers(nc, ffn, a, keep, out)


def first_attention(nc, ctx, a, keep):
    def sb(name, shape, dt=F32):
        return ctx.enter_context(nc.sbuf_tensor(name, shape, dt))

    def sem(name):
        return ctx.enter_context(nc.semaphore(name))

    ps, x, ident, identb = keep["ps"], keep["x"], keep["ident"], keep["identb"]
    half, mv, rstd, stat = keep["half"], keep["mv"], keep["rstd"], keep["stat"]

    early, wo, pick = keep["early"], keep["wo"], keep["pick"]
    xn = early[:, 0, :].rearrange("p (t c) -> p t c", t=T)
    xT = early[:, 1, :]
    rope = early[:, 2:4, :]
    outT = early
    wqk = sb("wqk", [P, 4, D])
    wv = sb("wv", [P, D])
    mask_q = sb("mask_q", [P, P], BF16)
    mask_k = sb("mask_k", [P, P], BF16)
    probs = sb("probs", [P, 2, 2, 2, BLK])
    prod = probs[:, 0, :, :, :]
    full = probs[:, 1, 0, :, :]
    rest = probs[:, 1, 1, :, :]
    part = sb("split_part", [P, 2, 2, 3, BLK], BF16)
    qs = sb("q_stack", [P, NB // 2, PAIRS, 2, BLK], BF16)
    ks = sb("k_stack", [P, 2, NB // 2, PAIRS, 2, BLK], BF16)
    v = sb("v_rows", [P, T, H, VW])
    mpart = sb("max_part", [P, TPB, 4, NB])
    mneg = sb("max_neg", [P, 2, TPB, 4])
    mrow = sb("max_rows", [4, 2, BLK], BF16)

    s_x = [sem(f"x_loaded{g}") for g in range(NB)]
    s_w, s_rope, s_const = sem("weights_loaded"), sem("rope_loaded"), sem("const_loaded")
    nil = sb("zero", [P, 1])
    s_half, s_vset, s_nil = sem("half_set"), sem("v_ones_set"), sem("zero_set")
    s_dve, s_dstat = sem("dve_chain"), sem("stats_done")
    s_pool, s_rstd = sem("pool_chain"), sem("rstd_done")
    s_xn, s_xt, s_xtc = sem("xn_done"), sem("xt_turned"), sem("xt_copied")
    s_proj, s_v, s_vc = sem("projected"), sem("v_projected"), sem("v_copied")
    s_prod, s_full, s_high, s_rest, s_mid, s_low = (sem(n) for n in (
        "rope_products", "rope_sum", "high_part", "rest_left", "middle_part", "low_part"))
    s_stack = [sem(f"stacked{h}") for h in range(NB // 2)]
    s_ones, s_zero = sem("ones_rows"), sem("stacks_zeroed")
    s_spread = [sem(f"spread{b}") for b in range(NB)]
    spread = nc.dram_tensor("spread", (NB // 2, 2, 3, 2 * DH, PAIRS, 2, BLK), BF16, kind="Internal").ap()

    def parts_to_dram(sp, h):
        both = range(2 * h, 2 * h + 2)
        for b in both:
            sp.wait_ge(s_low, 2 * b + 2)
            sp.dma_start(spread[h, :, :, :, :, b % 2, :].rearrange("i w r n s -> (r n) (i w) s"),
                         part[:, b % 2, :, :, :].rearrange("p i w s -> p (i w) s")).then_inc(s_spread[b], 16)

    def dram_to_stacks(sp, h):
        for b in range(2 * h, 2 * h + 2):
            sp.wait_ge(s_spread[b], 16)
        for par in range(2):
            row = HALF * par
            d = slice(DH * par, DH * (par + 1))
            for w, times in ((0, 3), (1, 2), (2, 1)):
                sp.dma_start(qs[row:row + DH * times, h, :, :, :].rearrange("r n b s -> r (n b s)"),
                             spread[h, 0, w:w + 1, d].rearrange("w d n b s -> w d (n b s)")
                             .to_broadcast([times, DH, PAIRS * 2 * BLK])).then_inc(s_stack[h], 16)
                sp.dma_start(ks[row:row + DH * times, par, h, :, :, :].rearrange("r n b s -> r (n b s)"),
                             spread[h, 1, 0:times, d].rearrange("w d n b s -> w d (n b s)")
                             ).then_inc(s_stack[h], 16)
                row += DH * times

    PIECE = 1024
    halves = [t.bitcast(F32) for t in (qs[:, :, :, :, :].rearrange("p h n b s -> p (h n b s)"),
                                       ks[:, 0, :, :, :, :].rearrange("p h n b s -> p (h n b s)"),
                                       ks[:, 1, :, :, :, :].rearrange("p h n b s -> p (h n b s)"))]
    pieces = [t[:, n:n + PIECE] for t in halves for n in range(0, NB * PAIRS * BLK // 2, PIECE)]
    ZEROS = len(pieces)
    by_act = 6

    with nc.Block() as block:
        @block.sync
        def _(sp):
            for g in range(NB):
                tiles = slice(TPB * g, TPB * (g + 1))
                sp.dma_start(x[:, tiles, :], a["x"].rearrange("(t p) c -> p t c", p=P)[:, tiles, :]).then_inc(s_x[g], 16)
            sp.dma_start(ident[:, :], a["ident"]).then_inc(s_w, 16)
            sp.dma_start(wqk[:, :, :], a["wqk"].rearrange("n c f -> c n f")).then_inc(s_w, 16)
            sp.dma_start(wv[:, :], a["wv"]).then_inc(s_w, 16)
            sp.dma_start(rope[:, :, :], a["rope"].rearrange("n r s -> r n s")).then_inc(s_rope, 16)
            for dst, name in ((wo, "wo"), (identb, "identb"), (mask_q, "mask_q"), (mask_k, "mask_k"), (pick, "pick")):
                sp.dma_start(dst[:, :], a[name]).then_inc(s_const, 16)
            parts_to_dram(sp, 0)
            sp.wait_ge(s_zero, ZEROS)
            for par in range(2):
                at = HALF * par + SPLIT
                sp.dma_start(ks[at:at + 2, par, :, :, :, :].rearrange("r h n b s -> r (h n b s)"), a["ones"]).then_inc(s_ones, 16)
            dram_to_stacks(sp, 0)
            sp.wait_ge(s_ones, 32)

        @block.gpsimd
        def _(pool):
            pool.memset(nil[:, :], 0.0).then_inc(s_nil, 1)
            pool.memset(half[:, :], -0.5).then_inc(s_half, 1)
            pool.memset(v[:, :, :, DH:DH + 1], 1.0).then_inc(s_vset, 1)
            pool.wait_ge(s_half, 1)
            for piece in pieces[by_act:by_act + 3]:
                pool.memset(piece, 0.0).then_inc(s_zero, 1)
            mine = pieces[by_act + 3:]
            for g in range(NB):
                tiles = slice(TPB * g, TPB * (g + 1))
                pool.wait_ge(s_dstat, TPB * (g + 1))
                pool.tensor_scalar(rstd[:, tiles], mv[:, tiles, 1], 1e-5, None, ALU.add).then_inc(s_pool, 1)
                pool.wait_ge(s_pool, g + 1)
                pool.tensor_tensor(rstd[:, tiles], rstd[:, tiles], half[:, 0:TPB], ALU.pow).then_inc(s_rstd, 1)
            before = 4
            for piece in mine[:before]:
                pool.memset(piece, 0.0).then_inc(s_zero, 1)
            for n in range(2 * NB):
                pool.wait_ge(s_prod, 2 * n + 2)
                if n >= 2:
                    pool.wait_ge(s_rest, n - 1)
                pool.tensor_tensor(full[:, n % 2, :], prod[:, n % 2, 0, :], prod[:, n % 2, 1, :],
                                   ALU.add).then_inc(s_full, 1)
                for piece in mine[before + 2 * n:before + 2 * n + 2]:
                    pool.memset(piece, 0.0).then_inc(s_zero, 1)

        @block.vector
        def _(dve):
            def stats(g):
                dve.wait_ge(s_x[g], 16)
                for t in range(TPB * g, TPB * (g + 1)):
                    dve.bn_stats(stat[:, t, :], x[:, t, :]).then_inc(s_dve, 1)
                for t in range(TPB * g, TPB * (g + 1)):
                    dve.wait_ge(s_dve, t + 1)
                    dve.bn_aggr(mv[:, t, :], stat[:, t, :]).then_inc(s_dstat, 1)

            stats(0)
            for g in range(NB):
                if g + 1 < NB:
                    stats(g + 1)
                dve.wait_ge(s_rstd, g + 1)
                for t in range(TPB * g, TPB * (g + 1)):
                    dve.tensor_scalar(xn[:, t, :], x[:, t, :], mv[:, t, 0:1], rstd[:, t:t + 1],
                                      ALU.subtract, ALU.mult).then_inc(s_xn, 1)
            dve.wait_ge(s_rope, 16)

            def products(n):
                b, i = divmod(n, 2)
                dve.wait_ge(s_proj, 2 * n + 2)
                if n >= 2:
                    dve.wait_ge(s_full, n - 1)
                for k in range(2):
                    dve.tensor_tensor(prod[:, i, k, :], ps[:, 2 + 2 * i + k, :], rope[:, k, b * BLK:(b + 1) * BLK],
                                      ALU.mult).then_inc(s_prod, 1)

            def take_high(n):
                b, i = divmod(n, 2)
                dve.wait_ge(s_high, n + 1)
                if n >= 2:
                    dve.wait_ge(s_low, n - 1)
                dve.tensor_tensor(rest[:, i, :], full[:, i, :], part[:, b % 2, i, 0, :],
                                  ALU.subtract).then_inc(s_rest, 1)

            def take_middle(n):
                b, i = divmod(n, 2)
                dve.wait_ge(s_rest, n + 1)
                dve.wait_ge(s_mid, n + 1)
                dve.tensor_tensor(part[:, b % 2, i, 2, :], rest[:, i, :], part[:, b % 2, i, 1, :],
                                  ALU.subtract).then_inc(s_low, 1)

            for n in range(2 * NB + 2):
                if n < 2 * NB:
                    products(n)
                if 0 <= n - 2 < 2 * NB:
                    take_middle(n - 2)
                if 0 <= n - 1 < 2 * NB:
                    take_high(n - 1)

        @block.scalar
        def _(act):
            def copy_turned(b):
                act.wait_ge(s_xt, TPB * (b + 1))
                act.activation(xT[:, b * BLK:(b + 1) * BLK], ps[:, b % 2, :], ACT.Copy).then_inc(s_xtc, 1)

            act.wait_ge(s_nil, 1)
            act.activation(v[:, :, :, DH + 1:VW], nil[:, :].unsqueeze(2).unsqueeze(3)
                           .to_broadcast([P, T, H, VW - DH - 1]), ACT.Copy).then_inc(s_vset, 1)
            copy_turned(0)
            copy_turned(1)
            for b in range(NB):
                act.wait_ge(s_v, b + 1)
                act.wait_ge(s_vset, 2)
                act.activation(v[:, TPB * b:TPB * (b + 1), :, 0:DH],
                               ps[:, 6, :].rearrange("p (t h d) -> p t h d", t=TPB, h=H), ACT.Copy).then_inc(s_vc, 1)
                if b == 0:
                    for piece in pieces[:by_act]:
                        act.activation(piece, nil[:, :].to_broadcast([P, PIECE]), ACT.Copy).then_inc(s_zero, 1)
                for i in range(2):
                    n = 2 * b + i
                    act.wait_ge(s_full, n + 1)
                    if b >= 2:
                        act.wait_ge(s_spread[b - 2], 16)
                    act.activation(part[:, b % 2, i, 0, :], full[:, i, :], ACT.Copy).then_inc(s_high, 1)
                    if i == 0 and b + 2 < NB:
                        copy_turned(b + 2)
                    act.wait_ge(s_rest, n + 1)
                    act.activation(part[:, b % 2, i, 1, :], rest[:, i, :], ACT.Copy).then_inc(s_mid, 1)

        @block.tensor
        def _(pe):
            pe.wait_ge(s_w, 48)

            def turn(b):
                if b >= 2:
                    pe.wait_ge(s_xtc, b - 1)
                for j in range(TPB):
                    t = TPB * b + j
                    pe.wait_ge(s_xn, t + 1)
                    pe.transpose(ps[:, b % 2, j * P:(j + 1) * P], xn[:, t, :], ident[:, :]).then_inc(s_xt, 1)

            def project(b):
                pe.wait_ge(s_xtc, b + 1)
                if b >= 1:
                    pe.wait_ge(s_vc, b)
                for j in range(TPB):
                    t = TPB * b + j
                    mm = pe.matmul(ps[:, 6, j * P:(j + 1) * P], xT[:, t * P:(t + 1) * P], wv[:, :],
                                   start=True, stop=True)
                mm.then_inc(s_v, 1)
                for i in range(2):
                    if b >= 1:
                        pe.wait_ge(s_prod, 4 * (b - 1) + 2 * i + 2)
                    for k in range(2):
                        pe.matmul(ps[:, 2 + 2 * i + k, :], wqk[:, 2 * i + k, :], xT[:, b * BLK:(b + 1) * BLK],
                                  start=True, stop=True).then_inc(s_proj, 1)

            turn(0)
            turn(1)
            for b in range(NB):
                project(b)
                if b + 2 < NB:
                    turn(b + 2)

    OB, SM, RING = 4, 5, 3
    scale = float(DH) ** -0.5
    s_sm, s_smr = sem("max_scores"), sem("max_taken")
    s_mneg, s_mh = sem("row_max"), sem("max_high")
    s_mrow = [sem(f"max_rows_in{i}") for i in range(2)]
    s_st, s_e, s_av, s_oc = sem("scores"), sem("exps"), sem("values"), sem("out_copied")

    units, step_at = [], []
    for q, g in CHUNKS:
        units.append(max_units(q, g))
        step_at.append(step_at[-1] + TPB * (CHUNKS[len(step_at) - 1][0] + 1) if step_at else 0)

    def n_steps(k):
        return TPB * (CHUNKS[k][0] + 1) if k >= 0 else 1

    def width(unit):
        t, pair, c, par = unit
        return min(BLK, P * (t + 1) - BLK * c)

    START = 64
    plan = {}
    for k in range(-2, NC - 2):
        q = CHUNKS[k][0] if k >= 0 else 0
        steps = [START + BLK - max(0, kt - TPB * q) * P for kt in range(n_steps(k)) for third in range(3)]
        plan[k] = share([START + width(unit) for unit in units[k + 2]], steps)

    def beside(k, i, third):
        return plan[k][3 * i + third] if k in plan and i < n_steps(k) else []

    slot, turn_slot = {}, {}
    for k in range(-2, NC):
        if k == -1:
            turn_slot[0] = len(slot)
        for i in range(n_steps(k) + 1):
            for third in range(3):
                for n in beside(k, i, third):
                    slot[k + 2, n] = len(slot) + len(turn_slot)
            if i == 0 and 0 < k + 1 < NC:
                turn_slot[k + 1] = len(slot) + len(turn_slot)

    with nc.Block() as block:
        @block.tensor
        def _(pe):
            def max_scores(k, n_unit):
                t, pair, c, par = units[k][n_unit]
                n = slot[k, n_unit]
                keys = width(units[k][n_unit])
                if n >= RING:
                    pe.wait_ge(s_smr, n - RING + 1)
                last = c == t // TPB
                dst = ps[:, SM + n % RING, :]
                mm = pe.matmul(dst[:, 0:keys], qs[:, t // TPB // 2, pair, t // TPB % 2, t % TPB * P:(t % TPB + 1) * P],
                               ks[:, par, c // 2, pair, c % 2, 0:keys], start=True, stop=not last)
                if last:
                    mm = pe.matmul(dst[:, keys - P:keys], identb[:, :], mask_q[:, :], start=False, stop=True)
                mm.then_inc(s_sm, 1)

            def scores(k, kt, pr):
                q, g = CHUNKS[k]
                n = 2 * (step_at[k] + kt) + pr
                off = max(0, kt - TPB * q) * P
                pair = 2 * g + pr
                if n >= 2:
                    pe.wait_ge(s_e, n - 1)
                diag = kt >= TPB * q
                for par in range(2):
                    dst = ps[:, 2 * (n % 2) + par, 0:BLK - off]
                    mm = pe.matmul(dst, ks[:, par, kt // TPB // 2, pair, kt // TPB % 2, kt % TPB * P:(kt % TPB + 1) * P],
                                   qs[:, q // 2, pair, q % 2, off:BLK], start=True, stop=not diag)
                if diag:
                    for par in range(2):
                        mm = pe.matmul(ps[:, 2 * (n % 2) + par, 0:P], identb[:, :], mask_k[:, :],
                                       start=False, stop=True)
                mm.then_inc(s_st, 1)

            def values(k, kt):
                q, g = CHUNKS[k]
                n = step_at[k] + kt
                off = max(0, kt - TPB * q) * P
                pe.wait_ge(s_e, 2 * n + 2)
                if kt == 0 and k >= 1:
                    pe.wait_ge(s_oc, k)
                for j in range(4):
                    mm = pe.matmul(ps[VW * j:VW * (j + 1), OB, off:BLK], v[:, kt, 4 * g + j, :],
                                   probs[:, n % 2, j // 2, j % 2, 0:BLK - off],
                                   start=kt == 0, stop=kt == TPB * (q + 1) - 1)
                mm.then_inc(s_av, 1)

            def turn_max(k):
                n = turn_slot[k]
                pe.wait_ge(s_mneg, TPB * (k + 1))
                if n >= RING:
                    pe.wait_ge(s_smr, n - RING + 1)
                for j in range(TPB):
                    mm = pe.transpose(ps[0:4, SM + n % RING, j * P:(j + 1) * P], mneg[:, k % 2, j, :], ident[:, :])
                mm.then_inc(s_sm, 1)

            late = min(k for k in range(NC) if CHUNKS[k][0] >= NB // 2) - 2
            pe.wait_ge(s_const, 16 * 5)
            pe.wait_ge(s_stack[0], 16 * 12)
            for k in range(-2, NC):
                if k == late:
                    pe.wait_ge(s_stack[1], 16 * 12)
                if k >= 0:
                    pe.wait_ge(s_mrow[k % 2], 64 * (k // 2 + 1))
                if k == -1:
                    turn_max(0)
                for i in range(n_steps(k) + 1):
                    for third in range(3):
                        if k >= 0 and third < 2 and i < n_steps(k):
                            scores(k, i, third)
                        if k >= 0 and third == 2 and i >= 1:
                            values(k, i - 1)
                        for n in beside(k, i, third):
                            max_scores(k + 2, n)
                    if i == 0 and 0 < k + 1 < NC:
                        turn_max(k + 1)

        @block.scalar
        def _(act):
            for k, (q, g) in enumerate(CHUNKS):
                for kt in range(n_steps(k)):
                    off = max(0, kt - TPB * q) * P
                    for pr in range(2):
                        n = 2 * (step_at[k] + kt) + pr
                        act.wait_ge(s_st, n + 1)
                        if n >= 4:
                            act.wait_ge(s_av, n // 2 - 1)
                        act.activation(probs[:, n // 2 % 2, pr, :, 0:BLK - off],
                                       ps[:, 2 * (n % 2):2 * (n % 2) + 2, 0:BLK - off], ACT.Exp,
                                       scale=scale).then_inc(s_e, 1)

        @block.vector
        def _(dve):
            def take_max(k, n):
                t, pair, c, par = units[k][n]
                keys = width(units[k][n])
                dve.wait_ge(s_sm, slot[k, n] + 1)
                at = 2 * par + pair % 2
                dve.tensor_reduce(mpart[:, t % TPB, at, c:c + 1], ps[:, SM + slot[k, n] % RING, 0:keys], X_AXIS,
                                  ALU.max).then_inc(s_smr, 1)
                if n + 1 == len(units[k]) or units[k][n + 1][0] != t:
                    dve.wait_ge(s_smr, slot[k, n] + 1)
                    if k >= 2:
                        dve.wait_ge(s_sm, turn_slot[k - 2] + 1)
                    dve.tensor_reduce(mneg[:, k % 2, t % TPB, :], mpart[:, t % TPB, :, 0:t // TPB + 1], X_AXIS,
                                      ALU.max, negate=True).then_inc(s_mneg, 1)

            def copy_out(k):
                q, g = CHUNKS[k]
                dve.wait_ge(s_av, step_at[k] + n_steps(k))
                dve.tensor_copy(outT[:, g, q * BLK:(q + 1) * BLK], ps[:, OB, :]).then_inc(s_oc, 1)

            def split_max(k):
                n = turn_slot[k]
                dve.wait_ge(s_sm, n + 1)
                turned = ps[0:4, SM + n % RING, :]
                if k >= 1:
                    dve.wait_ge(s_mrow[(k - 1) % 2], 64 * ((k - 1) // 2 + 1))
                dve.tensor_copy(mrow[:, 0, :], turned).then_inc(s_mh, 1)
                dve.wait_ge(s_mh, k + 1)
                dve.tensor_tensor(mrow[:, 1, :], turned, mrow[:, 0, :], ALU.subtract).then_inc(s_smr, 1)

            for k in range(-2, NC):
                if k == -1:
                    split_max(0)
                for i in range(n_steps(k) + 1):
                    for third in range(3):
                        for n in beside(k, i, third):
                            take_max(k + 2, n)
                    if i == 0 and 0 < k + 1 < NC:
                        split_max(k + 1)
                if k >= 0:
                    copy_out(k)

        @block.sync
        def _(sp):
            parts_to_dram(sp, 1)
            dram_to_stacks(sp, 1)
            for k, (q, g) in enumerate(CHUNKS):
                sp.wait_ge(s_smr, turn_slot[k] + 1)
                for w in range(2):
                    for par in range(2):
                        at = HALF * par + SPLIT + w
                        sp.dma_start(qs[at:at + 1, q // 2, 2 * g:2 * g + 2, q % 2, :],
                                     mrow[2 * par:2 * par + 2, w, :]).then_inc(s_mrow[k % 2], 16)
            for k in (NC - 2, NC - 1):
                sp.wait_ge(s_mrow[k % 2], 64 * (k // 2 + 1))


def layers(nc, ctx, a, keep, out):
    def sb(name, shape, dt=F32):
        return ctx.enter_context(nc.sbuf_tensor(name, shape, dt))

    def sem(name):
        return ctx.enter_context(nc.semaphore(name))

    w = {
        "xs": sb("xs", [P, T, D]),
        "xa": sb("xa", [P, T, D]),
        "hT": sb("h_t", [P, WIN + S]),
        "wqkv": sb("wqkv", [P, LAYERS, 3 * INNER]),
        "wo": sb("wo_l", [P, LAYERS, INNER // P, D]),
        "w1": sb("w1", [P, LAYERS, 2 * HID]),
        "w2": sb("w2", [P, LAYERS, len(HCH), D]),
        "gb": sb("ln_gb", [P, LAYERS, 2]),
        "b1": sb("b1", [P, LAYERS, 2, len(HCH)]),
        "b2": sb("b2", [P, LAYERS, D]),
        "tab": sb("xpos_tab", [P, 2, T, 2, LD]),
        "qks": sb("qk_scale", [P, LAYERS, 2, LD]),
        "kT": sb("k_t", [P, INNER // P, WIN + S]),
        "qpad": sb("q_padded", [P, 2, 2, INNER // P, P]),
        "v": sb("v_l", [P, T + 1, LH, LD + 1]),
        "mask": sb("mask_l", [P, 2, KEYS], BF16),
        "shift": sb("shift", [P, 2, P]),
        "work": keep["early"][:, :, :].rearrange("p n s -> p (n s)")[:, 0:7 * 1024],
    }
    outT, wo, pick, ps, ident = (keep[n] for n in ("early", "wo", "pick", "ps", "ident"))
    rden = sb("rden", [P, 2, H])
    on = sb("o_norm", [P, 2, D])
    onT = sb("o_norm_t", [P, 2, P])
    xs, tab, qks = w["xs"], w["tab"], w["qks"]
    x, mv, rstd, stat, half = keep["x"], keep["mv"], keep["rstd"], keep["stat"], keep["half"]
    s_lw, s_tab, s_zero, s_scaled = sem("layer_weights"), sem("tables_in"), sem("pads_zeroed"), sem("tables_scaled")
    s_dve, s_stat, s_pool, s_rstd, s_xs = (sem(n) for n in (
        "l_dve_chain", "l_stats", "l_pool_chain", "l_rstd", "l_xs"))

    s_pick, s_rd, s_on, s_ont, s_ontc, s_y, s_yadd = (sem(n) for n in (
        "picked", "rden_done", "o_normed", "o_turned", "o_turned_copied", "o_projected", "o_added"))
    def close_tensor(pe):
        def gather(t):
            if t >= 2:
                pe.wait_ge(s_on, t - 1)
            for g in range(GROUPS):
                mm = pe.matmul(ps[:, t % 2, 36 * g:36 * (g + 1)], outT[:, g, t * P:(t + 1) * P], pick[:, :],
                               start=True, stop=True)
            mm.then_inc(s_pick, 1)

        def turn(t):
            pe.wait_ge(s_on, t + 1)
            if t >= 2:
                pe.wait_ge(s_ontc, t - 1)
            pe.transpose(ps[:, 2 + t % 2, 0:P], on[:, t % 2, :], ident[:, :]).then_inc(s_ont, 1)

        def project(t):
            pe.wait_ge(s_ontc, t + 1)
            if t >= 2:
                pe.wait_ge(s_yadd, t - 1)
            pe.matmul(ps[:, 4 + t % 2, 0:D], onT[:, t % 2, :], wo[:, :],
                      start=True, stop=True).then_inc(s_y, 1)

        for i in range(T + 2):
            if i < T:
                gather(i)
            if 0 <= i - 1 < T:
                turn(i - 1)
            if 0 <= i - 2 < T:
                project(i - 2)

    def close_scalar(act):
        for t in range(T):
            act.wait_ge(s_ont, t + 1)
            if t >= 2:
                act.wait_ge(s_y, t - 1)
            act.activation(onT[:, t % 2, :], ps[:, 2 + t % 2, 0:P],
                           ACT.Copy).then_inc(s_ontc, 1)

    def close_sync(sp):
        for i, n in enumerate(("q_scale", "k_scale")):
            sp.dma_start(qks[:, :, i, :], a[n].unsqueeze(0).to_broadcast([P, LAYERS, LD])).then_inc(s_tab, 16)
        for i in range(2):
            sp.dma_start(tab[:, i, :, :, :], a["xpos"][i]).then_inc(s_tab, 16)
        for dst, src in (
            (w["wqkv"][:, :, :], a["wqkv"].rearrange("l c f -> c l f")),
            (w["w1"][:, :, :], a["w1"].rearrange("l c f -> c l f")),
            (w["mask"][:, :, :], a["mask_l"]),
            (w["shift"][:, :, :], a["shift"]),
            (w["b2"][:, :, :], a["b2"].unsqueeze(0).to_broadcast([P, LAYERS, D])),
            (w["gb"][:, :, :], a["ln_gb"]),
            (w["b1"][:, :, :, :], a["b1"]),
        ):
            sp.dma_start(dst, src).then_inc(s_lw, 16)
        for layer in range(LAYERS):
            sp.dma_start(w["wo"][:, layer, :, :], a["lwo"][layer].rearrange("(c p) n -> p c n", p=P)).then_inc(s_lw, 16)
            for c, rows in enumerate(HCH):
                at = c * P
                sp.dma_start(w["w2"][0:rows, layer, c, :], a["w2"][layer, at:at + rows, :]).then_inc(s_lw, 16)
        sp.wait_ge(s_lw, 16 * (7 + LAYERS * (1 + len(HCH))))

    def close_gpsimd(pool):
        pool.memset(w["hT"][:, 0:WIN + 1], 0.0).then_inc(s_zero, 1)
        pool.memset(w["kT"][:, :, 0:WIN], 0.0).then_inc(s_zero, 1)
        for par in range(2):
            pool.wait_ge(s_zero, 2 + par)
            pool.memset(w["qpad"][HALF * (1 - par):HALF * (2 - par), par, :, :, :], 0.0).then_inc(s_zero, 1)
        pool.wait_ge(s_zero, 4)
        pool.memset(w["v"][:, :, :, LD:LD + 1], 1.0).then_inc(s_zero, 1)
        pool.wait_ge(s_tab, 16 * 4)
        for b in range(NB):
            if b % 2 == 0:
                scale_table(pool, w, 0, b // 2).then_inc(s_scaled, 1)
            tiles = slice(TPB * b, TPB * (b + 1))
            pool.wait_ge(s_stat, TPB * (b + 1))
            pool.tensor_scalar(rstd[:, tiles], mv[:, tiles, 1], 1e-5, None, ALU.add).then_inc(s_pool, 1)
            pool.wait_ge(s_pool, b + 1)
            pool.tensor_tensor(rstd[:, tiles], rstd[:, tiles], half[:, 0:TPB], ALU.pow).then_inc(s_rstd, 1)
        pool.wait_ge(s_zero, 5)
        pool.wait_ge(s_scaled, 2)

    def close_vector(dve):
        def norm(t):
            dve.wait_ge(s_pick, t + 1)
            got = ps[:, t % 2, 0:H * 9].rearrange("p (h d) -> p h d", d=9)
            dve.reciprocal(rden[:, t % 2, :], got[:, :, DH]).then_inc(s_rd, 1)
            dve.wait_ge(s_rd, t + 1)
            if t >= 2:
                dve.wait_ge(s_ont, t - 1)
            dve.tensor_tensor(on[:, t % 2, :].rearrange("p (h d) -> p h d", d=DH), got[:, :, 0:DH],
                              rden[:, t % 2, :].unsqueeze(2).to_broadcast([P, H, DH]), ALU.mult).then_inc(s_on, 1)

        def add(t):
            dve.wait_ge(s_y, t + 1)
            dve.tensor_tensor(x[:, t, :], x[:, t, :], ps[:, 4 + t % 2, 0:D], ALU.add).then_inc(s_yadd, 1)

        def stats(t):
            dve.wait_ge(s_yadd, t + 1)
            dve.bn_stats(stat[:, t, :], x[:, t, :]).then_inc(s_dve, 1)

        def mean_var(t):
            dve.wait_ge(s_dve, t + 1)
            dve.bn_aggr(mv[:, t, :], stat[:, t, :]).then_inc(s_stat, 1)

        def layer_norm(t):
            dve.wait_ge(s_rstd, t // TPB + 1)
            dve.tensor_scalar(xs[:, t, :], x[:, t, :], mv[:, t, 0:1], rstd[:, t:t + 1],
                              ALU.subtract, ALU.mult).then_inc(s_xs, 1)

        for i in range(T + 12):
            if i < T:
                norm(i)
            for lag, step in ((3, add), (4, stats), (5, mean_var), (12, layer_norm)):
                if 0 <= i - lag < T:
                    step(i - lag)
        dve.wait_ge(s_xs, T)

    close = {"tensor": close_tensor, "scalar": close_scalar, "sync": close_sync, "gpsimd": close_gpsimd,
             "vector": close_vector, "loaded": s_lw, "zeroed": s_zero, "scaled": s_scaled, "xs": s_xs, "picked": s_pick,
             "divided": s_on, "added": s_yadd}
    for layer in range(LAYERS):
        with ExitStack() as part:
            run_layer(nc, part, a, keep, w, layer, out, close if layer == 0 else None)


def scale_table(pool, w, layer, i):
    t4 = w["tab"][:, i, :, :, :]
    return pool.tensor_tensor(t4, t4, w["qks"][:, layer, :, :].unsqueeze(1).to_broadcast([P, T, 2, LD]), ALU.mult)


def run_layer(nc, ctx, a, keep, w, layer, out, close):
    def sem(name):
        return ctx.enter_context(nc.semaphore(f"{name}_{layer}"))

    def sb(name, shape):
        return ctx.enter_context(nc.sbuf_tensor(f"{name}_l{layer}", shape, F32))

    ps, ident, half = keep["ps"], keep["ident"], keep["half"]
    xs, xa, hT, kT, v, mask = w["xs"], w["xa"], w["hT"], w["kT"], w["v"], w["mask"]
    straight, exchanged = w["tab"][:, 0], w["tab"][:, 1]
    NH = 2 * LH
    HH = LH // 2
    U = 2 * T
    LAG = 3
    lanes = w["work"][:, :].rearrange("p (n f) -> p n f", n=7)
    sq, hat, turned, plain = lanes[:, 0, :], lanes[:, 1:3, :], lanes[:, 3:5, :], lanes[:, 5:7, :]
    norm = sb("norms", [P, 2, 2, NH])
    sub = sb("masked", [P, 2, HH, KEYS])
    pa = sb("probs_a", [P, 2, HH, P])
    pb = sb("probs_b", [WIN, 2, HH, WIN])
    o = sb("out", [P, 2, INNER])
    oT = sb("out_t", [P, INNER])
    nmax = sb("nmax", [P, 2, HH])
    rden = sb("rden", [P, 2, HH])
    qpad = w["qpad"]
    QK, VB, SC, PA, PB, OB = 0, 2, 3, 5, 6, 7
    s_tx, s_h, s_qk, s_v, s_vc, s_sq, s_ss, s_clip, s_inv, s_hat, s_turned, s_plain, s_sum, s_t, s_tc = (
        sem(n) for n in ("x_turned", "h_ready", "qk_ready", "v_ready", "v_copied", "squares", "square_sums", "clipped",
                         "inverse_norms", "normalised", "exchanged_part", "straight_part", "rotated", "qk_turned",
                         "qk_copied"))
    s_s, s_nm, s_sub, s_e, s_pa, s_pb, s_pac, s_pbc, s_av, s_rd, s_o, s_ot, s_otc, s_y, s_xa = (
        sem(n) for n in ("w_scores", "w_max", "w_masked", "w_exp", "w_turned_a", "w_turned_b", "w_copied_a",
                         "w_copied_b", "w_values", "w_rden", "w_out", "w_out_turned", "w_out_copied", "w_projected",
                         "w_added"))
    s_tab, s_scaled = sem("w_tables_in"), sem("w_tables_scaled")

    def x_bank(b):
        return PB if b == 0 else VB

    def qk_bank(t):
        return SC if t == 1 else QK

    def heads(ap):
        return ap.rearrange("p (i h d) -> p i h d", i=2, d=LD)

    shift, x, rstd, mv = w["shift"], keep["x"], keep["rstd"], keep["mv"]
    stat = ctx.enter_context(nc.sbuf_tensor(f"stat_{layer}", [P, TPB, 2, 6], F32))
    work = w["work"]
    hn = work[:, 0:TPB * D].rearrange("p (t c) -> p t c", t=TPB)
    hnT = work[:, 512:512 + 2 * BLK].rearrange("p (b s) -> p b s", b=2)
    gate = work[:, 1536:1536 + 2 * BLK].rearrange("p (b s) -> p b s", b=2)
    hid = work[:, 2560:2560 + 2 * 3 * BLK].rearrange("p (b c s) -> p b c s", b=2, c=3)
    res = work[:, 5632:5632 + 2 * TPB * D].rearrange("p (b t c) -> p b t c", b=2, t=TPB)
    SH, HB, HID_BANK, YB = 0, 1, 2, 6
    last = layer == LAYERS - 1
    C = len(HCH)
    s_sh, s_st, s_mv, s_eps, s_rs, s_hn, s_ht, s_htc, s_ag, s_gate, s_hid, s_down, s_x = (
        sem(n) for n in ("f_shifted", "f_stats", "f_mean_var", "f_eps", "f_rstd", "f_normed", "f_turned", "f_copied",
                         "f_hidden", "f_gate", "f_product", "f_out", "f_added"))
    s_store, s_res, s_bias = sem("stored"), sem("f_residual"), sem("f_bias_in")

    ROUNDS = T + LAG + 2

    with nc.Block() as block:
        if last:
            @block.sync
            def _(sp):
                for b in range(NB):
                    sp.wait_ge(s_x, b + 1)
                    sp.dma_start(out[b * BLK:(b + 1) * BLK, :].rearrange("(t p) c -> p t c", p=P),
                                 x[:, TPB * b:TPB * (b + 1), :]).then_inc(s_store, 16)
                sp.wait_ge(s_store, 16 * NB)
        else:
            @block.sync
            def _(sp):
                if close:
                    close["sync"](sp)
                sp.wait_ge(s_plain, T)
                sp.wait_ge(s_turned, 2 * T)
                for i in range(2):
                    sp.dma_start(w["tab"][:, i, :, :, :], a["xpos"][i]).then_inc(s_tab, 16)

        @block.tensor
        def _(pe):
            if close:
                close["tensor"](pe)

            def turn_x(b):
                if b >= 1:
                    pe.wait_ge(s_vc, TPB * (b - 1) + 2)
                if close:
                    pe.wait_ge(close["xs"], TPB * (b + 1))
                for j in range(TPB):
                    mm = pe.transpose(ps[:, x_bank(b), j * P:(j + 1) * P], xs[:, TPB * b + j, :], ident[:, :])
                mm.then_inc(s_tx, 1)

            def project(t):
                pe.wait_ge(s_h, 2 * (t // TPB + 1))
                if t >= 2:
                    read = t if t >= 3 else 1
                    pe.wait_ge(s_hat, read)
                    pe.wait_ge(s_sq, read)
                at = WIN + t * P
                for i in range(2):
                    mm = pe.matmul(ps[:, qk_bank(t) + i, :], hT[:, at:at + P],
                                   w["wqkv"][:, layer, i * INNER:(i + 1) * INNER], start=True, stop=True)
                mm.then_inc(s_qk, 1)

            def turn(t, i):
                if i == 0:
                    pe.wait_ge(s_sum, t + 1)
                    pe.wait_ge(s_vc, min(t + 2, T + 1))
                    if t % TPB == 0 and t // TPB + 1 < NB:
                        pe.wait_ge(s_h, 2 * (t // TPB + 2))
                    if t == T - 1:
                        pe.wait_ge(s_tc, 3 * t)
                else:
                    pe.wait_ge(s_tc, 3 * t + 2)
                for n in range(INNER // P):
                    mm = pe.transpose(ps[:, VB, n * P:(n + 1) * P],
                                      hat[:, t % 2, i * INNER + n * P:i * INNER + (n + 1) * P], ident[:, :])
                mm.then_inc(s_t, 1)

            def project_values(t):
                rows = P if t < T else WIN
                pe.wait_ge(s_h, 2 * min(t // TPB + 1, NB))
                if t >= 1:
                    pe.wait_ge(s_vc, t)
                if t >= 2:
                    pe.wait_ge(s_tc, 3 * (t - 1))
                pe.matmul(ps[0:rows, VB, :], hT[:, t * P:t * P + rows], w["wqkv"][:, layer, 2 * INNER:3 * INNER],
                          start=True, stop=True).then_inc(s_v, 1)

            def scores(u):
                t, par = divmod(u, 2)
                if u >= 1:
                    pe.wait_ge(s_sub, u)
                else:
                    pe.wait_ge(s_hat, 2)
                    pe.wait_ge(s_sq, 2)
                pe.wait_ge(s_tc, 3 * (t + 1))
                for b in range(2):
                    bank = ps[:, SC + b, 0:2 * KEYS].rearrange("p (h k) -> p h k", h=2)
                    for j in range(2):
                        n = 2 * b + j
                        mm = pe.matmul(bank[:, j, :], qpad[:, par, t % 2, n, :], kT[:, n, t * P:t * P + KEYS],
                                       start=True, stop=True)
                mm.then_inc(s_s, 1)

            def turn_probs(u):
                t, par = divmod(u, 2)
                pe.wait_ge(s_e, HH * (u + 1))
                if u >= 1:
                    pe.wait_ge(s_pac, u)
                if par == 0 and t >= 2:
                    pe.wait_ge(s_otc, t - 1)
                elif par == 0 and t == 1:
                    pe.wait_ge(s_pbc, u)
                elif par == 1 and t >= 2:
                    pe.wait_ge(s_xa, t - 1)
                elif par == 1:
                    pe.wait_ge(s_pbc, u)
                for n in range(HH):
                    mm = pe.transpose(ps[0:WIN, PB, n * WIN:(n + 1) * WIN], sub[WIN:P, u % 2, n, P:KEYS],
                                      ident[WIN:P, WIN:P])
                mm.then_inc(s_pb, 1)
                for n in range(HH):
                    mm = pe.transpose(ps[:, PA, n * P:(n + 1) * P], sub[:, u % 2, n, 0:P], ident[:, :])
                mm.then_inc(s_pa, 1)

            def values(u):
                t, par = divmod(u, 2)
                pe.wait_ge(s_pac, u + 1)
                pe.wait_ge(s_pbc, u + 1)
                pe.wait_ge(s_vc, t + 2)
                if u >= 1:
                    pe.wait_ge(s_o, u)
                for n in range(HH):
                    cols = slice(n * (LD + 1), (n + 1) * (LD + 1))
                    pe.matmul(ps[:, OB, cols], pa[:, u % 2, n, :], v[:, t, 2 * n + par, :],
                              start=True, stop=False, skip_group_check=True)
                    mm = pe.matmul(ps[WIN:P, OB, cols], pb[:, u % 2, n, :], v[0:WIN, t + 1, 2 * n + par, :],
                                   start=False, stop=True, skip_group_check=True)
                mm.then_inc(s_av, 1)

            def turn_out(t):
                pe.wait_ge(s_o, 2 * t + 2)
                pe.wait_ge(s_pbc, min(2 * t + 4, U))
                if t >= 1:
                    pe.wait_ge(s_xa, t)
                for c in range(INNER // P):
                    mm = pe.transpose(ps[:, PB, c * P:(c + 1) * P], o[:, t % 2, c * P:(c + 1) * P], ident[:, :])
                mm.then_inc(s_ot, 1)

            def project_out(t):
                pe.wait_ge(s_otc, t + 1)
                pe.wait_ge(s_pbc, min(2 * t + 5, U))
                for c in range(INNER // P):
                    mm = pe.matmul(ps[:, PB, 0:D], oT[:, c * P:(c + 1) * P], w["wo"][:, layer, c, :],
                                   start=c == 0, stop=c == INNER // P - 1)
                mm.then_inc(s_y, 1)

            def shift_tokens(b):
                pe.wait_ge(s_xa, TPB * (b + 1))
                if b >= 1:
                    pe.wait_ge(s_hn, 2 * TPB * b)
                else:
                    pe.wait_ge(s_hat, T)
                    pe.wait_ge(s_sq, T)
                for j in range(TPB):
                    t = TPB * b + j
                    dst = ps[:, SH, j * D // 2:(j + 1) * D // 2]
                    mm = pe.matmul(dst, shift[:, 0, :], xa[:, t, D // 2:D], start=True, stop=t == 0)
                    if t >= 1:
                        mm = pe.matmul(dst, shift[:, 1, :], xa[:, t - 1, D // 2:D], start=False, stop=True)
                mm.then_inc(s_sh, 1)

            def turn_normed(b):
                pe.wait_ge(s_hn, 2 * TPB * (b + 1))
                if b >= 1:
                    pe.wait_ge(s_htc, b)
                for j in range(TPB):
                    mm = pe.transpose(ps[:, HB, j * P:(j + 1) * P], hn[:, j, :], ident[:, :])
                mm.then_inc(s_ht, 1)

            def hidden(b, c):
                n = C * b + c
                rows = HCH[c]
                pe.wait_ge(s_htc, b + 1)
                if n == 0:
                    pe.wait_ge(s_vc, T + 1)
                    pe.wait_ge(s_tc, 3 * T)
                    pe.wait_ge(s_sub, U)
                elif n == 1:
                    pe.wait_ge(s_pac, U)
                if n >= 2:
                    pe.wait_ge(s_hid, n - 1)
                for i in range(2):
                    at = i * HID + c * P
                    mm = pe.matmul(ps[0:rows, HID_BANK + 2 * (n % 2) + i, :], w["w1"][:, layer, at:at + rows], hnT[:, b % 2, :],
                                   start=True, stop=True)
                mm.then_inc(s_ag, 1)

            def project_down(b):
                pe.wait_ge(s_hid, C * (b + 1))
                if b >= 2:
                    pe.wait_ge(s_x, b - 1)
                else:
                    pe.wait_ge(s_xa, T)
                for j in range(TPB):
                    for c, rows in enumerate(HCH):
                        mm = pe.matmul(ps[:, YB + b % 2, j * D:(j + 1) * D], hid[0:rows, b % 2, c, j * P:(j + 1) * P],
                                       w["w2"][0:rows, layer, c, :], start=c == 0, stop=c == C - 1)
                mm.then_inc(s_down, 1)

            turn_x(0)
            if close:
                pe.wait_ge(close["loaded"], 16 * (7 + LAYERS * (1 + C)))
                pe.wait_ge(close["zeroed"], 5)
                pe.wait_ge(close["divided"], T)
                pe.wait_ge(close["added"], T)
            for i in range(ROUNDS):
                u = 2 * (i - LAG)
                if 0 <= u < U:
                    scores(u)
                if 0 <= i - 2 < T:
                    turn(i - 2, 0)
                if i < T:
                    project(i)
                if 0 <= u - 1 < U:
                    turn_probs(u - 1)
                if 0 <= u - 2 < U:
                    values(u - 2)
                if 0 <= i - 2 < T:
                    turn(i - 2, 1)
                if 0 <= u - 4 < U:
                    turn_out(u // 2 - 2)
                if i == T + 3:
                    turn_normed(0)
                if i == T + 4:
                    hidden(0, 0)
                u += 1
                if 0 <= u < U:
                    scores(u)
                if i < T + 1:
                    project_values(i)
                if 0 <= u - 1 < U:
                    turn_probs(u - 1)
                if 0 <= u - 2 < U:
                    values(u - 2)
                if i % TPB == 1 and i // TPB + 1 < NB:
                    turn_x(i // TPB + 1)
                if 0 <= u - 5 < U:
                    project_out(u // 2 - 2)
                if i in (T + 2, T + 3):
                    shift_tokens(i - T - 2)
            for b in range(NB + 1):
                if 0 < b < NB:
                    hidden(b, 0)
                if b >= 1:
                    project_down(b - 1)
                if b < NB:
                    hidden(b, 1)
                if b + 1 < NB:
                    turn_normed(b + 1)
                if b + 2 < NB:
                    shift_tokens(b + 2)
                if b < NB:
                    hidden(b, 2)

        @block.scalar
        def _(act):
            if close:
                close["scalar"](act)

            def copy_h(b):
                act.wait_ge(s_tx, b + 1)
                at = WIN + b * BLK
                act.activation(hT[0:D // 2, at:at + BLK], ps[0:D // 2, x_bank(b), :], ACT.Copy).then_inc(s_h, 1)
                n = BLK if b < NB - 1 else BLK - 1
                act.activation(hT[D // 2:D, at + 1:at + 1 + n], ps[D // 2:D, x_bank(b), 0:n], ACT.Copy).then_inc(s_h, 1)

            def square(t):
                act.wait_ge(s_qk, t + 1)
                if t >= 1:
                    act.wait_ge(s_ss, t)
                act.activation(sq, ps[:, qk_bank(t):qk_bank(t) + 2, :].rearrange("p a b -> p (a b)"), ACT.Square).then_inc(s_sq, 1)

            def copy_values(t):
                rows = P if t < T else WIN
                act.wait_ge(s_v, t + 1)
                act.activation(v[0:rows, t, :, 0:LD], ps[0:rows, VB, :].rearrange("p (h d) -> p h d", d=LD),
                               ACT.Copy).then_inc(s_vc, 1)

            def copy_q(t):
                act.wait_ge(s_t, 2 * t + 1)
                if t >= 2:
                    act.wait_ge(s_s, 2 * (t - 1))
                for par in range(2):
                    rows = slice(HALF * par, HALF * (par + 1))
                    act.activation(qpad[rows, par, t % 2, :, :],
                                   ps[rows, VB, :].rearrange("p (n q) -> p n q", q=P), ACT.Copy).then_inc(s_tc, 1)

            def copy_k(t):
                act.wait_ge(s_t, 2 * t + 2)
                at = WIN + t * P
                act.activation(kT[:, :, at:at + P], ps[:, VB, :].rearrange("p (n q) -> p n q", q=P),
                               ACT.Copy).then_inc(s_tc, 1)

            def exp(u):
                act.wait_ge(s_nm, u + 1)
                for n in range(HH):
                    act.activation(sub[:, u % 2, n, :], sub[:, u % 2, n, :], ACT.Exp,
                                   bias=nmax[:, u % 2, n:n + 1]).then_inc(s_e, 1)

            def copy_probs(u):
                if u >= 2:
                    act.wait_ge(s_av, u - 1)
                act.wait_ge(s_pb, u + 1)
                act.activation(pb[:, u % 2].rearrange("p h q -> p (h q)"), ps[0:WIN, PB, 0:HH * WIN],
                               ACT.Copy).then_inc(s_pbc, 1)
                act.wait_ge(s_pa, u + 1)
                act.activation(pa[:, u % 2].rearrange("p h q -> p (h q)"), ps[:, PA, :], ACT.Copy).then_inc(s_pac, 1)

            def copy_out(t):
                act.wait_ge(s_ot, t + 1)
                if t >= 1:
                    act.wait_ge(s_y, t)
                act.activation(oT[:, :], ps[:, PB, :], ACT.Copy).then_inc(s_otc, 1)

            def copy_normed(b):
                act.wait_ge(s_ht, b + 1)
                if b == 0:
                    act.wait_ge(s_ss, T)
                elif b == 1:
                    act.wait_ge(s_t, 2 * T)
                if b >= 2:
                    act.wait_ge(s_ag, C * (b - 1))
                act.activation(hnT[:, b % 2, :], ps[:, HB, :], ACT.Identity, bias=w["gb"][:, layer, 1:2],
                               scale=w["gb"][:, layer, 0:1]).then_inc(s_htc, 1)

            def gelu(b, c):
                n = C * b + c
                rows = HCH[c]
                act.wait_ge(s_ag, n + 1)
                if n == 0:
                    act.wait_ge(s_t, 2 * T)
                if n >= 2:
                    act.wait_ge(s_hid, n - 1)
                act.activation(gate[0:rows, n % 2, :], ps[0:rows, HID_BANK + 2 * (n % 2) + 1, :], ACT.Gelu,
                               bias=w["b1"][0:rows, layer, 1, c:c + 1]).then_inc(s_gate, 1)

            if close:
                act.wait_ge(close["zeroed"], 5)
                act.wait_ge(close["picked"], T)
            copy_h(0)
            for i in range(ROUNDS):
                u = 2 * (i - LAG)
                if 0 <= i - 2 < T:
                    copy_q(i - 2)
                if 0 <= u - 1 < U:
                    copy_probs(u - 1)
                if i < T:
                    square(i)
                if 0 <= i - 2 < T:
                    copy_k(i - 2)
                if 0 <= u < U:
                    exp(u)
                if 0 <= u - 4 < U:
                    copy_out(u // 2 - 2)
                if i == T + 3:
                    copy_normed(0)
                u += 1
                if i < T + 1:
                    copy_values(i)
                if 0 <= u - 1 < U:
                    copy_probs(u - 1)
                if i % TPB == 1 and i // TPB + 1 < NB:
                    copy_h(i // TPB + 1)
                if 0 <= u < U:
                    exp(u)
            for b in range(NB):
                gelu(b, 0)
                gelu(b, 1)
                if b + 1 < NB:
                    copy_normed(b + 1)
                gelu(b, 2)

        @block.gpsimd
        def _(pool):
            if close:
                close["gpsimd"](pool)

            def inverse_norm(t):
                pool.wait_ge(s_ss, t + 1)
                pool.tensor_scalar(norm[:, t % 2, 0, :], norm[:, t % 2, 0, :], 1e-24, None, ALU.max).then_inc(s_clip, 1)
                pool.wait_ge(s_clip, t + 1)
                if t >= 2:
                    pool.wait_ge(s_hat, t - 1)
                pool.tensor_tensor(norm[:, t % 2, 1, :], norm[:, t % 2, 0, :], half[:, :], ALU.pow).then_inc(s_inv, 1)

            def plain_part(t):
                pool.wait_ge(s_hat, t + 1)
                if t >= 2:
                    pool.wait_ge(s_sum, t - 1)
                pool.tensor_tensor(heads(plain[:, t % 2, :]), heads(hat[:, t % 2, :]),
                                   straight[:, t].unsqueeze(2).to_broadcast([P, 2, LH, LD]), ALU.mult).then_inc(s_plain, 1)

            for t in range(T):
                inverse_norm(t)
                plain_part(t)
            if layer + 1 < LAYERS:
                pool.wait_ge(s_tab, 32)
                for i in range(2):
                    scale_table(pool, w, layer + 1, i).then_inc(s_scaled, 1)
                pool.wait_ge(s_scaled, 2)
            for b in range(NB):
                tiles = slice(TPB * b, TPB * (b + 1))
                pool.wait_ge(s_mv, TPB * (b + 1))
                pool.tensor_scalar(mv[:, tiles, 1], mv[:, tiles, 1], 1e-5, None, ALU.add).then_inc(s_eps, 1)
                pool.wait_ge(s_eps, b + 1)
                pool.tensor_tensor(rstd[:, tiles], mv[:, tiles, 1], half[:, 0:TPB], ALU.pow).then_inc(s_rs, 1)
                if b >= 2:
                    pool.wait_ge(s_x, b - 1)
                else:
                    pool.wait_ge(s_sum, T)
                ins = pool.tensor_tensor(res[:, b % 2, :, :], xa[:, tiles, :],
                                         w["b2"][:, layer, :].unsqueeze(1).to_broadcast([P, TPB, D]), ALU.add)
                if last:
                    ins.then_inc(s_bias, 1)
                    pool.wait_ge(s_bias, b + 1)
                    ins = pool.tensor_tensor(res[:, b % 2, :, :], res[:, b % 2, :, :], x[:, tiles, :], ALU.add)
                ins.then_inc(s_res, 1)

        @block.vector
        def _(dve):
            if close:
                close["vector"](dve)

            def sums(t):
                dve.wait_ge(s_sq, t + 1)
                if t >= 2:
                    dve.wait_ge(s_inv, t - 1)
                dve.tensor_reduce(norm[:, t % 2, 0, :], sq.rearrange("p (h d) -> p h d", d=LD), X_AXIS,
                                  ALU.add).then_inc(s_ss, 1)

            def normalise(t):
                dve.wait_ge(s_inv, t + 1)
                if t >= 2:
                    dve.wait_ge(s_t, 2 * (t - 1))
                qk = ps[:, qk_bank(t):qk_bank(t) + 2, :].rearrange("p i (h d) -> p (i h) d", d=LD)
                dve.tensor_tensor(hat[:, t % 2, :].rearrange("p (h d) -> p h d", d=LD), qk,
                                  norm[:, t % 2, 1, :].unsqueeze(2).to_broadcast([P, NH, LD]), ALU.mult).then_inc(s_hat, 1)

            def exchange(t):
                dve.wait_ge(s_hat, t + 1)
                if close and t == 0:
                    dve.wait_ge(close["scaled"], 2)
                for k in range(2):
                    a, b = k * LD // 2, (1 - k) * LD // 2
                    dve.tensor_tensor(heads(turned[:, t % 2, :])[:, :, :, b:b + LD // 2],
                                      heads(hat[:, t % 2, :])[:, :, :, a:a + LD // 2],
                                      exchanged[:, t, :, a:a + LD // 2].unsqueeze(2).to_broadcast([P, 2, LH, LD // 2]),
                                      ALU.mult).then_inc(s_turned, 1)

            def rotate(t):
                dve.wait_ge(s_turned, 2 * t + 2)
                dve.wait_ge(s_plain, t + 1)
                dve.tensor_tensor(hat[:, t % 2, :], turned[:, t % 2, :], plain[:, t % 2, :], ALU.add).then_inc(s_sum, 1)

            def mask_scores(u):
                dve.wait_ge(s_s, u + 1)
                if u >= 2:
                    dve.wait_ge(s_pa, u - 1)
                got = ps[:, SC:SC + 2, 0:2 * KEYS].rearrange("p b (h k) -> p b h k", h=2)
                first = min(u // 2, 1)
                dve.tensor_tensor(sub[:, u % 2].rearrange("p (b h) k -> p b h k", b=2), got,
                                  mask[:, first:first + 1, :].unsqueeze(1).to_broadcast([P, 2, 2, KEYS]),
                                  ALU.add).then_inc(s_sub, 1)
                dve.wait_ge(s_sub, u + 1)
                dve.tensor_reduce(nmax[:, u % 2, :], sub[:, u % 2], X_AXIS, ALU.max, negate=True).then_inc(s_nm, 1)

            def divide(u):
                t, par = divmod(u, 2)
                dve.wait_ge(s_av, u + 1)
                got = ps[:, OB, 0:HH * (LD + 1)].rearrange("p (h d) -> p h d", d=LD + 1)
                dve.reciprocal(rden[:, u % 2, :], got[:, :, LD]).then_inc(s_rd, 1)
                dve.wait_ge(s_rd, u + 1)
                if t >= 2:
                    dve.wait_ge(s_ot, t - 1)
                dve.tensor_tensor(o[:, t % 2, :].rearrange("p (h a d) -> p h a d", a=2, d=LD)[:, :, par, :],
                                  got[:, :, 0:LD], rden[:, u % 2, :].unsqueeze(2).to_broadcast([P, HH, LD]),
                                  ALU.mult).then_inc(s_o, 1)

            def add(t):
                dve.wait_ge(s_y, t + 1)
                dve.tensor_tensor(xa[:, t, :], xs[:, t, :], ps[:, PB, 0:D], ALU.add).then_inc(s_xa, 1)

            def shift_stats(b):
                n = 2 * TPB * b
                for j in range(TPB):
                    dve.bn_stats(stat[:, j, 0, :], xa[:, TPB * b + j, 0:D // 2]).then_inc(s_st, 1)
                dve.wait_ge(s_sh, b + 1)
                for j in range(TPB):
                    dve.bn_stats(stat[:, j, 1, :], ps[:, SH, j * D // 2:(j + 1) * D // 2]).then_inc(s_st, 1)
                for j in range(TPB):
                    dve.wait_ge(s_st, n + TPB + j + 1)
                    dve.bn_aggr(mv[:, TPB * b + j, :], stat[:, j, :, :].rearrange("p a b -> p (a b)")).then_inc(s_mv, 1)

            def normalise_shifted(b):
                dve.wait_ge(s_rs, b + 1)
                if b >= 1:
                    dve.wait_ge(s_ht, b)
                for j in range(TPB):
                    t = TPB * b + j
                    dve.tensor_scalar(hn[:, j, 0:D // 2], xa[:, t, 0:D // 2], mv[:, t, 0:1], rstd[:, t:t + 1],
                                      ALU.subtract, ALU.mult).then_inc(s_hn, 1)
                    dve.tensor_scalar(hn[:, j, D // 2:D], ps[:, SH, j * D // 2:(j + 1) * D // 2], mv[:, t, 0:1],
                                      rstd[:, t:t + 1], ALU.subtract, ALU.mult).then_inc(s_hn, 1)

            def product(b, c):
                n = C * b + c
                rows = HCH[c]
                dve.wait_ge(s_gate, n + 1)
                if b >= 2:
                    dve.wait_ge(s_down, b - 1)
                dve.scalar_tensor_tensor(out=hid[0:rows, b % 2, c, :], in0=ps[0:rows, HID_BANK + 2 * (n % 2), :],
                                         scalar=w["b1"][0:rows, layer, 0, c:c + 1], in1=gate[0:rows, n % 2, :],
                                         op0=ALU.add, op1=ALU.mult).then_inc(s_hid, 1)

            def add_down(b):
                tiles = slice(TPB * b, TPB * (b + 1))
                dve.wait_ge(s_down, b + 1)
                dve.wait_ge(s_res, b + 1)
                dve.tensor_tensor((x if last else xs)[:, tiles, :], res[:, b % 2, :, :],
                                  ps[:, YB + b % 2, :].rearrange("p (t c) -> p t c", t=TPB), ALU.add).then_inc(s_x, 1)

            for i in range(ROUNDS):
                u = 2 * (i - LAG)
                if 0 <= i - 1 < T:
                    exchange(i - 1)
                if 0 <= u < U:
                    mask_scores(u)
                if 0 <= u - 2 < U:
                    divide(u - 2)
                if i < T:
                    sums(i)
                if i == T + 3:
                    normalise_shifted(0)
                u += 1
                if 0 <= i - 1 < T:
                    rotate(i - 1)
                if 0 <= u < U:
                    mask_scores(u)
                if i < T:
                    normalise(i)
                if 0 <= u - 2 < U:
                    divide(u - 2)
                if 0 <= u - 5 < U:
                    add(u // 2 - 2)
                if i in (T + 2, T + 3):
                    shift_stats(i - T - 2)
            for b in range(NB + 1):
                if b < NB:
                    product(b, 0)
                if b + 1 < NB:
                    normalise_shifted(b + 1)
                if b >= 1:
                    add_down(b - 1)
                if b < NB:
                    product(b, 1)
                if b + 2 < NB:
                    shift_stats(b + 2)
                if b < NB:
                    product(b, 2)
            dve.wait_ge(s_x, NB)


def shape_constants():
    f32, bf16 = np.float32, mybir.dt.np(BF16)
    c = {}
    c["ident"] = np.eye(P, dtype=f32)
    c["identb"] = np.eye(P, dtype=bf16)
    ahead = np.where(np.arange(P)[None, :] > np.arange(P)[:, None], NEG, 0.0)
    c["mask_q"] = ahead.astype(bf16)
    c["mask_k"] = np.ascontiguousarray(ahead.T).astype(bf16)
    c["ones"] = np.ones((2, PAIRS * S), bf16)
    pick = np.zeros((P, 4 * 9), f32)
    for j in range(4):
        for d in range(9):
            pick[VW * j + d, 9 * j + d] = 1.0
    c["pick"] = pick
    inv = (1.0 / np.power(10000.0, np.arange(0, DH, 2, dtype=f32).astype(np.float64) / DH).astype(f32)).astype(f32)
    ang = np.outer(np.arange(S, dtype=f32), inv).astype(f32).astype(np.float64)
    ang = np.concatenate([ang, ang], axis=1)
    sign = np.where(np.arange(DH) < DH // 2, -1.0, 1.0)
    rows = np.arange(P) // PAIRS % DH
    c["rope"] = np.stack([np.cos(ang)[:, rows].T, (np.sin(ang) * sign)[:, rows].T]).astype(f32)
    inv = (1.0 / np.power(10000.0, np.arange(0, LD, 2, dtype=f32).astype(np.float64) / LD).astype(f32)).astype(f32)
    tok = np.arange(S, dtype=f32)
    ang = (tok[:, None] * inv[None, :]).astype(f32).astype(np.float64)
    base = (np.arange(0, LD, 2) + 0.4 * LD) / (1.4 * LD)
    power = (tok.astype(np.float64) - S // 2) / (WIN // 2)
    grow = base.astype(f32).astype(np.float64)[None, :] ** power[:, None]
    both = [np.concatenate([m, m], axis=1) for m in (np.cos(ang), np.sin(ang), grow)]
    sign = np.where(np.arange(LD) < LD // 2, 1.0, -1.0)
    tabs = []
    for m in (both[0], both[1] * sign):
        qk = np.stack([m * both[2] * SCORE_SCALE, m / both[2]], axis=1)
        tabs.append(qk.reshape(T, P, 2, LD).transpose(1, 0, 2, 3))
    c["xpos"] = np.ascontiguousarray(np.stack(tabs)).astype(f32)
    i, j = np.arange(P)[:, None], np.arange(KEYS)[None, :] - WIN
    hidden = (j > i) | (j < i - WIN)
    c["mask_l"] = np.where(np.stack([hidden | (j < 0), hidden], axis=1), NEG, 0.0).astype(bf16)
    c["shift"] = np.ascontiguousarray(np.stack([np.eye(P, k=1), np.eye(P, k=1 - P)], axis=1)).astype(f32)
    return c


def kernel(L0_attn_x, L0_attn_Wq, L0_attn_Wk, L0_attn_Wv, L0_attn_Wo, L0_ffn_wqkv, L0_ffn_q_scale, L0_ffn_k_scale,
           L0_ffn_wo, L0_ffn_ln_g, L0_ffn_ln_b, L0_ffn_w1, L0_ffn_b1, L0_ffn_w2, L0_ffn_b2):
    import concourse.bacc as _bacc
    from concourse.bass_utils import run_bass_kernel_spmd as _run

    arrays = shape_constants()
    order = np.array([(2 * pair + par) * DH + d for par in range(2) for d in range(DH) for pair in range(PAIRS)])
    turned = order // DH * DH + (order % DH + DH // 2) % DH
    wq, wk = np.asarray(L0_attn_Wq), np.asarray(L0_attn_Wk)
    arrays["wqk"] = np.ascontiguousarray(np.stack([wq[order].T, wq[turned].T, wk[order].T, wk[turned].T]))
    arrays["wv"] = np.ascontiguousarray(np.asarray(L0_attn_Wv).T)
    arrays["wo"] = np.ascontiguousarray(np.asarray(L0_attn_Wo).T)
    for name, value in (("wqkv", L0_ffn_wqkv), ("q_scale", L0_ffn_q_scale), ("k_scale", L0_ffn_k_scale),
                        ("lwo", L0_ffn_wo), ("w1", L0_ffn_w1), ("w2", L0_ffn_w2), ("b2", L0_ffn_b2)):
        arrays[name] = np.ascontiguousarray(np.asarray(value))
    arrays["ln_gb"] = np.ascontiguousarray(np.stack([np.asarray(L0_ffn_ln_g), np.asarray(L0_ffn_ln_b)], 2).transpose(1, 0, 2))
    b1 = np.zeros((P, LAYERS, 2, len(HCH)), np.float32)
    for c, rows in enumerate(HCH):
        for i in range(2):
            b1[:rows, :, i, c] = np.asarray(L0_ffn_b1)[:, i * HID + c * P:i * HID + c * P + rows].T
    arrays["b1"] = b1
    arrays["x"] = np.ascontiguousarray(np.asarray(L0_attn_x).reshape(S, D))

    nc = _bacc.Bacc("TRN2", target_bir_lowering=False, num_devices=1)
    arrays = {"in_" + n: v for n, v in arrays.items()}
    aps = {n[3:]: nc.dram_tensor(n, v.shape, mybir.dt.from_np(v.dtype), kind="ExternalInput").ap()
           for n, v in arrays.items()}
    out = nc.dram_tensor("out", (S, D), F32, kind="ExternalOutput").ap()
    build(nc, aps, out)
    r = _run(nc, [arrays], core_ids=[0])
    return r.results[0]["out"].reshape(1, S, D)
```
